# Optimizing a Trainium2 kernel written in Bass

```python
import numpy as np
import jax
import jax.numpy as jnp

def _softmax(x, axis=-1):
    return jax.nn.softmax(x, axis=axis)

def _gelu(x):
    return jax.nn.gelu(x, approximate=True)

def _silu(x):
    return jax.nn.silu(x)

def _sigmoid(x):
    return jax.nn.sigmoid(x)

def _layernorm(x, axis=-1, eps=1e-05):
    m = jnp.mean(x, axis=axis, keepdims=True)
    v = jnp.var(x, axis=axis, keepdims=True)
    return (x - m) / jnp.sqrt(v + eps)

def _scatter_add(tgt, idx, src, axis=0):
    return tgt.at[idx].add(src)

def _segment_sum(src, seg, n):
    return jax.ops.segment_sum(src, seg, n)
kernel_name = 'mk_xattn_ffn_d2_seqx_r2_cb551b'

def setup_inputs(seed: int=0):
    np.random.seed(seed)
    _w = jnp.asarray

    def _rec_inputs():
        import jax
        import jax.numpy as jnp
        _rk = jax.random.key(seed)
        x = 0.0002417 + 0.9998 * jax.random.normal(jax.random.fold_in(_rk, 1), (16, 256, 512), jnp.float32)
        _lenS = 256 - jax.random.randint(jax.random.fold_in(_rk, 7), (16,), 0, max(1, 256 // 4) + 1, jnp.int32)
        _lenS2 = 256 - jax.random.randint(jax.random.fold_in(_rk, 8), (16,), 0, max(1, 256 // 4) + 1, jnp.int32)
        _ctx_1024P = jax.random.normal(jax.random.fold_in(_rk, 11), (16, 16, 512), jnp.float32)
        _ctx_1024c = jax.random.dirichlet(jax.random.fold_in(_rk, 511), 0.3 * jnp.ones((16,), jnp.float32), (16, 256))
        _ctx_1024t = jnp.einsum('bsk,bkd->bsd', _ctx_1024c, _ctx_1024P)
        _ctx_1024t = _ctx_1024t * jax.lax.rsqrt(jnp.mean(jnp.square(_ctx_1024t)) + 1e-12) * 0.953939
        ctx_1024 = 7.22013e-05 + 1.00017 * (_ctx_1024t + 0.3 * jax.random.normal(jax.random.fold_in(_rk, 611), (16, 256, 512), jnp.float32))
        _validS = jnp.arange(256)[None, :] < _lenS[:, None]
        _validS2 = jnp.arange(256)[None, :] < _lenS2[:, None]
        _causal = jnp.tril(jnp.ones((256, 256), dtype=bool))
        mask_Bx1x1xS2_if1 = jnp.where(jnp.ones((16, 1, 1, 256), dtype=bool), 1, 0).astype(jnp.int32)
        mask_BxS2_bk0 = jnp.logical_not(jnp.broadcast_to(_validS2[:, :], (16, 256)))
        return (x, ctx_1024, mask_Bx1x1xS2_if1, mask_BxS2_bk0)
    x, ctx_1024, mask_Bx1x1xS2_if1, mask_BxS2_bk0 = _rec_inputs()

    def _L0_xattn_setup():
        import jax, jax.numpy as jnp
        import numpy as np
        EMBED = 512
        HEADS = 16
        HEAD_DIM = EMBED // HEADS
        key = jax.random.key(seed)
        ks = jax.random.split(key, 12)
        N, L, E = (4, 1024, EMBED)
        s = 1.0 / np.sqrt(E)
        return {'values': jax.random.normal(ks[0], (N, L, E), jnp.float32), 'keys': jax.random.normal(ks[1], (N, L, E), jnp.float32), 'query': jax.random.normal(ks[2], (N, L, E), jnp.float32), 'mask': jnp.ones((N, 1, 1, L), jnp.int32), 'Wv': jax.random.normal(ks[3], (E, E), jnp.float32) * s, 'bv': jnp.zeros((E,), jnp.float32), 'Wk': jax.random.normal(ks[4], (E, E), jnp.float32) * s, 'bk': jnp.zeros((E,), jnp.float32), 'Wq': jax.random.normal(ks[5], (E, E), jnp.float32) * s, 'bq': jnp.zeros((E,), jnp.float32), 'Wo': jax.random.normal(ks[6], (E, E), jnp.float32) * s, 'bo': jnp.zeros((E,), jnp.float32)}
    _L0_xattn_all = _L0_xattn_setup()
    _L0_xattn_in = {k: v for k, v in _L0_xattn_all.items() if k in ('Wv', 'bv', 'Wk', 'bk', 'Wq', 'bq', 'Wo', 'bo')}
    del _L0_xattn_all

    def _L0_ffn_setup():
        import jax, jax.numpy as jnp
        import numpy as np
        HIDDEN = 512
        INNER = 2048

        def _weight_quant(w):
            scale = 1.0 / jnp.clip(jnp.mean(jnp.abs(w)), 1e-05)
            wq = jnp.clip(jnp.round(w * scale), -1.0, 1.0) / scale
            return w + jax.lax.stop_gradient(wq - w)

        def _act_quant(x):
            scale = 127.0 / jnp.clip(jnp.max(jnp.abs(x), axis=-1, keepdims=True), 1e-05)
            xq = jnp.clip(jnp.round(x * scale), -128.0, 127.0) / scale
            return x + jax.lax.stop_gradient(xq - x)

        def _bitlinear(x, w):
            return jnp.einsum('bsi,oi->bso', _act_quant(x), _weight_quant(w))
        key = jax.random.key(seed)
        k0, k1, k2, k3 = jax.random.split(key, 4)
        x = jax.random.normal(k0, (4, 1024, HIDDEN), dtype=jnp.float32)
        w_gate = jax.random.normal(k1, (INNER, HIDDEN), dtype=jnp.float32) / np.sqrt(HIDDEN)
        w_up = jax.random.normal(k2, (INNER, HIDDEN), dtype=jnp.float32) / np.sqrt(HIDDEN)
        w_down = jax.random.normal(k3, (HIDDEN, INNER), dtype=jnp.float32) / np.sqrt(INNER)
        return {'x': x, 'w_gate': w_gate, 'w_up': w_up, 'w_down': w_down}
    _L0_ffn_all = _L0_ffn_setup()
    _L0_ffn_in = {k: v for k, v in _L0_ffn_all.items() if k in ('w_gate', 'w_up', 'w_down')}
    del _L0_ffn_all

    def _L1_xattn_setup():
        import jax, jax.numpy as jnp
        import numpy as np
        DIM = 512
        HEADS = 8
        DIM_HEAD = 64
        INNER = HEADS * DIM_HEAD
        LN_EPS = 1e-05

        def _layernorm(x, g, b):
            mu = jnp.mean(x, axis=-1, keepdims=True)
            var = jnp.var(x, axis=-1, keepdims=True)
            return (x - mu) * jax.lax.rsqrt(var + LN_EPS) * g + b
        key = jax.random.key(seed)
        ks = jax.random.split(key, 8)
        b, n, m = (4, 1024, 256)
        x = jax.random.normal(ks[0], (b, n, DIM), dtype=jnp.float32)
        media = jax.random.normal(ks[1], (b, m, DIM), dtype=jnp.float32)
        media_mask = jax.random.randint(ks[2], (b, m), 0, 2).astype(jnp.bool_)
        media_mask = media_mask.at[:, 0].set(True)
        ln_g = jnp.ones((DIM,), jnp.float32)
        ln_b = jnp.zeros((DIM,), jnp.float32)
        s = 0.02
        Wq = jax.random.normal(ks[3], (DIM, INNER), jnp.float32) * s
        Wkv = jax.random.normal(ks[4], (DIM, 2 * INNER), jnp.float32) * s
        Wo = jax.random.normal(ks[5], (INNER, DIM), jnp.float32) * s
        return {'x': x, 'media': media, 'media_mask': media_mask, 'ln_g': ln_g, 'ln_b': ln_b, 'Wq': Wq, 'Wkv': Wkv, 'Wo': Wo}
    _L1_xattn_all = _L1_xattn_setup()
    _L1_xattn_in = {k: v for k, v in _L1_xattn_all.items() if k in ('ln_g', 'ln_b', 'Wq', 'Wkv', 'Wo')}
    del _L1_xattn_all

    def _L1_ffn_setup():
        import jax, jax.numpy as jnp
        import numpy as np
        E = 8
        G = 4
        LG = 2
        TOPK = 2
        ROUTE_SCALE = 1.0

        def _grouped_mm(x, w, counts):
            counts = counts.astype(jnp.int32)
            if hasattr(jax.lax, 'ragged_dot'):
                return jax.lax.ragged_dot(x, w, counts)
            offs = jnp.cumsum(counts)
            eid = jnp.searchsorted(offs, jnp.arange(x.shape[0]), side='right')
            oh = jax.nn.one_hot(eid, w.shape[0], dtype=x.dtype)
            return jnp.einsum('nd,ne,edh->nh', x, oh, w)
        key = jax.random.key(seed)
        ks = jax.random.split(key, 8)
        bs, slen, dim, hid, shid = (2, 1024, 512, 256, 512)
        std = 0.02
        return {'x': jax.random.normal(ks[0], (bs, slen, dim), jnp.float32), 'w_gate': jax.random.normal(ks[1], (E, dim), jnp.float32) * std, 'w1': jax.random.normal(ks[2], (E, dim, hid), jnp.float32) * std, 'w2': jax.random.normal(ks[3], (E, hid, dim), jnp.float32) * std, 'w3': jax.random.normal(ks[4], (E, dim, hid), jnp.float32) * std, 'sw1': jax.random.normal(ks[5], (shid, dim), jnp.float32) * std, 'sw2': jax.random.normal(ks[6], (dim, shid), jnp.float32) * std, 'sw3': jax.random.normal(ks[7], (shid, dim), jnp.float32) * std, 'expert_bias': jnp.zeros((E,), jnp.float32)}
    _L1_ffn_all = _L1_ffn_setup()
    _L1_ffn_in = {k: v for k, v in _L1_ffn_all.items() if k in ('w_gate', 'w1', 'w2', 'w3', 'sw1', 'sw2', 'sw3', 'expert_bias')}
    del _L1_ffn_all
    return {'x': x, 'ctx_1024': ctx_1024, 'mask_Bx1x1xS2_if1': mask_Bx1x1xS2_if1, 'mask_BxS2_bk0': mask_BxS2_bk0, 'L0_xattn_Wv': _L0_xattn_in['Wv'], 'L0_xattn_bv': _L0_xattn_in['bv'], 'L0_xattn_Wk': _L0_xattn_in['Wk'], 'L0_xattn_bk': _L0_xattn_in['bk'], 'L0_xattn_Wq': _L0_xattn_in['Wq'], 'L0_xattn_bq': _L0_xattn_in['bq'], 'L0_xattn_Wo': _L0_xattn_in['Wo'], 'L0_xattn_bo': _L0_xattn_in['bo'], 'L0_ffn_w_gate': _L0_ffn_in['w_gate'], 'L0_ffn_w_up': _L0_ffn_in['w_up'], 'L0_ffn_w_down': _L0_ffn_in['w_down'], 'L1_xattn_ln_g': _L1_xattn_in['ln_g'], 'L1_xattn_ln_b': _L1_xattn_in['ln_b'], 'L1_xattn_Wq': _L1_xattn_in['Wq'], 'L1_xattn_Wkv': _L1_xattn_in['Wkv'], 'L1_xattn_Wo': _L1_xattn_in['Wo'], 'L1_ffn_w_gate': _L1_ffn_in['w_gate'], 'L1_ffn_w1': _L1_ffn_in['w1'], 'L1_ffn_w2': _L1_ffn_in['w2'], 'L1_ffn_w3': _L1_ffn_in['w3'], 'L1_ffn_sw1': _L1_ffn_in['sw1'], 'L1_ffn_sw2': _L1_ffn_in['sw2'], 'L1_ffn_sw3': _L1_ffn_in['sw3'], 'L1_ffn_expert_bias': _L1_ffn_in['expert_bias']}

def reference(x, ctx_1024, mask_Bx1x1xS2_if1, mask_BxS2_bk0, L0_xattn_Wv, L0_xattn_bv, L0_xattn_Wk, L0_xattn_bk, L0_xattn_Wq, L0_xattn_bq, L0_xattn_Wo, L0_xattn_bo, L0_ffn_w_gate, L0_ffn_w_up, L0_ffn_w_down, L1_xattn_ln_g, L1_xattn_ln_b, L1_xattn_Wq, L1_xattn_Wkv, L1_xattn_Wo, L1_ffn_w_gate, L1_ffn_w1, L1_ffn_w2, L1_ffn_w3, L1_ffn_sw1, L1_ffn_sw2, L1_ffn_sw3, L1_ffn_expert_bias):
    import jax
    import jax.numpy as jnp

    def _L0_xattn_ref(values, keys, query, mask, Wv, bv, Wk, bk, Wq, bq, Wo, bo):
        import jax, jax.numpy as jnp
        import numpy as np
        EMBED = 512
        HEADS = 16
        HEAD_DIM = EMBED // HEADS
        N, L, E = values.shape
        H, D = (HEADS, HEAD_DIM)
        v = (values @ Wv + bv).reshape(N, L, H, D)
        k = (keys @ Wk + bk).reshape(N, L, H, D)
        q = (query @ Wq + bq).reshape(N, L, H, D)
        energy = jnp.einsum('nqhd,nkhd->nhqk', q, k)
        energy = jnp.where(mask == 0, jnp.float32(-1e+20), energy)
        attn = jax.nn.softmax(energy / np.sqrt(D), axis=3)
        out = jnp.einsum('nhqk,nkhd->nqhd', attn, v).reshape(N, L, E)
        return out @ Wo + bo

    def _L0_ffn_ref(x, w_gate, w_up, w_down):
        import jax, jax.numpy as jnp
        import numpy as np
        HIDDEN = 512
        INNER = 2048

        def _weight_quant(w):
            scale = 1.0 / jnp.clip(jnp.mean(jnp.abs(w)), 1e-05)
            wq = jnp.clip(jnp.round(w * scale), -1.0, 1.0) / scale
            return w + jax.lax.stop_gradient(wq - w)

        def _act_quant(x):
            scale = 127.0 / jnp.clip(jnp.max(jnp.abs(x), axis=-1, keepdims=True), 1e-05)
            xq = jnp.clip(jnp.round(x * scale), -128.0, 127.0) / scale
            return x + jax.lax.stop_gradient(xq - x)

        def _bitlinear(x, w):
            return jnp.einsum('bsi,oi->bso', _act_quant(x), _weight_quant(w))
        gate = jax.nn.silu(_bitlinear(x, w_gate))
        up = _bitlinear(x, w_up)
        return _bitlinear(gate * up, w_down)

    def _L1_xattn_ref(x, media, media_mask, ln_g, ln_b, Wq, Wkv, Wo):
        import jax, jax.numpy as jnp
        import numpy as np
        DIM = 512
        HEADS = 8
        DIM_HEAD = 64
        INNER = HEADS * DIM_HEAD
        LN_EPS = 1e-05

        def _layernorm(x, g, b):
            mu = jnp.mean(x, axis=-1, keepdims=True)
            var = jnp.var(x, axis=-1, keepdims=True)
            return (x - mu) * jax.lax.rsqrt(var + LN_EPS) * g + b
        scale = DIM_HEAD ** (-0.5)
        xn = _layernorm(x, ln_g, ln_b)
        q = xn @ Wq
        kv = media @ Wkv
        k, v = jnp.split(kv, 2, axis=-1)

        def split_heads(t):
            b_, s_, _ = t.shape
            return t.reshape(b_, s_, HEADS, DIM_HEAD).transpose(0, 2, 1, 3)
        q, k, v = (split_heads(q) * scale, split_heads(k), split_heads(v))
        sim = jnp.einsum('bhid,bhjd->bhij', q, k)
        neg_inf = jnp.finfo(sim.dtype).min
        sim = jnp.where(media_mask[:, None, None, :], sim, neg_inf)
        attn = jax.nn.softmax(sim, axis=-1)
        out = jnp.einsum('bhij,bhjd->bhid', attn, v)
        out = out.transpose(0, 2, 1, 3).reshape(x.shape[0], x.shape[1], INNER)
        return out @ Wo

    def _L1_ffn_ref(x, w_gate, w1, w2, w3, sw1, sw2, sw3, expert_bias):
        import jax, jax.numpy as jnp
        import numpy as np
        E = 8
        G = 4
        LG = 2
        TOPK = 2
        ROUTE_SCALE = 1.0

        def _grouped_mm(x, w, counts):
            counts = counts.astype(jnp.int32)
            if hasattr(jax.lax, 'ragged_dot'):
                return jax.lax.ragged_dot(x, w, counts)
            offs = jnp.cumsum(counts)
            eid = jnp.searchsorted(offs, jnp.arange(x.shape[0]), side='right')
            oh = jax.nn.one_hot(eid, w.shape[0], dtype=x.dtype)
            return jnp.einsum('nd,ne,edh->nh', x, oh, w)
        bs, slen, dim = x.shape
        xf = x.reshape(-1, dim)
        N = xf.shape[0]
        logits = xf @ w_gate.T
        scores = jax.nn.softmax(logits.astype(jnp.float32), axis=-1)
        original = scores
        s = (scores + expert_bias).reshape(N, G, E // G)
        group_scores = jax.lax.top_k(s, 2)[0].sum(-1)
        top_groups = jax.lax.top_k(group_scores, LG)[1]
        keep = jnp.zeros((N, G), bool).at[jnp.arange(N)[:, None], top_groups].set(True)
        masked = jnp.where(keep[:, :, None], s, -jnp.inf).reshape(N, E)
        topk_idx = jax.lax.top_k(masked, TOPK)[1]
        weights = (jnp.take_along_axis(original, topk_idx, axis=1) * ROUTE_SCALE).astype(x.dtype)
        counts = jnp.bincount(topk_idx.reshape(-1), length=E)
        flat_idx = topk_idx.reshape(-1)
        routed_in = xf[flat_idx]
        routed_in = (routed_in.astype(jnp.float32) * weights.reshape(-1, 1)).astype(x.dtype)
        h = jax.nn.silu(_grouped_mm(routed_in, w1, counts)) * _grouped_mm(routed_in, w3, counts)
        routed_out = _grouped_mm(h, w2, counts)
        shared = jax.nn.silu(xf @ sw1.T) * (xf @ sw3.T) @ sw2.T
        out = shared.at[flat_idx].add(routed_out)
        return out.reshape(bs, slen, dim)
    x = x + _L0_xattn_ref(ctx_1024, ctx_1024, _layernorm(x, axis=-1), mask_Bx1x1xS2_if1, L0_xattn_Wv, L0_xattn_bv, L0_xattn_Wk, L0_xattn_bk, L0_xattn_Wq, L0_xattn_bq, L0_xattn_Wo, L0_xattn_bo)
    x = x + _L0_ffn_ref(_layernorm(x, axis=-1), L0_ffn_w_gate, L0_ffn_w_up, L0_ffn_w_down)
    x = x + _L1_xattn_ref(_layernorm(x, axis=-1), ctx_1024, mask_BxS2_bk0, L1_xattn_ln_g, L1_xattn_ln_b, L1_xattn_Wq, L1_xattn_Wkv, L1_xattn_Wo)
    x = x + _L1_ffn_ref(_layernorm(x, axis=-1), L1_ffn_w_gate, L1_ffn_w1, L1_ffn_w2, L1_ffn_w3, L1_ffn_sw1, L1_ffn_sw2, L1_ffn_sw3, L1_ffn_expert_bias)
    return x

_drawn_inputs = setup_inputs


def setup_inputs(seed=0):
    import zlib

    import numpy as np

    out = dict(_drawn_inputs(seed))
    spreads = {'L0_xattn_bv': (0.0, 0.1),
     'L0_xattn_bk': (0.0, 0.8),
     'L0_xattn_bq': (0.0, 0.404),
     'L0_xattn_bo': (0.0, 0.1),
     'L1_xattn_ln_g': (1.0, 0.6),
     'L1_xattn_ln_b': (0.0, 0.8),
     'L1_ffn_expert_bias': (0.0, 0.326)}
    factors = {'L1_xattn_Wq': 6.527, 'L1_ffn_w_gate': 7.282}
    for name, (base, spread) in spreads.items():
        noise = np.random.default_rng([zlib.crc32(name.encode()), seed]).standard_normal(out[name].shape)
        drawn = base * np.exp(spread * noise) if base else spread * noise
        out[name] = jnp.asarray(drawn.astype(out[name].dtype))
    for name, factor in factors.items():
        out[name] = (out[name] * factor).astype(out[name].dtype)
    return out
```

```python
import concourse.bass as bass
from concourse import mybir
from contextlib import ExitStack

F32 = mybir.dt.float32
F32R = mybir.dt.float32r
BF16 = mybir.dt.bfloat16
U32 = mybir.dt.uint32
ALU = mybir.AluOpType
ACT = mybir.ActivationFunctionType
AX = mybir.AxisListType

P = 128
BATCH, SEQ, DIM = 16, 256, 512
TOK = BATCH * SEQ
KC = DIM // P
QT = SEQ // P
EPS = 1e-5
BIG = 3.0e38

HI, LO = 0, 1
TERMS = ((HI, HI), (LO, HI), (HI, LO))


def wait_for(engine, semaphore, count):
    if not isinstance(count, int) or count > 0:
        engine.wait_ge(semaphore, count)


def wait_apart(engine, semaphore, count):
    if not isinstance(count, int) or count > 0:
        engine.wait_ge(semaphore, count)
        engine.nop(nofuse=True)


class Element:

    def __init__(self, index, parity, count, group=2):
        self.index, self.par, self.count, self.group = index + parity // group, parity % group, count, group
        self.n = group * self.index + self.par

    def plus(self, k):
        return Element(self.index, self.par + k, self.count, self.group)

    def has(self, k):
        return not isinstance(self.n, int) or self.n + k < self.count

    def dma(self):
        return self.index * 16 + 16


def run_elements(engine, count, iteration, ahead=2, group=2):
    for par in range(group):
        iteration(Element(0, par, count, group))
    with engine.Fori(1, (count - ahead) // group) as index:
        for par in range(group):
            iteration(Element(index, par, count, group))
    for n in range((count - ahead) // group * group, count):
        iteration(Element(n // group, n % group, count, group))


def clear_semaphores(nc, sems):
    nums = sorted(s.num for s in sems)
    with nc.Block() as block:
        @block.gpsimd
        def _(pool):
            at = 0
            while at < len(nums):
                end = at + 1
                while end < len(nums) and nums[end] == nums[end - 1] + 1:
                    end += 1
                nc.gpsimd.sem_clear(range(nums[at], nums[end - 1] + 1))
                at = end


def rows_of(t, el, tiles=QT):
    return t[bass.ts(el.n, tiles * P), :].rearrange("(t p) d -> p t d", p=P)


def attention_phase(nc, tag, heads, x_in, ctx_in, mask_in, mask_value, x_out, w_views, q_bias, k_bias,
                    v_bias, out_bias, ln_gain, ln_bias, batches=BATCH):
    hd = DIM // heads
    hpg = P // hd
    GROUPS = KC
    pairs = heads // 2
    ring = 4
    sm_scale = float(hd) ** -0.5
    normed_twice = ln_gain is not None

    with ExitStack() as ctx:
        def sb(name, shape, dt=F32):
            return ctx.enter_context(nc.sbuf_tensor(f"{tag}_{name}", shape, dt))

        sems = []

        def sem(name):
            sems.append(ctx.enter_context(nc.semaphore(f"{tag}_{name}")))
            return sems[-1]

        def bank(name):
            return ctx.enter_context(nc.psum_tensor(f"{tag}_{name}", [P, 512], F32))

        weights = [sb(w, [P, 2, KC, DIM], F32R) for w in ("wq", "wk", "wv", "wo")]
        wq, wk, wv, wo = weights
        ident = sb("ident", [P, P])
        cols = sb("cols", [P, 6, KC])
        BQ, BK, BV, GAIN, LBIAS = range(5)
        bo_row = sb("bo_row", [P, DIM])
        neg_half = sb("neg_half", [P, QT])
        xbuf = sb("xbuf", [P, 2, QT, DIM])
        cbuf = sb("cbuf", [P, 2, QT, DIM])
        resb = sb("resb", [P, 2, QT, DIM])
        mraw = sb("mraw", [P, 2, SEQ], mask_in.dtype)
        mbias = sb("mbias", [P, 2, SEQ])
        xn = sb("xn", [P, QT, DIM])
        stats = sb("stats", [P, QT, 6])
        mv = sb("mv", [P, QT, 2])
        ln = sb("ln", [P, 6, QT])
        xnT = sb("xnT", [P, 2, KC, SEQ], F32R)
        cT = sb("cT", [P, 2, KC, SEQ], F32R)
        qT = sb("qT", [P, 2, 2, KC, SEQ], F32R)
        kT = sb("kT", [P, 2, 2, KC, SEQ], F32R)
        vb = sb("vb", [P, 2, QT, DIM])
        probs = sb("probs", [P, ring, 2, QT, SEQ])
        negm = sb("negm", [P, ring, 2, QT])
        ssum = sb("ssum", [P, ring, 2 * QT])
        rinv = sb("rinv", [P, ring, 2 * QT])
        pT = sb("pT", [P, 2, hpg, QT, SEQ])
        oT = sb("oT", [P, 2, KC, SEQ], F32R)
        stage = [probs[:, 0:2].rearrange("p s h t k -> p (s h t k)"),
                 probs[:, 2:4].rearrange("p s h t k -> p (s h t k)"),
                 vb[:].rearrange("p s t k -> p (s t k)"),
                 xbuf[:].rearrange("p s t k -> p (s t k)")]

        s_bank = [bank(f"s{i}") for i in range(4)]
        x_bank = [bank("x0"), bank("x1")]
        pt_bank = bank("pt")
        o_bank = bank("o")

        w_loaded = [sem(f"w_loaded{i}") for i in range(4)]
        (cols_loaded, ident_zero, consts_ready, w_gained, w_hi, w_lo, qbias_mm, cols_ready,
         x_loaded0, x_loaded1, c_loaded0, c_loaded1, m_loaded0, m_loaded1, r_loaded0, r_loaded1,
         stored0, stored1, bn_done, stats_ready, ln_step, xn_ready, mbias_ready, res_ready,
         x_done, hi_done, lo_done, v_done, s_done, ttr_done, exp_done, recip_done, even_normed, odd_normed,
         pt_done, even_out, odd_out, pv_done, othi_done, otlo_done, op_done, out_done) = [sem(s) for s in (
             "cols_loaded ident_zero consts_ready w_gained w_hi w_lo qbias_mm cols_ready "
             "x_loaded0 x_loaded1 c_loaded0 c_loaded1 m_loaded0 m_loaded1 r_loaded0 r_loaded1 "
             "stored0 stored1 bn_done stats_ready ln_step xn_ready mbias_ready res_ready "
             "x_done hi_done lo_done v_done s_done ttr_done exp_done recip_done even_normed odd_normed "
             "pt_done even_out odd_out pv_done othi_done otlo_done op_done out_done").split()]
        x_loaded, c_loaded = (x_loaded0, x_loaded1), (c_loaded0, c_loaded1)
        m_loaded, r_loaded, stored = (m_loaded0, m_loaded1), (r_loaded0, r_loaded1), (stored0, stored1)

        USES = ["tc0", "tc1", "v0", "v1", "tx0", "tx1", "k0", "k1", "q0", "q1"]
        NU = len(USES)
        SPLIT = [u for u in USES if u[0] != "v"]
        NL = len(SPLIT)
        LEAD, HEAD = ["tc0", "tc1"], ["v0"]
        if pairs == 8:
            BETWEEN = [[], [], [], [], [], ["k0b"], ["k1b"], ["q0b"]]
            MID = [["v1a"], ["v1b"], ["tx0"], ["k0a"], ["tx1"], ["k1a"], ["q0a"], ["q1a"]]
            LAST = ["q1b"], []
        else:
            BETWEEN = [[], ["tx1"], ["k1a"], ["q0b"]]
            MID = [["v1", "tx0"], ["k0a", "k0b"], ["k1b", "q0a"], ["q1a"]]
            LAST = ["q1b"], []
        NCOLS = sum(b is not None for b in (q_bias, k_bias, v_bias, ln_gain, ln_bias, out_bias))

        def group_after(pair):
            return (2 * pair + 1) // hpg if pair >= 0 and (2 * pair + 2) % hpg == 0 else None

        def finished(uses):
            return [u.rstrip("b") for u in uses if u[-1] != "a"]

        def feature_rows(u):
            bias = {"q": BQ, "k": BK}[u[0]]
            if (q_bias is None and not normed_twice) if u[0] == "q" else k_bias is None:
                bias = None
            return [2 * int(u[1]), 2 * int(u[1]) + 1], bias

        with nc.Block() as block:

            @block.sync
            def _(sp):
                for n, v in enumerate(w_views):
                    sp.dma_start(stage[n].rearrange("p (k n) -> p k n", k=KC),
                                 v.rearrange("(k p) n -> p k n", p=P)).then_inc(w_loaded[n], 16)
                for n, b in enumerate((q_bias, k_bias, v_bias, ln_gain, ln_bias)):
                    if b is not None:
                        sp.dma_start(cols[:, n, :], b.rearrange("(k p) -> p k", p=P),
                                     allow_slow_non_contiguous=True).then_inc(cols_loaded, 16)
                if out_bias is not None:
                    sp.dma_start(bo_row[:], out_bias.rearrange("(a n) -> a n", a=1).broadcast_to([P, DIM])) \
                      .then_inc(cols_loaded, 16)

                def load(el, first=False):
                    xs, cs = rows_of(x_in, el), rows_of(ctx_in, el)
                    ms = mask_in[bass.ds(el.n, 1), :].broadcast_to([P, SEQ])
                    if not first:
                        wait_apart(sp, xn_ready, (el.n - 1) * QT)
                    sp.dma_start(xbuf[:, el.par], xs).then_inc(x_loaded[el.par], 16)
                    if not first:
                        wait_apart(sp, x_done, (el.n - 2) * NU + 2)
                    sp.dma_start(cbuf[:, el.par], cs).then_inc(c_loaded[el.par], 16)
                    if not first:
                        wait_apart(sp, mbias_ready, el.n - 1)
                    sp.dma_start(mraw[:, el.par], ms).then_inc(m_loaded[el.par], 16)

                sp.wait_ge(w_lo, 4)
                load(Element(0, 0, batches), True)
                load(Element(0, 1, batches), True)
                sp.dma_start(resb[:, 0], rows_of(x_in, Element(0, 0, batches))).then_inc(r_loaded[0], 16)

                def iteration(el):
                    if el.has(2):
                        load(el.plus(2))
                    if el.has(1):
                        nxt, prev = el.plus(1), el.plus(-1)
                        rs = rows_of(x_in, nxt)
                        wait_apart(sp, stored[prev.par], prev.dma())
                        sp.dma_start(resb[:, nxt.par], rs).then_inc(r_loaded[nxt.par], 16)
                    dst = rows_of(x_out, el)
                    wait_apart(sp, out_done, (el.n + 1) * QT)
                    sp.dma_start(dst, resb[:, el.par]).then_inc(stored[el.par], 16)

                run_elements(sp, batches, iteration)
                for par in range(2):
                    sp.wait_ge(stored[par], batches // 2 * 16)

            @block.gpsimd
            def _(pool):
                nc.gpsimd.memset(ident[:], 0.0).then_inc(ident_zero, 1)
                nc.gpsimd.memset(neg_half[:], -0.5).then_inc(consts_ready, 1)
                pool.wait_ge(ident_zero, 1)
                nc.gpsimd.affine_select(out=ident[:], in_=ident[:], compare_op=ALU.not_equal, fill=1.0, base=0,
                                        pattern=[[-1, P]], channel_multiplier=1).then_inc(consts_ready, 1)
                pool.wait_ge(consts_ready, 2)

                LN_STEPS = 9 if normed_twice else 4

                def normalise(el):
                    step = [0]

                    def chained(ins):
                        step[0] += 1
                        ins.then_inc(ln_step, 1)
                        wait_apart(pool, ln_step, el.n * LN_STEPS + step[0])

                    pool.wait_ge(stats_ready, el.n + 1)
                    wait_apart(pool, x_done, (el.n - 1) * NU + USES.index("tx1") + 1)
                    mean, var = mv[:, :, 0], mv[:, :, 1]
                    chained(nc.gpsimd.tensor_scalar(ln[:, 0], var, 1.0, EPS, ALU.mult, ALU.add))
                    chained(nc.gpsimd.tensor_tensor(ln[:, 1], ln[:, 0], neg_half[:], ALU.pow))
                    r = ln[:, 1]
                    if normed_twice:
                        chained(nc.gpsimd.tensor_tensor(ln[:, 2], var, r, ALU.mult))
                        chained(nc.gpsimd.tensor_tensor(ln[:, 0], ln[:, 2], r, ALU.mult))
                        chained(nc.gpsimd.tensor_scalar(ln[:, 2], ln[:, 0], 1.0, EPS, ALU.mult, ALU.add))
                        chained(nc.gpsimd.tensor_tensor(ln[:, 3], ln[:, 2], neg_half[:], ALU.pow))
                        chained(nc.gpsimd.tensor_tensor(ln[:, 1], r, ln[:, 3], ALU.mult))
                    chained(nc.gpsimd.tensor_tensor(ln[:, 4], mean, r, ALU.mult))
                    chained(nc.gpsimd.tensor_scalar(ln[:, 5], ln[:, 4], -1.0, 0.0, ALU.mult, ALU.add))
                    for t in range(QT):
                        nc.gpsimd.tensor_scalar(xn[:, t], xbuf[:, el.par, t], r[:, t:t + 1], ln[:, 5, t:t + 1],
                                                ALU.mult, ALU.add).then_inc(xn_ready, 1)

                def norm_probs(el, p):
                    wait_apart(pool, recip_done, el.n * pairs + p + 1)
                    for t in range(QT):
                        pr = probs[:, p % ring, 1, t]
                        last = nc.gpsimd.tensor_scalar(pr, pr, rinv[:, p % ring, QT + t:QT + t + 1], 0.0,
                                                       ALU.mult, ALU.add)
                    last.then_inc(odd_normed, 1)

                def add_out_bias(el):
                    pool.wait_ge(r_loaded[el.par], el.dma())
                    for t in range(QT):
                        nc.gpsimd.tensor_tensor(resb[:, el.par, t], resb[:, el.par, t], bo_row[:], ALU.add) \
                            .then_inc(res_ready, 1)

                pool.wait_ge(cols_loaded, NCOLS * 16)
                normalise(Element(0, 0, batches))
                normalise(Element(0, 1, batches))

                def iteration(el):
                    for p in range(pairs):
                        norm_probs(el, p)
                        if p == pairs - 2 and out_bias is not None:
                            add_out_bias(el)
                    if el.has(2):
                        normalise(el.plus(2))

                run_elements(pool, batches, iteration)

            @block.scalar
            def _(act):
                for n, w in enumerate(weights):
                    act.wait_ge(w_loaded[n], 16)
                    if n == 0 and normed_twice:
                        act.wait_ge(w_gained, KC)
                    nc.scalar.activation(w[:, HI].rearrange("p k n -> p (k n)"), stage[n], ACT.Copy) \
                        .then_inc(w_hi, 1)
                if normed_twice:
                    act.wait_ge(qbias_mm, 1)
                    nc.scalar.activation(cols[:, BQ], o_bank[:, 0:KC], ACT.Copy).then_inc(cols_ready, 1)
                    act.wait_ge(cols_ready, 1)
                act.wait_ge(cols_loaded, NCOLS * 16)

                def hi_of(el, u):
                    act.wait_ge(x_done, el.n * NU + USES.index(u) + 1)
                    src = x_bank[USES.index(u) % 2]
                    t = int(u[-1])
                    if u[0] == "v":
                        nc.scalar.activation(vb[:, el.par, t], src[:], ACT.Copy).then_inc(v_done, 1)
                    elif u[0] == "t":
                        dst = {"c": cT, "x": xnT}[u[1]]
                        nc.scalar.activation(dst[:, HI, :, t * P:(t + 1) * P],
                                             src[:].rearrange("p (k n) -> p k n", k=KC), ACT.Copy) \
                            .then_inc(hi_done, 1)
                    else:
                        dst = {"q": qT, "k": kT}[u[0]]
                        fs, bias = feature_rows(u)
                        if bias is None:
                            nc.scalar.activation(dst[:, el.par, HI, fs[0]:fs[0] + 2].rearrange("p f n -> p (f n)"),
                                                 src[:], ACT.Copy).then_inc(hi_done, 1)
                        else:
                            for m, f in enumerate(fs):
                                last = nc.scalar.activation(dst[:, el.par, HI, f], src[:, m * SEQ:(m + 1) * SEQ],
                                                            ACT.Identity, bias=cols[:, bias, f:f + 1])
                            last.then_inc(hi_done, 1)

                def exps(el, p, hs=(0, 1)):
                    for h in hs:
                        for t in range(QT):
                            act.wait_ge(ttr_done, (el.n * pairs + p) * 2 * QT + 2 * h + t + 1)
                            pr = probs[:, p % ring, h, t]
                            nc.scalar.activation(pr, pr, ACT.Exp, bias=negm[:, p % ring, h, t:t + 1], scale=-1.0,
                                                 accum_out=ssum[:, p % ring, 2 * h + t:2 * h + t + 1]) \
                                .then_inc(exp_done, 1)

                def probs_out(el, p):
                    h = 2 * p + 1
                    act.wait_ge(pt_done, el.n * heads + h + 1)
                    nc.scalar.activation(pT[:, (h // hpg) % 2, h % hpg].rearrange("p t n -> p (t n)"),
                                         pt_bank[:], ACT.Copy).then_inc(odd_out, 1)

                def attn_hi(el, g):
                    act.wait_ge(pv_done, el.n * GROUPS + g + 1)
                    if v_bias is None:
                        nc.scalar.activation(oT[:, HI, g], o_bank[:, 0:SEQ], ACT.Copy).then_inc(othi_done, 1)
                    else:
                        nc.scalar.activation(oT[:, HI, g], o_bank[:, 0:SEQ], ACT.Identity,
                                             bias=cols[:, BV, g:g + 1]).then_inc(othi_done, 1)

                for u in USES:
                    hi_of(Element(0, 0, batches), u)
                for u in LEAD:
                    hi_of(Element(0, 1, batches), u)

                def iteration(el):
                    exps(el, 0)
                    exps(el, 1)
                    for u in HEAD if el.has(1) else ():
                        hi_of(el.plus(1), u)
                    for p in range(pairs):
                        if p == 0:
                            exps(el, 2)
                        for u in finished(BETWEEN[p]) if el.has(1) else ():
                            hi_of(el.plus(1), u)
                        probs_out(el, p)
                        if group_after(p - 1) is not None:
                            attn_hi(el, group_after(p - 1))
                        if p + 3 < pairs:
                            exps(el, p + 3, (0,))
                        for u in finished(MID[p]) if el.has(1) else ():
                            hi_of(el.plus(1), u)
                        if p + 3 < pairs:
                            exps(el, p + 3, (1,))
                    for u in finished(LAST[0]) if el.has(1) else ():
                        hi_of(el.plus(1), u)
                    attn_hi(el, GROUPS - 1)
                    for u in finished(LAST[1]) if el.has(1) else ():
                        hi_of(el.plus(1), u)
                    if el.has(2):
                        hi_of(el.plus(2), LEAD[0])
                    if el.has(2):
                        hi_of(el.plus(2), LEAD[1])

                run_elements(act, batches, iteration)

            @block.vector
            def _(dve):
                if normed_twice:
                    dve.wait_ge(w_loaded[0], 16)
                    dve.wait_ge(cols_loaded, NCOLS * 16)
                    dve.wait_ge(qbias_mm, 1)
                    for k in range(KC):
                        wk_rows = stage[0][:, k * DIM:(k + 1) * DIM]
                        nc.vector.tensor_scalar(wk_rows, wk_rows, cols[:, GAIN, k:k + 1], None, ALU.mult) \
                            .then_inc(w_gained, 1)
                    dve.wait_ge(w_gained, KC)
                for n, w in enumerate(weights):
                    dve.wait_ge(w_hi, n + 1)
                    nc.vector.tensor_tensor(w[:, LO].rearrange("p k n -> p (k n)"), stage[n],
                                            w[:, HI].rearrange("p k n -> p (k n)").bitcast(F32), ALU.subtract) \
                        .then_inc(w_lo, 1)
                if normed_twice:
                    dve.wait_ge(cols_ready, 1)
                dve.wait_ge(cols_loaded, NCOLS * 16)

                def row_stats(el):
                    dve.wait_ge(x_loaded[el.par], el.dma())
                    wait_for(dve, xn_ready, el.n * QT)
                    for t in range(QT):
                        nc.vector.bn_stats(stats[:, t], xbuf[:, el.par, t]).then_inc(bn_done, 1)
                    wait_apart(dve, bn_done, (el.n + 1) * QT)
                    for t in range(QT):
                        last = nc.vector.bn_aggr(mv[:, t], stats[:, t])
                    last.then_inc(stats_ready, 1)

                def mask_bias(el):
                    dve.wait_ge(m_loaded[el.par], el.dma())
                    nc.vector.tensor_scalar(mbias[:, el.par], mraw[:, el.par], 0.0, mask_value,
                                            ALU.is_equal, ALU.mult).then_inc(mbias_ready, 1)

                def scores_out(el, p):
                    wait_apart(dve, s_done, el.n * pairs + p + 1)
                    for h in range(2):
                        for t in range(QT):
                            nc.vector.tensor_tensor_reduce(
                                out=probs[:, p % ring, h, t], in0=s_bank[2 * (p % 2) + h][:, t * SEQ:(t + 1) * SEQ],
                                in1=mbias[:, el.par], scale=-sm_scale, scalar=BIG, op0=ALU.add, op1=ALU.min,
                                accum_out=negm[:, p % ring, h, t:t + 1]).then_inc(ttr_done, 1)

                def probs_out(el, p):
                    h = 2 * p
                    dve.wait_ge(pt_done, el.n * heads + h + 1)
                    nc.vector.tensor_copy(pT[:, (h // hpg) % 2, h % hpg].rearrange("p t n -> p (t n)"), pt_bank[:]) \
                        .then_inc(even_out, 1)

                def recip(el, p):
                    dve.wait_ge(exp_done, (el.n * pairs + p + 1) * 2 * QT)
                    nc.vector.reciprocal(rinv[:, p % ring], ssum[:, p % ring]).then_inc(recip_done, 1)
                    dve.wait_ge(recip_done, el.n * pairs + p + 1)
                    for t in range(QT):
                        pr = probs[:, p % ring, 0, t]
                        last = nc.vector.tensor_scalar(pr, pr, rinv[:, p % ring, t:t + 1], None, ALU.mult)
                    last.then_inc(even_normed, 1)

                def lo_of(el, u):
                    if u[0] == "v":
                        return
                    dve.wait_ge(hi_done, el.n * NL + SPLIT.index(u) + 1)
                    src = x_bank[USES.index(u) % 2]
                    t = int(u[-1])
                    if u[0] == "t":
                        dst = {"c": cT, "x": xnT}[u[1]]
                        cut = slice(t * P, (t + 1) * P)
                        nc.vector.tensor_tensor(dst[:, LO, :, cut], src[:].rearrange("p (k n) -> p k n", k=KC),
                                                dst[:, HI, :, cut].bitcast(F32), ALU.subtract).then_inc(lo_done, 1)
                        return
                    dst = {"q": qT, "k": kT}[u[0]]
                    fs, bias = feature_rows(u)
                    if bias is None:
                        hi, lo = (dst[:, el.par, part, fs[0]:fs[0] + 2].rearrange("p f n -> p (f n)")
                                  for part in (HI, LO))
                        nc.vector.tensor_tensor(lo, src[:], hi.bitcast(F32), ALU.subtract).then_inc(lo_done, 1)
                    else:
                        for m, f in enumerate(fs):
                            last = nc.vector.scalar_tensor_tensor(
                                dst[:, el.par, LO, f], src[:, m * SEQ:(m + 1) * SEQ], cols[:, bias, f:f + 1],
                                dst[:, el.par, HI, f].bitcast(F32), ALU.add, ALU.subtract)
                        last.then_inc(lo_done, 1)

                def attn_lo(el, g):
                    dve.wait_ge(othi_done, el.n * GROUPS + g + 1)
                    if v_bias is None:
                        nc.vector.tensor_tensor(oT[:, LO, g], o_bank[:, 0:SEQ], oT[:, HI, g].bitcast(F32),
                                                ALU.subtract).then_inc(otlo_done, 1)
                    else:
                        nc.vector.scalar_tensor_tensor(oT[:, LO, g], o_bank[:, 0:SEQ], cols[:, BV, g:g + 1],
                                                       oT[:, HI, g].bitcast(F32), ALU.add, ALU.subtract) \
                            .then_inc(otlo_done, 1)

                def rows_out(el):
                    if out_bias is None:
                        dve.wait_ge(r_loaded[el.par], el.dma())
                    else:
                        dve.wait_ge(res_ready, (el.n + 1) * QT)
                    for t in range(QT):
                        dve.wait_ge(op_done, el.n * QT + t + 1)
                        nc.vector.tensor_tensor(resb[:, el.par, t], s_bank[2 + t][:], resb[:, el.par, t], ALU.add) \
                            .then_inc(out_done, 1)

                row_stats(Element(0, 0, batches))
                mask_bias(Element(0, 0, batches))
                for u in USES:
                    lo_of(Element(0, 0, batches), u)
                row_stats(Element(0, 1, batches))
                for u in LEAD:
                    lo_of(Element(0, 1, batches), u)

                def iteration(el):
                    scores_out(el, 0)
                    scores_out(el, 1)
                    recip(el, 0)
                    recip(el, 1)
                    scores_out(el, 2)
                    for u in HEAD if el.has(1) else ():
                        lo_of(el.plus(1), u)
                    for p in range(pairs):
                        probs_out(el, p)
                        if p == 0 and el.has(1):
                            mask_bias(el.plus(1))
                        for u in finished(MID[p - 1]) if p > 0 and el.has(1) else ():
                            lo_of(el.plus(1), u)
                        if p + 3 < pairs:
                            scores_out(el, p + 3)
                        if p + 2 < pairs:
                            recip(el, p + 2)
                        for u in finished(BETWEEN[p]) if el.has(1) else ():
                            lo_of(el.plus(1), u)
                        if group_after(p - 1) is not None:
                            attn_lo(el, group_after(p - 1))
                        if p == pairs - 1 and el.has(2):
                            row_stats(el.plus(2))
                    for u in finished(MID[pairs - 1] + LAST[0]) if el.has(1) else ():
                        lo_of(el.plus(1), u)
                    attn_lo(el, GROUPS - 1)
                    for u in finished(LAST[1]) if el.has(1) else ():
                        lo_of(el.plus(1), u)
                    if el.has(2):
                        lo_of(el.plus(2), LEAD[0])
                    rows_out(el)
                    if el.has(2):
                        lo_of(el.plus(2), LEAD[1])

                run_elements(dve, batches, iteration)

            @block.tensor
            def _(pe):
                if normed_twice:
                    pe.wait_ge(w_loaded[0], 16)
                    pe.wait_ge(cols_loaded, NCOLS * 16)
                    for f in range(KC):
                        for k in range(KC):
                            last = nc.tensor.matmul(o_bank[:, f:f + 1], stage[0][:, k * DIM + f * P:k * DIM + (f + 1) * P],
                                                    cols[:, LBIAS, k:k + 1], start=(k == 0), stop=(k == KC - 1))
                    last.then_inc(qbias_mm, 1)
                    pe.wait_ge(cols_ready, 1)
                pe.wait_ge(w_lo, 4)
                pe.wait_ge(consts_ready, 2)

                def use(el, u):
                    part, u = (u[-1], u[:-1]) if u[-1] in "ab" else ("", u)
                    n = USES.index(u)
                    before = el if n >= 2 else el.plus(-1)
                    prev = USES[(n - 2) % NU]
                    if part == "b":
                        pass
                    elif prev[0] == "v":
                        wait_for(pe, v_done, before.n * QT + int(prev[1]) + 1)
                    else:
                        wait_for(pe, lo_done, before.n * NL + SPLIT.index(prev) + 1)
                    dst, t = x_bank[n % 2], int(u[-1])
                    if u[0] == "t":
                        if u[1] == "x":
                            pe.wait_ge(xn_ready, el.n * QT + t + 1)
                            src = xn[:, t]
                        else:
                            pe.wait_ge(c_loaded[el.par], el.dma())
                            src = cbuf[:, el.par, t]
                        for k in range(KC):
                            last = nc.tensor.transpose(dst[:, k * P:(k + 1) * P], src[:, k * P:(k + 1) * P], ident[:])
                    elif u[0] == "v":
                        pe.wait_ge(lo_done, el.n * NL + SPLIT.index("tc1") + 1)
                        for k in {"a": range(KC // 2), "b": range(KC // 2, KC), "": range(KC)}[part]:
                            for a, b in TERMS:
                                last = nc.tensor.matmul(dst[:], cT[:, a, k, t * P:(t + 1) * P], wv[:, b, k],
                                                        start=(k == 0 and (a, b) == TERMS[0]),
                                                        stop=(k == KC - 1 and (a, b) == TERMS[-1]))
                    else:
                        w, src, need = (wq, xnT, "tx1") if u[0] == "q" else (wk, cT, "tc1")
                        pe.wait_ge(lo_done, el.n * NL + SPLIT.index(need) + 1)
                        for m, f in enumerate(feature_rows(u)[0]):
                            if part == "ab"[1 - m]:
                                continue
                            for k in range(KC):
                                for a, b in TERMS:
                                    last = nc.tensor.matmul(dst[:, m * SEQ:(m + 1) * SEQ],
                                                            w[:, b, k, f * P:(f + 1) * P], src[:, a, k],
                                                            start=(k == 0 and (a, b) == TERMS[0]),
                                                            stop=(k == KC - 1 and (a, b) == TERMS[-1]))
                    if part != "a":
                        last.then_inc(x_done, 1)

                def scores(el, p):
                    if p == 0:
                        pe.wait_ge(lo_done, (el.n + 1) * NL)
                    wait_for(pe, ttr_done, (el.n * pairs + p - 1) * 2 * QT)
                    if p == 1:
                        wait_for(pe, out_done, el.n * QT)
                    for t in range(QT):
                        for a, b in TERMS:
                            for m in range(2):
                                h = 2 * p + m
                                r = slice((h % hpg) * hd, (h % hpg + 1) * hd)
                                last = nc.tensor.matmul(
                                    s_bank[2 * (p % 2) + m][:, t * SEQ:(t + 1) * SEQ],
                                    qT[r, el.par, a, h // hpg, t * P:(t + 1) * P], kT[r, el.par, b, h // hpg],
                                    start=((a, b) == TERMS[0]), stop=((a, b) == TERMS[-1]))
                    last.then_inc(s_done, 1)

                def transpose_probs(el, h):
                    p, m = h // 2, h % 2
                    pe.wait_ge(odd_normed if m else even_normed, el.n * pairs + p + 1)
                    wait_for(pe, even_out if m else odd_out, el.n * pairs + p + m)
                    for kt in range(QT):
                        for t in range(QT):
                            last = nc.tensor.transpose(pt_bank[:, kt * SEQ + t * P:kt * SEQ + (t + 1) * P],
                                                       probs[:, p % ring, m, t, kt * P:(kt + 1) * P], ident[:])
                    last.then_inc(pt_done, 1)

                def probs_v(el, g):
                    pe.wait_ge(even_out, el.n * pairs + (g + 1) * hpg // 2)
                    pe.wait_ge(odd_out, el.n * pairs + (g + 1) * hpg // 2)
                    pe.wait_ge(v_done, (el.n + 1) * QT)
                    wait_for(pe, otlo_done, el.n * GROUPS + g)
                    for kt in range(QT):
                        for m in range(hpg):
                            c = slice(m * hd, (m + 1) * hd)
                            last = nc.tensor.matmul(o_bank[c, 0:SEQ], vb[:, el.par, kt, g * P + m * hd:g * P + (m + 1) * hd],
                                                    pT[:, g % 2, m, kt], start=(kt == 0), stop=(kt == QT - 1),
                                                    skip_group_check=True)
                    last.then_inc(pv_done, 1)

                def project(el):
                    for t in range(QT):
                        for k in range(KC):
                            if t == 0:
                                pe.wait_ge(otlo_done, el.n * GROUPS + k + 1)
                            for a, b in TERMS:
                                last = nc.tensor.matmul(s_bank[2 + t][:], oT[:, a, k, t * P:(t + 1) * P], wo[:, b, k],
                                                        start=(k == 0 and (a, b) == TERMS[0]),
                                                        stop=(k == KC - 1 and (a, b) == TERMS[-1]))
                        last.then_inc(op_done, 1)

                for u in USES:
                    use(Element(0, 0, batches), u)
                for u in LEAD:
                    use(Element(0, 1, batches), u)

                def iteration(el):
                    scores(el, 0)
                    scores(el, 1)
                    for u in HEAD if el.has(1) else ():
                        use(el.plus(1), u)
                    scores(el, 2)
                    for p in range(pairs):
                        transpose_probs(el, 2 * p)
                        if p + 3 < pairs:
                            scores(el, p + 3)
                        for u in BETWEEN[p] if el.has(1) else ():
                            use(el.plus(1), u)
                        transpose_probs(el, 2 * p + 1)
                        if group_after(p - 1) is not None:
                            probs_v(el, group_after(p - 1))
                        for u in MID[p] if el.has(1) else ():
                            use(el.plus(1), u)
                    for u in LAST[0] if el.has(1) else ():
                        use(el.plus(1), u)
                    probs_v(el, GROUPS - 1)
                    for u in LAST[1] if el.has(1) else ():
                        use(el.plus(1), u)
                    if el.has(2):
                        use(el.plus(2), LEAD[0])
                    project(el)
                    if el.has(2):
                        use(el.plus(2), LEAD[1])

                run_elements(pe, batches, iteration)

        clear_semaphores(nc, sems)


def ternary_ffn_phase(nc, tag, x_in, x_out, w_gate, w_up, w_down, tiles=TOK // P):
    inner = w_gate.shape[0]
    NC = inner // DIM
    IK = inner // P
    WN = inner * DIM // P
    MAGIC = 1.5 * 2.0 ** 23
    QMAX = 127.0

    with ExitStack() as ctx:
        def sb(name, shape, dt=F32):
            return ctx.enter_context(nc.sbuf_tensor(f"{tag}_{name}", shape, dt))

        sems = []

        def sem(name):
            sems.append(ctx.enter_context(nc.semaphore(f"{tag}_{name}")))
            return sems[-1]

        wg = sb("wg", [P, KC, inner], BF16)
        wu = sb("wu", [P, KC, inner], BF16)
        wd = sb("wd", [P, IK, DIM], BF16)
        wscale = sb("wscale", [P, 3])
        ident = sb("ident", [P, P], BF16)

        with ExitStack() as prep:
            def psb(name, shape, dt=F32):
                return prep.enter_context(nc.sbuf_tensor(f"{tag}_{name}", shape, dt))

            raw = psb("raw", [P, 3, WN])
            tern = psb("tern", [P, 3, WN], BF16)
            ones = psb("ones", [P, P])
            wsum = psb("wsum", [P, 3, 4])
            wpart = psb("wpart", [P, 3])
            winv = psb("winv", [P, 3])
            wmean = psb("wmean", [P, 3])
            sum_bank = prep.enter_context(nc.psum_tensor(f"{tag}_sum_bank", [P, 512], F32))
            t_bank = [prep.enter_context(nc.psum_tensor(f"{tag}_t_bank{i}", [P, 1024], BF16)) for i in range(4)]
            (w_abs, w_part, w_total, w_scale, w_step, w_ternary, w_turned, w_out_act, w_out_dve, consts_ready,
             ident_zero) = [sem(n) for n in ("w_abs w_part w_total w_scale w_step w_ternary w_turned w_out_act "
                                             "w_out_dve consts_ready ident_zero").split()]
            w_loaded = [sem(f"w_loaded{i}") for i in range(3)]
            SLICES = 4
            SN = WN // SLICES
            turns = []
            for n, dst in enumerate((wg, wu)):
                for k in range(KC):
                    for half in range(IK // 8):
                        pieces = [(o, k) for o in range(half * 8, half * 8 + 8)]
                        turns.append((n, dst[:, k, half * 1024:(half + 1) * 1024],
                                      [(o * DIM + k * P) for o, k in pieces]))
            for ik in range(0, IK, 2):
                turns.append((2, wd[:, ik:ik + 2].rearrange("p a b -> p (a b)"),
                              [o * inner + (ik + a) * P for a in range(2) for o in range(KC)]))

            with nc.Block() as block:
                @block.sync
                def _(sp):
                    for n, w in enumerate((w_gate, w_up, w_down)):
                        cols = w.shape[1]
                        sp.dma_start(raw[:, n].rearrange("p (t c) -> p t c", c=cols),
                                     w.rearrange("(t p) c -> p t c", p=P)).then_inc(w_loaded[n], 16)

                @block.gpsimd
                def _(pool):
                    nc.gpsimd.memset(ident[:], 0.0).then_inc(ident_zero, 1)
                    nc.gpsimd.memset(ones[:], 1.0).then_inc(consts_ready, 1)
                    pool.wait_ge(ident_zero, 1)
                    nc.gpsimd.affine_select(out=ident[:], in_=ident[:], compare_op=ALU.not_equal, fill=1.0, base=0,
                                            pattern=[[-1, P]], channel_multiplier=1).then_inc(consts_ready, 1)

                @block.scalar
                def _(act):
                    for n in range(3):
                        act.wait_ge(w_loaded[n], 16)
                        for c in range(SLICES):
                            nc.scalar.activation(tern[:, n, c * SN:(c + 1) * SN], raw[:, n, c * SN:(c + 1) * SN], ACT.Abs,
                                                 accum_out=wsum[:, n, c:c + 1]).then_inc(w_abs, 1)
                    for n in range(3):
                        for c in range(SLICES):
                            act.wait_ge(w_step, n * 2 * SLICES + 2 * c + 2)
                            nc.scalar.activation(tern[:, n, c * SN:(c + 1) * SN], raw[:, n, c * SN:(c + 1) * SN],
                                                 ACT.Copy, bias=-MAGIC).then_inc(w_ternary, 1)
                        for i, (m, dst, src) in enumerate(turns):
                            if m == n and i % 2 == 0:
                                act.wait_ge(w_turned, i + 1)
                                nc.scalar.activation(dst, t_bank[i % 4][:], ACT.Copy).then_inc(w_out_act, 1)

                @block.vector
                def _(dve):
                    for n in range(3):
                        dve.wait_ge(w_abs, (n + 1) * SLICES)
                        nc.vector.reduce_sum(wpart[:, n:n + 1], wsum[:, n], AX.X).then_inc(w_part, 1)
                    for n in range(3):
                        dve.wait_ge(w_total, n + 1)
                        nc.vector.tensor_scalar(wmean[:, n:n + 1], sum_bank[:, n:n + 1], 1.0 / (inner * DIM), None,
                                                ALU.mult).then_inc(w_scale, 1)
                        dve.wait_ge(w_scale, 3 * n + 1)
                        nc.vector.tensor_scalar(wscale[:, n:n + 1], wmean[:, n:n + 1], 1e-5, None,
                                                ALU.max).then_inc(w_scale, 1)
                        dve.wait_ge(w_scale, 3 * n + 2)
                        nc.vector.reciprocal(winv[:, n:n + 1], wscale[:, n:n + 1]).then_inc(w_scale, 1)
                    dve.wait_ge(w_scale, 9)
                    for n in range(3):
                        for c in range(SLICES):
                            piece = raw[:, n, c * SN:(c + 1) * SN]
                            nc.vector.tensor_scalar(piece, piece, winv[:, n:n + 1], 1.0, ALU.mult, ALU.min) \
                                .then_inc(w_step, 1)
                            dve.wait_ge(w_step, n * 2 * SLICES + 2 * c + 1)
                            nc.vector.tensor_scalar(piece, piece, -1.0, MAGIC, ALU.max, ALU.add).then_inc(w_step, 1)
                        for i, (m, dst, src) in enumerate(turns):
                            if m == n and i % 2 == 1:
                                dve.wait_ge(w_turned, i + 1)
                                nc.vector.tensor_copy(dst, t_bank[i % 4][:]).then_inc(w_out_dve, 1)

                @block.tensor
                def _(pe):
                    pe.wait_ge(consts_ready, 2)
                    for n in range(3):
                        pe.wait_ge(w_part, n + 1)
                        nc.tensor.matmul(sum_bank[:, n:n + 1], ones[:], wpart[:, n:n + 1], start=True, stop=True) \
                            .then_inc(w_total, 1)
                        if n < 2:
                            pe.wait_ge(w_scale, 3 * n + 1)
                    for i, (n, dst, src) in enumerate(turns):
                        pe.wait_ge(w_ternary, (n + 1) * SLICES)
                        if i >= 4:
                            pe.wait_ge(w_out_dve if i % 2 else w_out_act, (i - 4) // 2 + 1)
                        for m, at in enumerate(src):
                            last = nc.tensor.transpose(t_bank[i % 4][:, m * P:(m + 1) * P], tern[:, n, at:at + P], ident[:])
                        last.then_inc(w_turned, 1)

        neg_half = sb("neg_half", [P, 1])
        xbuf = sb("xbuf", [P, 2, DIM])
        resb = sb("resb", [P, 2, DIM])
        stats = sb("stats", [P, 2, 6])
        mv = sb("mv", [P, 2, 2])
        ln = sb("ln", [P, 2, 4])
        xn = sb("xn", [P, 2, DIM])
        xmax = sb("xmax", [P, 2, 3])
        xs = sb("xs", [P, 2, 2])
        xround = sb("xround", [P, 2, DIM])
        xq = sb("xq", [P, 2, DIM], BF16)
        xqT = sb("xqT", [P, 2, KC, P], BF16)
        gate = sb("gate", [P, 4, DIM])
        hid = sb("hid", [P, 2, inner])
        hmax = sb("hmax", [P, 2, 3])
        hpart = sb("hpart", [P, 2, NC])
        hs = sb("hs", [P, 2, 1])
        hround = sb("hround", [P, 2, inner])
        hq = sb("hq", [P, 2, inner], BF16)
        hqT = sb("hqT", [P, 2, IK, P], BF16)

        g_bank = [ctx.enter_context(nc.psum_tensor(f"{tag}_g{i}", [P, 512], F32)) for i in range(2)]
        u_bank = [ctx.enter_context(nc.psum_tensor(f"{tag}_u{i}", [P, 512], F32)) for i in range(2)]
        tx_bank = ctx.enter_context(nc.psum_tensor(f"{tag}_tx", [P, 1024], BF16))
        th_bank = [ctx.enter_context(nc.psum_tensor(f"{tag}_th{i}", [P, 1024], BF16)) for i in range(IK // 8)]
        d_bank = ctx.enter_context(nc.psum_tensor(f"{tag}_d", [P, 512], F32))
        TH = IK // 8

        (const_ready, x_loaded0, x_loaded1, r_loaded0, r_loaded1, stored0, stored1, bn_done, stats_ready, ln_step,
         xn_ready, xmax_ready, xmax_step, xs_ready, x_round, xq_ready, tx_done, th_done, tx_out, th_out, g_done, silu_done, u_done,
         h_done, hmax_step, hpart_ready, hs_ready, hmax_ready, h_round, hq_ready, d_done, out_done) = [sem(n) for n in (
             "const_ready x_loaded0 x_loaded1 r_loaded0 r_loaded1 stored0 stored1 bn_done stats_ready ln_step "
             "xn_ready xmax_ready xmax_step xs_ready x_round xq_ready tx_done th_done tx_out th_out g_done silu_done u_done "
             "h_done hmax_step hpart_ready hs_ready hmax_ready h_round hq_ready d_done out_done").split()]
        x_loaded, r_loaded, stored = (x_loaded0, x_loaded1), (r_loaded0, r_loaded1), (stored0, stored1)
        first = [Element(0, n, tiles) for n in range(4)]

        def rows(t, el):
            return t[bass.ts(el.n, P), :]

        def quant_scales(dve, el, m, step):
            nc.vector.tensor_scalar(m[:, 1:2], m[:, 0:1], 1e-5, 1.0 / QMAX, ALU.max, ALU.mult).then_inc(step, 1)
            wait_apart(dve, step, el.n * 2 + 1)
            nc.vector.reciprocal(m[:, 2:3], m[:, 1:2]).then_inc(step, 1)

        with nc.Block() as block:
            @block.sync
            def _(sp):
                def load_x(el):
                    src = rows(x_in, el)
                    wait_apart(sp, xn_ready, el.n - 1)
                    sp.dma_start(xbuf[:, el.par], src).then_inc(x_loaded[el.par], 16)

                def load_res(el):
                    src, prev = rows(x_in, el), el.plus(-2)
                    wait_apart(sp, stored[el.par], prev.dma())
                    sp.dma_start(resb[:, el.par], src).then_inc(r_loaded[el.par], 16)

                for el in first:
                    load_x(el)
                load_res(first[0])

                def iteration(el):
                    if el.has(4):
                        load_x(el.plus(4))
                    if el.has(1):
                        load_res(el.plus(1))
                    dst = rows(x_out, el)
                    wait_apart(sp, out_done, el.n + 1)
                    sp.dma_start(dst, resb[:, el.par]).then_inc(stored[el.par], 16)

                run_elements(sp, tiles, iteration, ahead=4)
                for par in range(2):
                    sp.wait_ge(stored[par], tiles // 2 * 16)

            @block.gpsimd
            def _(pool):
                nc.gpsimd.memset(neg_half[:], -0.5).then_inc(const_ready, 1)
                pool.wait_ge(const_ready, 1)

                def normalise(el):
                    def chained(k, ins):
                        ins.then_inc(ln_step, 1)
                        wait_apart(pool, ln_step, el.n * 4 + k)

                    wait_apart(pool, stats_ready, el.n + 1)
                    l, m = ln[:, el.par], mv[:, el.par]
                    chained(1, nc.gpsimd.tensor_scalar(l[:, 0:1], m[:, 1:2], 1.0, EPS, ALU.mult, ALU.add))
                    chained(2, nc.gpsimd.tensor_tensor(l[:, 1:2], l[:, 0:1], neg_half[:], ALU.pow))
                    chained(3, nc.gpsimd.tensor_tensor(l[:, 2:3], m[:, 0:1], l[:, 1:2], ALU.mult))
                    chained(4, nc.gpsimd.tensor_scalar(l[:, 3:4], l[:, 2:3], -1.0, 0.0, ALU.mult, ALU.add))
                    wait_apart(pool, xmax_ready, el.n - 1)
                    nc.gpsimd.tensor_scalar(xn[:, el.par], xbuf[:, el.par], l[:, 1:2], l[:, 3:4],
                                            ALU.mult, ALU.add).then_inc(xn_ready, 1)

                def quantise_x(el):
                    wait_apart(pool, xmax_step, el.n * 2 + 2)
                    nc.gpsimd.tensor_scalar(xround[:, el.par], xn[:, el.par], xmax[:, el.par, 2:3], MAGIC,
                                            ALU.mult, ALU.add).then_inc(x_round, 1)
                    wait_apart(pool, x_round, el.n + 1)
                    wait_apart(pool, tx_done, el.n - 1)
                    nc.gpsimd.tensor_scalar(xq[:, el.par], xround[:, el.par], -MAGIC, 1.0,
                                            ALU.add, ALU.mult).then_inc(xq_ready, 1)

                def quantise_h(el):
                    wait_apart(pool, hmax_step, el.n * 2 + 2)
                    nc.gpsimd.tensor_scalar(hround[:, el.par], hid[:, el.par], hmax[:, el.par, 2:3], MAGIC,
                                            ALU.mult, ALU.add).then_inc(h_round, 1)
                    wait_apart(pool, h_round, el.n + 1)
                    wait_apart(pool, th_done, (el.n - 1) * TH)
                    nc.gpsimd.tensor_scalar(hq[:, el.par], hround[:, el.par], -MAGIC, 1.0,
                                            ALU.add, ALU.mult).then_inc(hq_ready, 1)

                normalise(first[0])
                quantise_x(first[0])
                normalise(first[1])
                quantise_x(first[1])
                normalise(first[2])
                quantise_h(first[0])

                def iteration(el):
                    if el.has(2):
                        quantise_x(el.plus(2))
                    if el.has(3):
                        normalise(el.plus(3))
                    if el.has(1):
                        quantise_h(el.plus(1))

                run_elements(pool, tiles, iteration, ahead=4)

            @block.scalar
            def _(act):
                def turned_x(el):
                    act.wait_ge(tx_done, el.n + 1)
                    nc.scalar.activation(xqT[:, el.par].rearrange("p k n -> p (k n)"), tx_bank[:, 0:DIM],
                                         ACT.Copy).then_inc(tx_out, 1)

                def silus(el, cs):
                    for c in cs:
                        act.wait_ge(g_done, el.n * NC + c + 1)
                        wait_for(act, h_done, (el.n - 1) * NC + c + 1)
                        if c == 0:
                            act.wait_ge(xs_ready, el.n * 2 + 1)
                        nc.scalar.activation(gate[:, c % 4], g_bank[c % 2][:], ACT.Silu, scale=xs[:, el.par, 0:1]) \
                            .then_inc(silu_done, 1)

                def turned_h(el):
                    for m in range(IK // 8):
                        act.wait_ge(th_done, el.n * TH + m + 1)
                        nc.scalar.activation(hqT[:, el.par, 8 * m:8 * m + 8].rearrange("p k n -> p (k n)"),
                                             th_bank[m][:], ACT.Copy).then_inc(th_out, 1)

                turned_x(first[0])
                silus(first[0], range(NC))
                turned_x(first[1])

                def iteration(el):
                    if el.has(1):
                        silus(el.plus(1), range(NC - 1))
                    turned_h(el)
                    if el.has(1):
                        silus(el.plus(1), range(NC - 1, NC))
                    if el.has(2):
                        turned_x(el.plus(2))

                run_elements(act, tiles, iteration, ahead=4)

            @block.vector
            def _(dve):
                def row_stats(el):
                    dve.wait_ge(x_loaded[el.par], el.dma())
                    wait_for(dve, ln_step, (el.n - 1) * 4)
                    nc.vector.bn_stats(stats[:, el.par], xbuf[:, el.par]).then_inc(bn_done, 1)
                    wait_apart(dve, bn_done, el.n + 1)
                    nc.vector.bn_aggr(mv[:, el.par], stats[:, el.par]).then_inc(stats_ready, 1)

                def x_scale(el):
                    dve.wait_ge(xn_ready, el.n + 1)
                    wait_for(dve, x_round, el.n - 1)
                    nc.vector.tensor_reduce(xmax[:, el.par, 0:1], xn[:, el.par], AX.X, ALU.max,
                                            apply_absolute_value=True).then_inc(xmax_ready, 1)
                    wait_apart(dve, xmax_ready, el.n + 1)
                    quant_scales(dve, el, xmax[:, el.par], xmax_step)
                    wait_for(dve, silu_done, (el.n - 1) * NC)
                    for n in range(2):
                        nc.vector.tensor_tensor(xs[:, el.par, n:n + 1], xmax[:, el.par, 1:2], wscale[:, n:n + 1],
                                                ALU.mult).then_inc(xs_ready, 1)

                def hidden(el):
                    wait_for(dve, h_round, el.n - 1)
                    dve.wait_ge(xs_ready, (el.n + 1) * 2)
                    def largest(c):
                        dve.wait_ge(h_done, el.n * NC + c + 1)
                        nc.vector.tensor_reduce(hpart[:, el.par, c:c + 1], hid[:, el.par, c * DIM:(c + 1) * DIM], AX.X,
                                                ALU.max, apply_absolute_value=True).then_inc(hpart_ready, 1)

                    for c in range(NC):
                        dve.wait_ge(u_done, el.n * NC + c + 1)
                        dve.wait_ge(silu_done, el.n * NC + c + 1)
                        nc.vector.scalar_tensor_tensor(hid[:, el.par, c * DIM:(c + 1) * DIM], u_bank[c % 2][:],
                                                       xs[:, el.par, 1:2], gate[:, c % 4], ALU.mult, ALU.mult) \
                            .then_inc(h_done, 1)
                        if c > 0:
                            largest(c - 1)
                    largest(NC - 1)
                    dve.wait_ge(hpart_ready, (el.n + 1) * NC)
                    nc.vector.reduce_max(hmax[:, el.par, 0:1], hpart[:, el.par], AX.X).then_inc(hmax_ready, 1)
                    wait_apart(dve, hmax_ready, el.n + 1)
                    quant_scales(dve, el, hmax[:, el.par], hmax_step)
                    nc.vector.tensor_tensor(hs[:, el.par], hmax[:, el.par, 1:2], wscale[:, 2:3], ALU.mult) \
                        .then_inc(hs_ready, 1)

                def rows_out(el):
                    dve.wait_ge(r_loaded[el.par], el.dma())
                    dve.wait_ge(hs_ready, el.n + 1)
                    dve.wait_ge(d_done, el.n + 1)
                    nc.vector.scalar_tensor_tensor(resb[:, el.par], d_bank[:], hs[:, el.par], resb[:, el.par],
                                                   ALU.mult, ALU.add).then_inc(out_done, 1)

                for el in first[:2]:
                    row_stats(el)
                    x_scale(el)
                row_stats(first[2])
                hidden(first[0])

                def iteration(el):
                    if el.has(2):
                        x_scale(el.plus(2))
                    if el.has(3):
                        row_stats(el.plus(3))
                    if el.has(1):
                        hidden(el.plus(1))
                    rows_out(el)

                run_elements(dve, tiles, iteration, ahead=4)

            @block.tensor
            def _(pe):
                def turn_x(el):
                    pe.wait_ge(xq_ready, el.n + 1)
                    wait_for(pe, tx_out, el.n)
                    for k in range(KC):
                        last = nc.tensor.transpose(tx_bank[:, k * P:(k + 1) * P], xq[:, el.par, k * P:(k + 1) * P], ident[:])
                    last.then_inc(tx_done, 1)

                def gate_up(el, cs):
                    if cs[0] == 0:
                        pe.wait_ge(tx_out, el.n + 1)
                    for c in cs:
                        for w, bank, done, read in ((wg, g_bank, g_done, silu_done), (wu, u_bank, u_done, h_done)):
                            wait_for(pe, read, el.n * NC + c - 1)
                            for k in range(KC):
                                last = nc.tensor.matmul(bank[c % 2][:], xqT[:, el.par, k], w[:, k, c * DIM:(c + 1) * DIM],
                                                        start=(k == 0), stop=(k == KC - 1))
                            last.then_inc(done, 1)

                def turn_h(el):
                    pe.wait_ge(hq_ready, el.n + 1)
                    wait_for(pe, th_out, el.n * TH)
                    for m in range(TH):
                        for k in range(8):
                            c = (8 * m + k) * P
                            last = nc.tensor.transpose(th_bank[m][:, k * P:(k + 1) * P], hq[:, el.par, c:c + P], ident[:])
                        last.then_inc(th_done, 1)

                def down(el):
                    wait_for(pe, out_done, el.n)
                    for m in range(TH):
                        pe.wait_ge(th_out, el.n * TH + m + 1)
                        for k in range(8 * m, 8 * m + 8):
                            last = nc.tensor.matmul(d_bank[:], hqT[:, el.par, k], wd[:, k], start=(k == 0), stop=(k == IK - 1))
                    last.then_inc(d_done, 1)

                turn_x(first[0])
                gate_up(first[0], range(NC))
                turn_x(first[1])

                def iteration(el):
                    if el.has(1):
                        gate_up(el.plus(1), range(NC - 1))
                    turn_h(el)
                    if el.has(1):
                        gate_up(el.plus(1), range(NC - 1, NC))
                    if el.has(2):
                        turn_x(el.plus(2))
                    down(el)

                run_elements(pe, tiles, iteration, ahead=4)

        clear_semaphores(nc, sems)


def routed_ffn_phase(nc, tag, x_in, out, w_gate, w1, w2, w3, sw1, sw2, sw3, expert_bias, tiles=TOK // P):
    EXPERTS, HID = w1.shape[0], w1.shape[2]
    GROUPS = EXPERTS // 2
    PAIRS = EXPERTS * EXPERTS
    HK = HID // P
    NE = tiles * EXPERTS

    with ExitStack() as ctx:
        sems = []

        def sb(name, shape, dt=F32):
            return ctx.enter_context(nc.sbuf_tensor(f"{tag}_{name}", shape, dt))

        def sem(name):
            sems.append(ctx.enter_context(nc.semaphore(f"{tag}_{name}")))
            return sems[-1]

        ew13 = sb("ew13", [P, EXPERTS, KC, 2 * HID])
        ew2 = sb("ew2", [P, EXPERTS, HK, DIM])
        ident = sb("ident", [P, P])
        neg_half = sb("neg_half", [P, 1])
        first_out = sb("first_out", [EXPERTS, DIM])
        xT_first = sb("xT_first", [P, KC, 2 * PAIRS])
        table = sb("table", [PAIRS, 2, 2 * HID], F32R)
        pair = sb("pair", [P, tiles, 2])
        weight = sb("weight", [P, tiles, 2])
        pair_no = sb("pair_no", [P, PAIRS])
        experts_loaded = sem("experts_loaded")
        ident_ready = sem("ident_ready")
        first_ready = sem("first_ready")

        with ExitStack() as shared:
            def ssb(name, shape, dt=F32):
                return shared.enter_context(nc.sbuf_tensor(f"{tag}_{name}", shape, dt))

            def bank(name):
                return shared.enter_context(nc.psum_tensor(f"{tag}_{name}", [P, 512], F32))

            lg_bank = bank("lg")
            with ExitStack() as stage1:
                def tsb(name, shape, dt=F32):
                    return stage1.enter_context(nc.sbuf_tensor(f"{tag}_{name}", shape, dt))

                def tbank(name):
                    return stage1.enter_context(nc.psum_tensor(f"{tag}_{name}", [P, 512], F32))

                raw = ew2[:].rearrange("p e k n -> p (e k) n")[:, 0:3 * KC].rearrange("p (w k) n -> p w k n", k=KC)
                raw_gate = tsb("raw_gate", [P, DIM])
                sw = [tsb(n, [P, 2, KC, DIM], F32R) for n in ("s1", "s3", "s2")]
                gateT = tsb("gateT", [P, KC, EXPERTS])
                xbuf = tsb("xbuf", [P, 2, DIM])
                resb = tsb("resb", [P, 2, DIM])
                stats = tsb("stats", [P, 2, 6])
                mv = tsb("mv", [P, 2, 2])
                ln = tsb("ln", [P, 2, 4])
                xn = tsb("xn", [P, 2, DIM])
                xnT = tsb("xnT", [P, 2, 2, DIM], F32R)
                act_gate = tsb("act_gate", [P, 2, DIM])
                hid = tsb("hid", [P, 2, DIM])
                hidT = tsb("hidT", [P, 2, 2, DIM], F32R)
                tx_bank, th_bank, g_bank, u_bank, z_bank = [tbank(n) for n in ("tx", "th", "g", "u", "z")]
                w_bank = [tx_bank, th_bank, g_bank, u_bank]

                (ident_zero, first_zero, gate_loaded, gate_ready, w_turned, w_hi, w_lo, x_loaded0, x_loaded1, r_loaded0,
                 r_loaded1, stored0, stored1, bn_done, stats_ready, ln_step, xn_ready, tx_done, tx_hi,
                 tx_lo, lg_done, g_done, u_done, silu_done, h_done, th_done, th_hi, th_lo, z_done, out_done) = [
                     sem(n) for n in (
                         "ident_zero first_zero gate_loaded gate_ready w_turned w_hi w_lo x_loaded0 x_loaded1 r_loaded0 "
                         "r_loaded1 stored0 stored1 bn_done stats_ready ln_step xn_ready tx_done tx_hi "
                         "tx_lo lg_done g_done u_done silu_done h_done th_done th_hi th_lo z_done out_done").split()]
                x_loaded, r_loaded, stored = (x_loaded0, x_loaded1), (r_loaded0, r_loaded1), (stored0, stored1)
                w_loaded = [sem(f"sw_loaded{n}") for n in range(3)]
                first = [Element(0, n, tiles) for n in range(4)]
                turns = [(n, k) for n in range(3) for k in range(KC)]

                def rows(t, el):
                    return t[bass.ts(el.n, P), :]

                with nc.Block() as block:
                    @block.sync
                    def _(sp):
                        def load_x(el):
                            src = rows(x_in, el)
                            wait_apart(sp, xn_ready, el.n - 1)
                            sp.dma_start(xbuf[:, el.par], src).then_inc(x_loaded[el.par], 16)

                        for n, w in enumerate((sw1, sw3, sw2)):
                            sp.dma_start(raw[:, n], w.rearrange("(t p) c -> p t c", p=P)).then_inc(w_loaded[n], 16)
                            if n == 0:
                                sp.dma_start(raw_gate[0:EXPERTS, :], w_gate).then_inc(gate_loaded, 16)
                                for el in first[:2]:
                                    load_x(el)
                        sp.dma_start(resb[:, 0], rows(x_in, first[0])).then_inc(r_loaded[0], 16)
                        for el in first[2:]:
                            load_x(el)
                        for e in range(EXPERTS):
                            for n, w in enumerate((w1, w3)):
                                sp.dma_start(ew13[:, e, :, n * HID:(n + 1) * HID],
                                             w[e].rearrange("(k p) h -> p k h", p=P)).then_inc(experts_loaded, 16)

                        def iteration(el):
                            if el.has(4):
                                load_x(el.plus(4))
                            if el.has(1):
                                nxt, prev = el.plus(1), el.plus(-1)
                                src = rows(x_in, nxt)
                                wait_apart(sp, stored[prev.par], prev.dma())
                                if isinstance(el.n, int) and el.n == 1:
                                    sp.wait_ge(first_ready, 2)
                                sp.dma_start(resb[:, nxt.par], src).then_inc(r_loaded[nxt.par], 16)
                            dst = rows(out, el)
                            wait_apart(sp, out_done, el.n + 1)
                            sp.dma_start(dst, resb[:, el.par]).then_inc(stored[el.par], 16)

                        run_elements(sp, tiles, iteration, ahead=4)
                        for par in range(2):
                            sp.wait_ge(stored[par], tiles // 2 * 16)

                    @block.gpsimd
                    def _(pool):
                        nc.gpsimd.memset(ident[:], 0.0).then_inc(ident_zero, 1)
                        nc.gpsimd.memset(neg_half[:], -0.5).then_inc(ident_ready, 1)
                        nc.gpsimd.memset(xT_first[:], 0.0).then_inc(first_zero, 1)
                        pool.wait_ge(ident_zero, 1)
                        nc.gpsimd.affine_select(out=ident[:], in_=ident[:], compare_op=ALU.not_equal, fill=1.0,
                                                base=0, pattern=[[-1, P]], channel_multiplier=1).then_inc(ident_ready, 1)
                        pool.wait_ge(ident_ready, 2)

                        def normalise(el):
                            def chained(k, ins):
                                ins.then_inc(ln_step, 1)
                                wait_apart(pool, ln_step, el.n * 4 + k)

                            wait_apart(pool, stats_ready, el.n + 1)
                            l, m = ln[:, el.par], mv[:, el.par]
                            chained(1, nc.gpsimd.tensor_scalar(l[:, 0:1], m[:, 1:2], 1.0, EPS, ALU.mult, ALU.add))
                            chained(2, nc.gpsimd.tensor_tensor(l[:, 1:2], l[:, 0:1], neg_half[:], ALU.pow))
                            chained(3, nc.gpsimd.tensor_tensor(l[:, 2:3], m[:, 0:1], l[:, 1:2], ALU.mult))
                            chained(4, nc.gpsimd.tensor_scalar(l[:, 3:4], l[:, 2:3], -1.0, 0.0, ALU.mult, ALU.add))
                            wait_apart(pool, tx_done, el.n - 1)
                            nc.gpsimd.tensor_scalar(xn[:, el.par], xbuf[:, el.par], l[:, 1:2], l[:, 3:4],
                                                    ALU.mult, ALU.add).then_inc(xn_ready, 1)

                        for el in first[:3]:
                            normalise(el)

                        def iteration(el):
                            if el.has(3):
                                normalise(el.plus(3))

                        run_elements(pool, tiles, iteration, ahead=4)

                    @block.scalar
                    def _(act):
                        for i, (n, k) in enumerate(turns):
                            act.wait_ge(w_turned, i + 1)
                            nc.scalar.activation(sw[n][:, HI, k], w_bank[i % 4][:], ACT.Copy) \
                                .then_inc(w_hi, 1)
                        for e in range(EXPERTS):
                            act.dma_start(ew2[:, e], w2[e].rearrange("(k p) d -> p k d", p=P)).then_inc(experts_loaded, 16)

                        def hi_x(el):
                            act.wait_ge(tx_done, el.n + 1)
                            nc.scalar.activation(xnT[:, el.par, HI], tx_bank[:], ACT.Copy).then_inc(tx_hi, 1)

                        def silu(el):
                            act.wait_ge(g_done, el.n + 1)
                            wait_for(act, h_done, el.n - 1)
                            nc.scalar.activation(act_gate[:, el.par], g_bank[:], ACT.Silu).then_inc(silu_done, 1)

                        def hi_h(el):
                            act.wait_ge(th_done, el.n + 1)
                            nc.scalar.activation(hidT[:, el.par, HI], th_bank[:], ACT.Copy).then_inc(th_hi, 1)

                        hi_x(first[0])
                        silu(first[0])
                        hi_x(first[1])

                        def iteration(el):
                            if el.has(1):
                                silu(el.plus(1))
                            hi_h(el)
                            if el.has(2):
                                hi_x(el.plus(2))

                        run_elements(act, tiles, iteration, ahead=4)

                    @block.vector
                    def _(dve):
                        dve.wait_ge(gate_ready, 1)
                        nc.vector.tensor_copy(gateT[:].rearrange("p k e -> p (k e)"), z_bank[:, 0:KC * EXPERTS]) \
                            .then_inc(gate_ready, 1)
                        for i, (n, k) in enumerate(turns):
                            dve.wait_ge(w_hi, i + 1)
                            nc.vector.tensor_tensor(sw[n][:, LO, k], w_bank[i % 4][:],
                                                    sw[n][:, HI, k].bitcast(F32), ALU.subtract).then_inc(w_lo, 1)

                        def row_stats(el):
                            dve.wait_ge(x_loaded[el.par], el.dma())
                            wait_for(dve, ln_step, (el.n - 1) * 4)
                            nc.vector.bn_stats(stats[:, el.par], xbuf[:, el.par]).then_inc(bn_done, 1)
                            wait_apart(dve, bn_done, el.n + 1)
                            nc.vector.bn_aggr(mv[:, el.par], stats[:, el.par]).then_inc(stats_ready, 1)

                        def lo_x(el):
                            dve.wait_ge(tx_hi, el.n + 1)
                            nc.vector.tensor_tensor(xnT[:, el.par, LO], tx_bank[:], xnT[:, el.par, HI].bitcast(F32),
                                                    ALU.subtract).then_inc(tx_lo, 1)

                        def lo_h(el):
                            dve.wait_ge(th_hi, el.n + 1)
                            nc.vector.tensor_tensor(hidT[:, el.par, LO], th_bank[:], hidT[:, el.par, HI].bitcast(F32),
                                                    ALU.subtract).then_inc(th_lo, 1)

                        def hidden(el):
                            dve.wait_ge(silu_done, el.n + 1)
                            dve.wait_ge(u_done, el.n + 1)
                            wait_for(dve, th_done, el.n - 1)
                            nc.vector.tensor_tensor(hid[:, el.par], u_bank[:], act_gate[:, el.par], ALU.mult) \
                                .then_inc(h_done, 1)

                        def rows_out(el):
                            dve.wait_ge(r_loaded[el.par], el.dma())
                            dve.wait_ge(z_done, el.n + 1)
                            nc.vector.tensor_tensor(resb[:, el.par], z_bank[:], resb[:, el.par], ALU.add) \
                                .then_inc(out_done, 1)

                        for el in first[:3]:
                            row_stats(el)
                        dve.wait_ge(first_zero, 1)
                        dve.wait_ge(tx_done, 1)
                        dve.wait_ge(tx_hi, 1)
                        nc.vector.tensor_copy(xT_first[:, :, PAIRS:PAIRS + EXPERTS],
                                              tx_bank[:].rearrange("p (k n) -> p k n", k=KC)[:, :, 0:EXPERTS]) \
                            .then_inc(first_ready, 1)
                        lo_x(first[0])
                        hidden(first[0])
                        lo_x(first[1])

                        def keep_first():
                            dve.wait_ge(out_done, 1)
                            nc.vector.tensor_copy(first_out[:], resb[0:EXPERTS, 0]).then_inc(first_ready, 1)

                        def iteration(el):
                            lo_h(el)
                            if el.has(1):
                                hidden(el.plus(1))
                            if el.has(2):
                                lo_x(el.plus(2))
                            if el.has(3):
                                row_stats(el.plus(3))
                            rows_out(el)
                            if isinstance(el.n, int) and el.n == 0:
                                keep_first()

                        run_elements(dve, tiles, iteration, ahead=4)

                    @block.tensor
                    def _(pe):
                        pe.wait_ge(ident_ready, 2)
                        pe.wait_ge(gate_loaded, 16)
                        for k in range(KC):
                            last = nc.tensor.transpose(z_bank[:, k * EXPERTS:(k + 1) * EXPERTS],
                                                       raw_gate[0:EXPERTS, k * P:(k + 1) * P],
                                                       ident[0:EXPERTS, 0:EXPERTS])
                        last.then_inc(gate_ready, 1)
                        for i, (n, k) in enumerate(turns):
                            if k == 0:
                                pe.wait_ge(w_loaded[n], 16)
                            if i >= 4:
                                pe.wait_ge(w_lo, i - 3)
                            for o in range(KC):
                                last = nc.tensor.transpose(w_bank[i % 4][:, o * P:(o + 1) * P],
                                                           raw[:, n, o, k * P:(k + 1) * P], ident[:])
                            last.then_inc(w_turned, 1)
                        pe.wait_ge(gate_ready, 2)
                        pe.wait_ge(w_lo, len(turns))

                        def turn(bank, src, done):
                            for k in range(KC):
                                last = nc.tensor.transpose(bank[:, k * P:(k + 1) * P], src[:, k * P:(k + 1) * P], ident[:])
                            last.then_inc(done, 1)

                        def turn_x(el):
                            pe.wait_ge(xn_ready, el.n + 1)
                            wait_for(pe, tx_lo, el.n)
                            turn(tx_bank, xn[:, el.par], tx_done)

                        def turn_h(el):
                            pe.wait_ge(h_done, el.n + 1)
                            wait_for(pe, th_lo, el.n)
                            turn(th_bank, hid[:, el.par], th_done)

                        def product(bank, srcT, w, done):
                            for k in range(KC):
                                for a, b in TERMS:
                                    last = nc.tensor.matmul(bank[:], srcT[:, a, k * P:(k + 1) * P], w[:, b, k],
                                                            start=(k == 0 and (a, b) == TERMS[0]),
                                                            stop=(k == KC - 1 and (a, b) == TERMS[-1]))
                            last.then_inc(done, 1)

                        def logits(el):
                            pe.wait_ge(tx_lo, el.n + 1)
                            for k in range(KC):
                                for a in (HI, LO):
                                    last = nc.tensor.matmul(lg_bank[:, bass.ds(el.n * EXPERTS, EXPERTS)],
                                                            xnT[:, el.par, a, k * P:(k + 1) * P].bitcast(F32),
                                                            gateT[:, k], start=(k == 0 and a == HI),
                                                            stop=(k == KC - 1 and a == LO))
                            last.then_inc(lg_done, 1)

                        def gate(el):
                            wait_for(pe, silu_done, el.n)
                            product(g_bank, xnT[:, el.par], sw[0], g_done)

                        def up(el):
                            wait_for(pe, h_done, el.n)
                            product(u_bank, xnT[:, el.par], sw[1], u_done)

                        def down(el):
                            pe.wait_ge(th_lo, el.n + 1)
                            wait_for(pe, out_done, el.n)
                            product(z_bank, hidT[:, el.par], sw[2], z_done)

                        turn_x(first[0])
                        logits(first[0])
                        gate(first[0])
                        up(first[0])
                        turn_x(first[1])

                        def iteration(el):
                            if el.has(1):
                                logits(el.plus(1))
                                gate(el.plus(1))
                            turn_h(el)
                            if el.has(1):
                                up(el.plus(1))
                            if el.has(2):
                                turn_x(el.plus(2))
                            down(el)

                        run_elements(pe, tiles, iteration, ahead=4)

            with ExitStack() as stage2:
                def rsb(name, shape, dt=F32):
                    return stage2.enter_context(nc.sbuf_tensor(f"{tag}_{name}", shape, dt))

                te = [P, tiles, EXPERTS]
                tc = [P, tiles, 2, EXPERTS]
                top = rsb("top", [P, tiles])
                total = rsb("total", [P, tiles])
                inverse = rsb("inverse", [P, tiles])
                expo = rsb("expo", te)
                prob = rsb("prob", te)
                score = rsb("score", te)
                gscore = rsb("gscore", [P, tiles, GROUPS])
                grank = rsb("grank", [P, tiles, GROUPS])
                gkeep = rsb("gkeep", [P, tiles, GROUPS])
                gdrop = rsb("gdrop", [P, tiles, GROUPS])
                masked = rsb("masked", te)
                above = rsb("above", [P, tiles, PAIRS])
                ties = rsb("ties", [P, tiles, PAIRS])
                lower_g = rsb("lower_g", [P, GROUPS, GROUPS])
                lower_e = rsb("lower_e", [P, EXPERTS, EXPERTS])
                rank = rsb("rank", te)
                chosen = rsb("chosen", te)
                counts = rsb("counts", [P, EXPERTS])
                before = rsb("before", [P, EXPERTS, EXPERTS])
                run_start = rsb("run_start", [P, EXPERTS])
                run_end = rsb("run_end", [P, EXPERTS])
                past = rsb("past", tc)
                run = rsb("run", [P, tiles, 2])
                row = rsb("row", [P, tiles, 2])
                choice = rsb("choice", tc)
                marked = rsb("marked", tc)
                picked = rsb("picked", tc)
                position = rsb("position", [P, tiles, 2])
                choice_no = rsb("choice_no", [P, 2])
                expert_no = rsb("expert_no", [P, EXPERTS])
                ones = rsb("ones", [P, P])
                bias_row = rsb("bias_row", [P, EXPERTS])
                count_bank = stage2.enter_context(nc.psum_tensor(f"{tag}_count_bank", [P, 512], F32))
                table_bank = stage2.enter_context(nc.psum_tensor(f"{tag}_table_bank", [PAIRS, 512], F32))

                (bias_loaded, shifted, exp_ready, route_step, consts_step, consts_ready, counts_ready, counted,
                 table_done, table_hi, table_lo) = [
                     sem(n) for n in (
                         "bias_loaded shifted exp_ready route_step consts_step route_consts counts_ready counted "
                         "table_done table_hi table_lo").split()]

                with nc.Block() as block:
                    @block.sync
                    def _(sp):
                        sp.dma_start(bias_row[:], expert_bias.rearrange("(a n) -> a n", a=1).broadcast_to([P, EXPERTS])) \
                          .then_inc(bias_loaded, 16)

                    @block.gpsimd
                    def _(pool):
                        exact = dict(allow_small_or_imprecise_dtypes=True)
                        nc.gpsimd.memset(lower_g[:], 1.0).then_inc(consts_step, 1)
                        nc.gpsimd.memset(lower_e[:], 1.0).then_inc(consts_step, 1)
                        pool.wait_ge(consts_step, 2)
                        for t, n in ((lower_g, GROUPS), (lower_e, EXPERTS)):
                            nc.gpsimd.affine_select(out=t[:], in_=t[:], compare_op=ALU.is_gt, fill=0.0, base=0,
                                                    pattern=[[1, n], [-1, n]], channel_multiplier=0) \
                                .then_inc(consts_ready, 1)
                        nc.gpsimd.memset(ones[:], 1.0).then_inc(consts_ready, 1)
                        for t, pattern, each in ((position, [[2 * P, tiles], [1, 2]], 2), (choice_no, [[1, 2]], 0),
                                                 (expert_no, [[1, EXPERTS]], 0), (pair_no, [[1, PAIRS]], 0)):
                            nc.gpsimd.iota(t[:], pattern=pattern, base=0, channel_multiplier=each, **exact) \
                                .then_inc(consts_ready, 1)

                    @block.scalar
                    def _(act):
                        act.wait_ge(shifted, 1)
                        nc.scalar.activation(expo[:], expo[:], ACT.Exp).then_inc(exp_ready, 1)
                        act.wait_ge(table_done, 1)
                        nc.scalar.activation(table[:, HI], table_bank[:], ACT.Copy).then_inc(table_hi, 1)

                    @block.vector
                    def _(dve):
                        count = [0]

                        def step(ins):
                            count[0] += 1
                            ins.then_inc(route_step, 1)
                            dve.wait_ge(route_step, count[0])

                        V = nc.vector

                        def over_experts(ap):
                            return ap.unsqueeze(2).broadcast_to([P, ap.shape[1], EXPERTS])

                        def ranks(dst, src, lower, n):
                            other = src.unsqueeze(2).broadcast_to([P, tiles, n, n])
                            own = src.unsqueeze(3).broadcast_to([P, tiles, n, n])
                            ab = above[:, :, 0:n * n].rearrange("p t (a b) -> p t a b", b=n)
                            ti = ties[:, :, 0:n * n].rearrange("p t (a b) -> p t a b", b=n)
                            V.tensor_tensor(ab, other, own, ALU.is_gt)
                            step(V.tensor_tensor(ti, other, own, ALU.is_equal))
                            step(V.tensor_tensor(ti, ti, lower.unsqueeze(1).broadcast_to([P, tiles, n, n]), ALU.mult))
                            step(V.tensor_tensor(ab, ab, ti, ALU.add))
                            step(V.reduce_sum(dst, ab, AX.X))

                        def by_choice(ap):
                            return ap.unsqueeze(2).broadcast_to(tc)

                        lg = lg_bank[:, 0:NE].rearrange("p (t e) -> p t e", e=EXPERTS)
                        step(V.reduce_max(top[:], lg, AX.X))
                        V.tensor_tensor(expo[:], lg, over_experts(top[:]), ALU.subtract).then_inc(shifted, 1)
                        dve.wait_ge(exp_ready, 1)
                        step(V.reduce_sum(total[:], expo[:], AX.X))
                        step(V.reciprocal(inverse[:], total[:]))
                        step(V.tensor_tensor(prob[:], expo[:], over_experts(inverse[:]), ALU.mult))
                        dve.wait_ge(bias_loaded, 16)
                        step(V.tensor_tensor(score[:], prob[:], bias_row[:].unsqueeze(1).broadcast_to(te), ALU.add))
                        halves = score[:].rearrange("p t (g a) -> p t g a", a=2)
                        step(V.tensor_tensor(gscore[:], halves[:, :, :, 0], halves[:, :, :, 1], ALU.add))
                        dve.wait_ge(consts_ready, 7)
                        ranks(grank[:], gscore[:], lower_g[:], GROUPS)
                        step(V.tensor_scalar(gkeep[:], grank[:], 1.5, None, ALU.is_lt))
                        step(V.tensor_scalar(gdrop[:], gkeep[:], -1.0, BIG, ALU.add, ALU.mult))
                        mp = masked[:].rearrange("p t (g a) -> p t g a", a=2)
                        for a in range(2):
                            step(V.tensor_tensor(mp[:, :, :, a], halves[:, :, :, a], gkeep[:], ALU.mult))
                            step(V.tensor_tensor(mp[:, :, :, a], mp[:, :, :, a], gdrop[:], ALU.add))
                        ranks(rank[:], masked[:], lower_e[:], EXPERTS)
                        step(V.tensor_scalar(chosen[:], rank[:], 1.5, None, ALU.is_lt))
                        V.reduce_sum(counts[:], chosen[:].rearrange("p t e -> p e t"), AX.X).then_inc(counts_ready, 1)
                        step(V.tensor_tensor(choice[:], by_choice(rank[:]), choice_no[:].unsqueeze(1).unsqueeze(3)
                                             .broadcast_to(tc), ALU.is_equal))
                        V.tensor_tensor(marked[:], choice[:], expert_no[:].unsqueeze(1).unsqueeze(1).broadcast_to(tc),
                                        ALU.mult)
                        step(V.tensor_tensor(picked[:], choice[:], by_choice(prob[:]), ALU.mult))
                        V.reduce_sum(row[:], marked[:], AX.X)
                        step(V.reduce_sum(weight[:], picked[:], AX.X))
                        dve.wait_ge(counted, 1)
                        step(V.tensor_tensor(before[:], count_bank[:, 0:EXPERTS].unsqueeze(1)
                                             .broadcast_to([P, EXPERTS, EXPERTS]), lower_e[:], ALU.mult))
                        step(V.reduce_sum(run_start[:], before[:], AX.X))
                        step(V.tensor_tensor(run_end[:], run_start[:], count_bank[:, 0:EXPERTS], ALU.add))
                        step(V.tensor_tensor(past[:], position[:].unsqueeze(3).broadcast_to(tc),
                                             run_end[:].unsqueeze(1).unsqueeze(1).broadcast_to(tc), ALU.is_ge))
                        step(V.reduce_sum(run[:], past[:], AX.X))
                        step(V.scalar_tensor_tensor(pair[:], run[:], float(EXPERTS), row[:], ALU.mult, ALU.add))
                        dve.wait_ge(table_hi, 1)
                        V.tensor_tensor(table[:, LO], table_bank[:], table[:, HI].bitcast(F32), ALU.subtract) \
                            .then_inc(table_lo, 1)
                        dve.wait_ge(table_lo, 1)

                    @block.tensor
                    def _(pe):
                        pe.wait_ge(first_ready, 2)
                        pe.wait_ge(experts_loaded, 3 * EXPERTS * 16)
                        for e in range(EXPERTS):
                            window = slice(PAIRS - e * EXPERTS, 2 * PAIRS - e * EXPERTS)
                            for k in range(KC):
                                last = nc.tensor.matmul(table_bank[:], xT_first[:, k, window], ew13[:, e, k],
                                                        start=(e == 0 and k == 0), stop=(e == EXPERTS - 1 and k == KC - 1))
                        last.then_inc(table_done, 1)
                        pe.wait_ge(counts_ready, 1)
                        pe.wait_ge(consts_ready, 7)
                        nc.tensor.matmul(count_bank[:, 0:EXPERTS], ones[:], counts[:], start=True, stop=True) \
                            .then_inc(counted, 1)

        with ExitStack() as stage3:
            def esb(name, shape, dt=F32):
                return stage3.enter_context(nc.sbuf_tensor(f"{tag}_{name}", shape, dt))

            def ebank(name, rows=P):
                return stage3.enter_context(nc.psum_tensor(f"{tag}_{name}", [rows, 512], F32))

            onehot = esb("onehot", [P, 4, 2, PAIRS])
            wcol = esb("wcol", [P, 4, 2])
            onehotT = esb("onehotT", [PAIRS, 4, 2 * P], F32R)
            act_a = esb("act_a", [P, 4, 2, HID])
            hrow = esb("hrow", [P, 4, 2, HID])
            hsum = esb("hsum", [PAIRS, HID])
            hsumT = esb("hsumT", [P, HK, PAIRS])
            ohT_bank = [ebank(f"ohT{i}", PAIRS) for i in range(2)]
            ab_bank = [[ebank(f"ab{i}{c}") for c in range(2)] for i in range(2)]
            sum_bank = ebank("sum", PAIRS)
            end_bank = ebank("end")
            (oh_ready, ohT_done, ohT_out, ab_done, asilu_done, hrow_done, sum_done, hsum_ready, hsumT_done,
             hsumT_ready, y_done, first_done, first_stored) = [sem(n) for n in (
                 "oh_ready ohT_done ohT_out ab_done asilu_done hrow_done sum_done hsum_ready hsumT_done "
                 "hsumT_ready y_done first_done first_stored").split()]
            first = [Element(0, n, tiles, 4) for n in range(3)]

            with nc.Block() as block:
                @block.sync
                def _(sp):
                    sp.wait_ge(first_done, 1)
                    sp.dma_start(out[0:EXPERTS, :], first_out[:]).then_inc(first_stored, 16)
                    sp.wait_ge(first_stored, 16)

                @block.scalar
                def _(act):
                    def ohT(el):
                        act.wait_ge(ohT_done, el.n + 1)
                        wait_for(act, ab_done, (el.n - 3) * 2)
                        nc.scalar.activation(onehotT[:, el.par], ohT_bank[el.par % 2][:, 0:2 * P], ACT.Copy).then_inc(ohT_out, 1)

                    def silu(el):
                        wait_for(act, hrow_done, (el.n - 3) * 2)
                        for c in range(2):
                            act.wait_ge(ab_done, el.n * 2 + c + 1)
                            nc.scalar.activation(act_a[:, el.par, c], ab_bank[el.par % 2][c][:, 0:HID], ACT.Silu,
                                                 scale=wcol[:, el.par, c:c + 1]).then_inc(asilu_done, 1)

                    for el in first:
                        ohT(el)
                    silu(first[0])

                    def iteration(el):
                        if el.has(1):
                            silu(el.plus(1))
                        if el.has(3):
                            ohT(el.plus(3))

                    run_elements(act, tiles, iteration, ahead=4, group=4)
                    act.wait_ge(hsumT_done, 1)
                    nc.scalar.activation(hsumT[:].rearrange("p k n -> p (k n)"), end_bank[:, 0:HK * PAIRS], ACT.Copy) \
                        .then_inc(hsumT_ready, 1)

                @block.vector
                def _(dve):
                    def one_hot(el):
                        wait_for(dve, sum_done, el.n - 3)
                        nc.vector.tensor_copy(wcol[:, el.par], weight[:, bass.ds(el.n, 1)].rearrange("p a c -> p (a c)"))
                        nc.vector.tensor_tensor(onehot[:, el.par], pair_no[:].unsqueeze(1).broadcast_to([P, 2, PAIRS]),
                                                pair[:, bass.ds(el.n, 1)].rearrange("p a c -> p (a c)").unsqueeze(2)
                                                .broadcast_to([P, 2, PAIRS]), ALU.is_equal).then_inc(oh_ready, 1)

                    def hidden(el):
                        dve.wait_ge(oh_ready, el.n + 1)
                        wait_for(dve, sum_done, el.n - 3)
                        for c in range(2):
                            dve.wait_ge(asilu_done, el.n * 2 + c + 1)
                            nc.vector.scalar_tensor_tensor(hrow[:, el.par, c], ab_bank[el.par % 2][c][:, HID:2 * HID],
                                                           wcol[:, el.par, c:c + 1], act_a[:, el.par, c],
                                                           ALU.mult, ALU.mult).then_inc(hrow_done, 1)

                    for el in first:
                        one_hot(el)
                    hidden(first[0])

                    def iteration(el):
                        if el.has(3):
                            one_hot(el.plus(3))
                        if el.has(1):
                            hidden(el.plus(1))

                    run_elements(dve, tiles, iteration, ahead=4, group=4)
                    dve.wait_ge(sum_done, tiles)
                    nc.vector.tensor_copy(hsum[:], sum_bank[:, 0:HID]).then_inc(hsum_ready, 1)
                    dve.wait_ge(y_done, 1)
                    nc.vector.tensor_tensor(first_out[:], ab_bank[0][0][0:EXPERTS, :], first_out[:], ALU.add) \
                        .then_inc(first_done, 1)

                @block.tensor
                def _(pe):
                    def turn(el):
                        wait_apart(pe, oh_ready, el.n + 1)
                        wait_apart(pe, ohT_out, el.n - 1)
                        for c in range(2):
                            last = nc.tensor.transpose(ohT_bank[el.par % 2][:, c * P:(c + 1) * P], onehot[:, el.par, c], ident[:])
                        last.then_inc(ohT_done, 1)

                    def pick(el):
                        pe.wait_ge(ohT_out, el.n + 1)
                        wait_for(pe, hrow_done, (el.n - 1) * 2)
                        for c in range(2):
                            for part in (HI, LO):
                                last = nc.tensor.matmul(ab_bank[el.par % 2][c][:], onehotT[:, el.par, c * P:(c + 1) * P],
                                                        table[:, part], start=(part == HI), stop=(part == LO))
                            last.then_inc(ab_done, 1)

                    def add_up(el):
                        for c in range(2):
                            pe.wait_ge(hrow_done, el.n * 2 + c + 1)
                            last = nc.tensor.matmul(sum_bank[:, 0:HID], onehot[:, el.par, c], hrow[:, el.par, c],
                                                    start=(c == 0 and isinstance(el.n, int) and el.n == 0),
                                                    stop=(c == 1 and isinstance(el.n, int) and el.n == tiles - 1),
                                                    skip_group_check=True)
                        last.then_inc(sum_done, 1)

                    for el in first:
                        turn(el)
                    pick(first[0])

                    def iteration(el):
                        if el.has(1):
                            pick(el.plus(1))
                        if el.has(3):
                            turn(el.plus(3))
                        add_up(el)

                    run_elements(pe, tiles, iteration, ahead=4, group=4)
                    pe.wait_ge(hsum_ready, 1)
                    for k in range(HK):
                        last = nc.tensor.transpose(end_bank[:, k * PAIRS:(k + 1) * PAIRS], hsum[:, k * P:(k + 1) * P],
                                                   ident[0:PAIRS, 0:PAIRS])
                    last.then_inc(hsumT_done, 1)
                    pe.wait_ge(hsumT_ready, 1)
                    for e in range(EXPERTS):
                        for k in range(HK):
                            last = nc.tensor.matmul(ab_bank[0][0][0:EXPERTS, :], hsumT[:, k, e * EXPERTS:(e + 1) * EXPERTS],
                                                    ew2[:, e, k], start=(e == 0 and k == 0),
                                                    stop=(e == EXPERTS - 1 and k == HK - 1))
                    last.then_inc(y_done, 1)

        clear_semaphores(nc, sems)


def decoder_kernel(nc, x, ctx_1024, mask_if, mask_bk, a_wv, a_bv, a_wk, a_bk, a_wq, a_bq, a_wo, a_bo, f_gate, f_up, f_down,
                   c_gain, c_bias, c_wq, c_wkv, c_wo, m_gate, m_w1, m_w2, m_w3, m_sw1, m_sw2, m_sw3, m_bias, out):
    def rows(t):
        return t.rearrange("b s d -> (b s) d")

    def internal(name, shape):
        return nc.dram_tensor(name, shape, F32, kind="Internal").ap()

    x_rows, ctx_rows, out_rows = rows(x), rows(ctx_1024), rows(out)
    x1, x2, x3 = [internal(n, (TOK, DIM)) for n in ("x1", "x2", "x3")]

    attention_phase(nc, "a", 16, x_rows, ctx_rows, mask_if.rearrange("b o q k -> (b o q) k"), -1e20, x1,
                    (a_wq, a_wk, a_wv, a_wo), a_bq, a_bk, a_bv, a_bo, None, None)
    ternary_ffn_phase(nc, "b", x1, x2, f_gate, f_up, f_down)
    attention_phase(nc, "c", 8, x2, ctx_rows, mask_bk, -1e30, x3, (c_wq, c_wkv[:, 0:DIM], c_wkv[:, DIM:2 * DIM], c_wo),
                    None, None, None, None, c_gain, c_bias)
    routed_ffn_phase(nc, "m", x3, out_rows, m_gate, m_w1, m_w2, m_w3, m_sw1, m_sw2, m_sw3, m_bias)


INPUTS = ["x", "ctx_1024", "mask_Bx1x1xS2_if1", "mask_BxS2_bk0", "L0_xattn_Wv", "L0_xattn_bv", "L0_xattn_Wk",
          "L0_xattn_bk", "L0_xattn_Wq", "L0_xattn_bq", "L0_xattn_Wo", "L0_xattn_bo", "L0_ffn_w_gate", "L0_ffn_w_up",
          "L0_ffn_w_down", "L1_xattn_ln_g", "L1_xattn_ln_b", "L1_xattn_Wq", "L1_xattn_Wkv", "L1_xattn_Wo",
          "L1_ffn_w_gate", "L1_ffn_w1", "L1_ffn_w2", "L1_ffn_w3", "L1_ffn_sw1", "L1_ffn_sw2", "L1_ffn_sw3",
          "L1_ffn_expert_bias"]


def kernel(**inputs):
    import numpy as np
    import concourse.bacc as bacc
    from concourse.bass_utils import run_bass_kernel_spmd

    nc = bacc.Bacc("TRN2", target_bir_lowering=False, num_devices=1)
    arrays, args = {}, []
    for name in INPUTS:
        a = np.ascontiguousarray(inputs[name])
        arrays[f"in_{name}_dram"] = a
        args.append(nc.dram_tensor(f"in_{name}_dram", a.shape, mybir.dt.from_np(a.dtype), kind="ExternalInput").ap())
    args.append(nc.dram_tensor("out_0_dram", (BATCH, SEQ, DIM), F32, kind="ExternalOutput").ap())
    decoder_kernel(nc, *args)
    return run_bass_kernel_spmd(nc, [arrays], core_ids=[0]).results[0]["out_0_dram"]
```

```python
import concourse.bass as bass
from concourse import mybir
from contextlib import ExitStack

F32 = mybir.dt.float32
F32R = mybir.dt.float32r
BF16 = mybir.dt.bfloat16
U32 = mybir.dt.uint32
ALU = mybir.AluOpType
ACT = mybir.ActivationFunctionType
AX = mybir.AxisListType

P = 128
BATCH, SEQ, DIM = 16, 256, 512
TOK = BATCH * SEQ
KC = DIM // P
QT = SEQ // P
EPS = 1e-5
BIG = 3.0e38

HI, LO = 0, 1
TERMS = ((HI, HI), (LO, HI), (HI, LO))


def wait_for(engine, semaphore, count):
    if not isinstance(count, int) or count > 0:
        engine.wait_ge(semaphore, count)


def wait_apart(engine, semaphore, count):
    if not isinstance(count, int) or count > 0:
        engine.wait_ge(semaphore, count)
        engine.nop(nofuse=True)


class Element:

    def __init__(self, index, parity, count, group=2):
        self.index, self.par, self.count, self.group = index + parity // group, parity % group, count, group
        self.n = group * self.index + self.par

    def plus(self, k):
        return Element(self.index, self.par + k, self.count, self.group)

    def has(self, k):
        return not isinstance(self.n, int) or self.n + k < self.count

    def dma(self):
        return self.index * 16 + 16


def run_elements(engine, count, iteration, ahead=2, group=2):
    for par in range(group):
        iteration(Element(0, par, count, group))
    with engine.Fori(1, (count - ahead) // group) as index:
        for par in range(group):
            iteration(Element(index, par, count, group))
    for n in range((count - ahead) // group * group, count):
        iteration(Element(n // group, n % group, count, group))


def clear_semaphores(nc, sems):
    nums = sorted(s.num for s in sems)
    at = 0
    while at < len(nums):
        end = at + 1
        while end < len(nums) and nums[end] == nums[end - 1] + 1:
            end += 1
        nc.gpsimd.sem_clear(range(nums[at], nums[end - 1] + 1))
        at = end


def rows_of(t, el, tiles=QT):
    return t[bass.ts(el.n, tiles * P), :].rearrange("(t p) d -> p t d", p=P)


def attention_phase(nc, tag, heads, x_in, ctx_in, mask_in, mask_value, x_out, w_views, q_bias, k_bias,
                    v_bias, out_bias, ln_gain, ln_bias, spent=(), batches=BATCH):
    hd = DIM // heads
    hpg = P // hd
    GROUPS = KC
    pairs = heads // 2
    ring = 4
    sm_scale = float(hd) ** -0.5
    normed_twice = ln_gain is not None

    with ExitStack() as ctx:
        def sb(name, shape, dt=F32):
            return ctx.enter_context(nc.sbuf_tensor(f"{tag}_{name}", shape, dt))

        sems = []

        def sem(name):
            sems.append(ctx.enter_context(nc.semaphore(f"{tag}_{name}")))
            return sems[-1]

        def bank(name):
            return ctx.enter_context(nc.psum_tensor(f"{tag}_{name}", [P, 512], F32))

        wq, wk, wv, wo = [sb(w, [P, 2, KC, DIM], F32R) for w in ("wq", "wk", "wv", "wo")]
        ident = sb("ident", [P, P])
        cols = sb("cols", [P, 6, KC])
        BQ, BK, BV, GAIN, LBIAS = range(5)
        bo_row = sb("bo_row", [P, DIM])
        neg_half = sb("neg_half", [P, QT])
        xbuf = sb("xbuf", [P, 2, QT, DIM])
        cbuf = sb("cbuf", [P, 2, QT, DIM])
        resb = sb("resb", [P, 2, QT, DIM])
        mraw = sb("mraw", [P, 2, SEQ], mask_in.dtype)
        mbias = sb("mbias", [P, 2, SEQ])
        xn = sb("xn", [P, QT, DIM])
        stats = sb("stats", [P, QT, 6])
        mv = sb("mv", [P, QT, 2])
        ln = sb("ln", [P, 6, QT])
        xnT = sb("xnT", [P, 2, KC, SEQ], F32R)
        cT = sb("cT", [P, 2, KC, SEQ], F32R)
        qT = sb("qT", [P, 2, 2, KC, SEQ], F32R)
        kT = sb("kT", [P, 2, 2, KC, SEQ], F32R)
        vb = sb("vb", [P, 2, QT, DIM])
        probs = sb("probs", [P, ring, 2, QT, SEQ])
        negm = sb("negm", [P, ring, 2, QT])
        ssum = sb("ssum", [P, ring, 2 * QT])
        rinv = sb("rinv", [P, ring, 2 * QT])
        pT = sb("pT", [P, 2, hpg, QT, SEQ])
        oT = sb("oT", [P, 2, KC, SEQ], F32R)
        stage_q = probs[:, 2:4].rearrange("p s h t k -> p (s h t k)")
        stage_k = probs[:, 0:2].rearrange("p s h t k -> p (s h t k)")
        stage_v = vb[:].rearrange("p s t k -> p (s t k)")
        stage_o = pT[:].rearrange("p g h t k -> p (g h t k)")[:, 0:KC * DIM]
        view_q, view_k, view_v, view_o = w_views
        WEIGHTS = {"Wv": (0, view_v, stage_v, wv), "Wk": (1, view_k, stage_k, wk), "Wq": (2, view_q, stage_q, wq),
                   "Wo": (3, view_o, stage_o, wo)}

        s_bank = [bank(f"s{i}") for i in range(4)]
        x_bank = [bank("x0"), bank("x1")]
        pt_bank = bank("pt")
        o_bank = bank("o")

        w_loaded = [sem(f"w_loaded{i}") for i in range(4)]
        (cols_loaded, ident_zero, consts_ready, w_gained, w_hi, w_lo, qbias_mm, cols_ready,
         x_loaded0, x_loaded1, c_loaded0, c_loaded1, m_loaded0, m_loaded1, r_loaded0, r_loaded1,
         stored0, stored1, bn_done, stats_ready, ln_step, xn_ready, mbias_ready, res_ready,
         x_done, hi_done, lo_done, v_done, s_done, ttr_done, exp_done, recip_done, even_normed, odd_normed,
         pt_done, even_out, odd_out, pv_done, othi_done, otlo_done, op_done, out_done) = [sem(s) for s in (
             "cols_loaded ident_zero consts_ready w_gained w_hi w_lo qbias_mm cols_ready "
             "x_loaded0 x_loaded1 c_loaded0 c_loaded1 m_loaded0 m_loaded1 r_loaded0 r_loaded1 "
             "stored0 stored1 bn_done stats_ready ln_step xn_ready mbias_ready res_ready "
             "x_done hi_done lo_done v_done s_done ttr_done exp_done recip_done even_normed odd_normed "
             "pt_done even_out odd_out pv_done othi_done otlo_done op_done out_done").split()]
        x_loaded, c_loaded = (x_loaded0, x_loaded1), (c_loaded0, c_loaded1)
        m_loaded, r_loaded, stored = (m_loaded0, m_loaded1), (r_loaded0, r_loaded1), (stored0, stored1)

        USES = ["tc0", "tc1", "v0", "v1", "tx0", "tx1", "k0", "k1", "q0", "q1"]
        NU = len(USES)
        SPLIT = [u for u in USES if u[0] != "v"]
        NL = len(SPLIT)
        LEAD, HEAD = ["tc0", "tc1"], ["v0"]
        if pairs == 8:
            BETWEEN = [[], [], [], [], [], ["k0b"], ["k1b"], ["q0b"]]
            MID = [["v1a"], ["v1b"], ["tx0"], ["k0a"], ["tx1"], ["k1a"], ["q0a"], ["q1a"]]
            LAST = ["q1b"], []
        else:
            BETWEEN = [[], ["tx1"], ["k1a"], ["q0b"]]
            MID = [["v1", "tx0"], ["k0a", "k0b"], ["k1b", "q0a"], ["q1a"]]
            LAST = ["q1b"], []
        PROLOGUE = ["Wv", "tc0", "tc1", "Wk", "v0", "v1", "tx0", "Wq", "tx1", "k0", "k1", "Wo", "q0", "q1"]
        PE_PROLOGUE = ["tc0", "tc1", "Wv", "v0", "v1", "tx0", "Wk", "tx1", "Wq", "k0", "k1", "q0", "q1", "Wo"]
        NCOLS = sum(b is not None for b in (q_bias, k_bias, v_bias, ln_gain, ln_bias, out_bias))

        def group_after(pair):
            return (2 * pair + 1) // hpg if pair >= 0 and (2 * pair + 2) % hpg == 0 else None

        def finished(uses):
            return [u.rstrip("b") for u in uses if u[-1] != "a"]

        def feature_rows(u):
            bias = {"q": BQ, "k": BK}[u[0]]
            if (q_bias is None and not normed_twice) if u[0] == "q" else k_bias is None:
                bias = None
            return [2 * int(u[1]), 2 * int(u[1]) + 1], bias

        with nc.Block() as block:

            @block.sync
            def _(sp):
                def load_weight(name):
                    n, view, stage, _ = WEIGHTS[name]
                    sp.dma_start(stage.rearrange("p (k n) -> p k n", k=KC), view.rearrange("(k p) n -> p k n", p=P)) \
                      .then_inc(w_loaded[n], 16)

                def load_columns():
                    for n, b in enumerate((q_bias, k_bias, v_bias, ln_gain, ln_bias)):
                        if b is not None:
                            sp.dma_start(cols[:, n, :], b.rearrange("(k p) -> p k", p=P),
                                         allow_slow_non_contiguous=True).then_inc(cols_loaded, 16)
                    if out_bias is not None:
                        sp.dma_start(bo_row[:], out_bias.rearrange("(a n) -> a n", a=1).broadcast_to([P, DIM])) \
                          .then_inc(cols_loaded, 16)

                def load(el):
                    xs, cs = rows_of(x_in, el), rows_of(ctx_in, el)
                    ms = mask_in[bass.ds(el.n, 1), :].broadcast_to([P, SEQ])
                    wait_apart(sp, xn_ready, (el.n - 1) * QT)
                    sp.dma_start(xbuf[:, el.par], xs).then_inc(x_loaded[el.par], 16)
                    wait_apart(sp, x_done, (el.n - 2) * NU + 2)
                    sp.dma_start(cbuf[:, el.par], cs).then_inc(c_loaded[el.par], 16)
                    wait_apart(sp, mbias_ready, el.n - 1)
                    sp.dma_start(mraw[:, el.par], ms).then_inc(m_loaded[el.par], 16)

                def load_first(dst, src, par, done):
                    sp.dma_start(dst[:, par], rows_of(src, Element(0, par, batches))).then_inc(done[par], 16)

                load_first(cbuf, ctx_in, 0, c_loaded)
                load_weight("Wv")
                load_first(xbuf, x_in, 0, x_loaded)
                load_columns()
                load_weight("Wk")
                load_weight("Wq")
                load_first(xbuf, x_in, 1, x_loaded)
                load_first(cbuf, ctx_in, 1, c_loaded)
                for par in range(2):
                    sp.dma_start(mraw[:, par], mask_in[par:par + 1, :].broadcast_to([P, SEQ])).then_inc(m_loaded[par], 16)
                load_weight("Wo")
                sp.dma_start(resb[:, 0], rows_of(x_in, Element(0, 0, batches))).then_inc(r_loaded[0], 16)

                def iteration(el):
                    if el.has(2):
                        load(el.plus(2))
                    if el.has(1):
                        nxt, prev = el.plus(1), el.plus(-1)
                        rs = rows_of(x_in, nxt)
                        wait_apart(sp, stored[prev.par], prev.dma())
                        sp.dma_start(resb[:, nxt.par], rs).then_inc(r_loaded[nxt.par], 16)
                    dst = rows_of(x_out, el)
                    wait_apart(sp, out_done, (el.n + 1) * QT)
                    sp.dma_start(dst, resb[:, el.par]).then_inc(stored[el.par], 16)

                run_elements(sp, batches, iteration)
                for par in range(2):
                    sp.wait_ge(stored[par], batches // 2 * 16)

            @block.gpsimd
            def _(pool):
                clear_semaphores(nc, spent)
                nc.gpsimd.memset(ident[:], 0.0).then_inc(ident_zero, 1)
                nc.gpsimd.memset(neg_half[:], -0.5).then_inc(consts_ready, 1)
                pool.wait_ge(ident_zero, 1)
                nc.gpsimd.affine_select(out=ident[:], in_=ident[:], compare_op=ALU.not_equal, fill=1.0, base=0,
                                        pattern=[[-1, P]], channel_multiplier=1).then_inc(consts_ready, 1)
                pool.wait_ge(consts_ready, 2)

                LN_STEPS = 9 if normed_twice else 4

                def normalise(el):
                    step = [0]

                    def chained(ins):
                        step[0] += 1
                        ins.then_inc(ln_step, 1)
                        wait_apart(pool, ln_step, el.n * LN_STEPS + step[0])

                    pool.wait_ge(stats_ready, el.n + 1)
                    wait_apart(pool, x_done, (el.n - 1) * NU + USES.index("tx1") + 1)
                    mean, var = mv[:, :, 0], mv[:, :, 1]
                    chained(nc.gpsimd.tensor_scalar(ln[:, 0], var, 1.0, EPS, ALU.mult, ALU.add))
                    chained(nc.gpsimd.tensor_tensor(ln[:, 1], ln[:, 0], neg_half[:], ALU.pow))
                    r = ln[:, 1]
                    if normed_twice:
                        chained(nc.gpsimd.tensor_tensor(ln[:, 2], var, r, ALU.mult))
                        chained(nc.gpsimd.tensor_tensor(ln[:, 0], ln[:, 2], r, ALU.mult))
                        chained(nc.gpsimd.tensor_scalar(ln[:, 2], ln[:, 0], 1.0, EPS, ALU.mult, ALU.add))
                        chained(nc.gpsimd.tensor_tensor(ln[:, 3], ln[:, 2], neg_half[:], ALU.pow))
                        chained(nc.gpsimd.tensor_tensor(ln[:, 1], r, ln[:, 3], ALU.mult))
                    chained(nc.gpsimd.tensor_tensor(ln[:, 4], mean, r, ALU.mult))
                    chained(nc.gpsimd.tensor_scalar(ln[:, 5], ln[:, 4], -1.0, 0.0, ALU.mult, ALU.add))
                    for t in range(QT):
                        nc.gpsimd.tensor_scalar(xn[:, t], xbuf[:, el.par, t], r[:, t:t + 1], ln[:, 5, t:t + 1],
                                                ALU.mult, ALU.add).then_inc(xn_ready, 1)

                def norm_probs(el, p):
                    wait_apart(pool, recip_done, el.n * pairs + p + 1)
                    for t in range(QT):
                        pr = probs[:, p % ring, 1, t]
                        last = nc.gpsimd.tensor_scalar(pr, pr, rinv[:, p % ring, QT + t:QT + t + 1], 0.0,
                                                       ALU.mult, ALU.add)
                    last.then_inc(odd_normed, 1)

                def add_out_bias(el):
                    pool.wait_ge(r_loaded[el.par], el.dma())
                    for t in range(QT):
                        nc.gpsimd.tensor_tensor(resb[:, el.par, t], resb[:, el.par, t], bo_row[:], ALU.add) \
                            .then_inc(res_ready, 1)

                normalise(Element(0, 0, batches))
                normalise(Element(0, 1, batches))
                pool.wait_ge(cols_loaded, NCOLS * 16)

                def iteration(el):
                    for p in range(pairs):
                        norm_probs(el, p)
                        if p == pairs - 2 and out_bias is not None:
                            add_out_bias(el)
                    if el.has(2):
                        normalise(el.plus(2))

                run_elements(pool, batches, iteration)

            @block.scalar
            def _(act):
                def hi_of_weight(name):
                    n, _, stage, w = WEIGHTS[name]
                    act.wait_ge(w_loaded[n], 16)
                    if name == "Wq" and normed_twice:
                        act.wait_ge(w_gained, KC)
                    nc.scalar.activation(w[:, HI].rearrange("p k n -> p (k n)"), stage, ACT.Copy).then_inc(w_hi, 1)
                    if name == "Wq" and normed_twice:
                        act.wait_ge(qbias_mm, 1)
                        nc.scalar.activation(cols[:, BQ], o_bank[:, 0:KC], ACT.Copy).then_inc(cols_ready, 1)
                        act.wait_ge(cols_ready, 1)
                    if name == "Wq":
                        act.wait_ge(cols_loaded, NCOLS * 16)

                def hi_of(el, u):
                    act.wait_ge(x_done, el.n * NU + USES.index(u) + 1)
                    src = x_bank[USES.index(u) % 2]
                    t = int(u[-1])
                    if u[0] == "v":
                        nc.scalar.activation(vb[:, el.par, t], src[:], ACT.Copy).then_inc(v_done, 1)
                    elif u[0] == "t":
                        dst = {"c": cT, "x": xnT}[u[1]]
                        nc.scalar.activation(dst[:, HI, :, t * P:(t + 1) * P],
                                             src[:].rearrange("p (k n) -> p k n", k=KC), ACT.Copy) \
                            .then_inc(hi_done, 1)
                    else:
                        dst = {"q": qT, "k": kT}[u[0]]
                        fs, bias = feature_rows(u)
                        if bias is None:
                            nc.scalar.activation(dst[:, el.par, HI, fs[0]:fs[0] + 2].rearrange("p f n -> p (f n)"),
                                                 src[:], ACT.Copy).then_inc(hi_done, 1)
                        else:
                            for m, f in enumerate(fs):
                                last = nc.scalar.activation(dst[:, el.par, HI, f], src[:, m * SEQ:(m + 1) * SEQ],
                                                            ACT.Identity, bias=cols[:, bias, f:f + 1])
                            last.then_inc(hi_done, 1)

                def exps(el, p, hs=(0, 1)):
                    for h in hs:
                        for t in range(QT):
                            act.wait_ge(ttr_done, (el.n * pairs + p) * 2 * QT + 2 * h + t + 1)
                            pr = probs[:, p % ring, h, t]
                            nc.scalar.activation(pr, pr, ACT.Exp, bias=negm[:, p % ring, h, t:t + 1], scale=-1.0,
                                                 accum_out=ssum[:, p % ring, 2 * h + t:2 * h + t + 1]) \
                                .then_inc(exp_done, 1)

                def probs_out(el, p):
                    h = 2 * p + 1
                    act.wait_ge(pt_done, el.n * heads + h + 1)
                    nc.scalar.activation(pT[:, (h // hpg) % 2, h % hpg].rearrange("p t n -> p (t n)"),
                                         pt_bank[:], ACT.Copy).then_inc(odd_out, 1)

                def attn_hi(el, g):
                    act.wait_ge(pv_done, el.n * GROUPS + g + 1)
                    if v_bias is None:
                        nc.scalar.activation(oT[:, HI, g], o_bank[:, 0:SEQ], ACT.Copy).then_inc(othi_done, 1)
                    else:
                        nc.scalar.activation(oT[:, HI, g], o_bank[:, 0:SEQ], ACT.Identity,
                                             bias=cols[:, BV, g:g + 1]).then_inc(othi_done, 1)

                for u in PROLOGUE:
                    if u in WEIGHTS:
                        hi_of_weight(u)
                    else:
                        hi_of(Element(0, 0, batches), u)
                for u in LEAD:
                    hi_of(Element(0, 1, batches), u)

                def iteration(el):
                    exps(el, 0)
                    exps(el, 1)
                    for u in HEAD if el.has(1) else ():
                        hi_of(el.plus(1), u)
                    for p in range(pairs):
                        if p == 0:
                            exps(el, 2)
                        for u in finished(BETWEEN[p]) if el.has(1) else ():
                            hi_of(el.plus(1), u)
                        probs_out(el, p)
                        if group_after(p - 1) is not None:
                            attn_hi(el, group_after(p - 1))
                        if p + 3 < pairs:
                            exps(el, p + 3, (0,))
                        for u in finished(MID[p]) if el.has(1) else ():
                            hi_of(el.plus(1), u)
                        if p + 3 < pairs:
                            exps(el, p + 3, (1,))
                    for u in finished(LAST[0]) if el.has(1) else ():
                        hi_of(el.plus(1), u)
                    attn_hi(el, GROUPS - 1)
                    for u in finished(LAST[1]) if el.has(1) else ():
                        hi_of(el.plus(1), u)
                    if el.has(2):
                        hi_of(el.plus(2), LEAD[0])
                    if el.has(2):
                        hi_of(el.plus(2), LEAD[1])

                run_elements(act, batches, iteration)

            @block.vector
            def _(dve):
                def lo_of_weight(name):
                    n, _, stage, w = WEIGHTS[name]
                    if name == "Wq" and normed_twice:
                        dve.wait_ge(w_loaded[n], 16)
                        dve.wait_ge(cols_loaded, NCOLS * 16)
                        dve.wait_ge(qbias_mm, 1)
                        for k in range(KC):
                            rows = stage[:, k * DIM:(k + 1) * DIM]
                            nc.vector.tensor_scalar(rows, rows, cols[:, GAIN, k:k + 1], None, ALU.mult) \
                                .then_inc(w_gained, 1)
                        dve.wait_ge(w_gained, KC)
                    dve.wait_ge(w_hi, n + 1)
                    nc.vector.tensor_tensor(w[:, LO].rearrange("p k n -> p (k n)"), stage,
                                            w[:, HI].rearrange("p k n -> p (k n)").bitcast(F32), ALU.subtract) \
                        .then_inc(w_lo, 1)
                    if name == "Wq" and normed_twice:
                        dve.wait_ge(cols_ready, 1)
                    if name == "Wq":
                        dve.wait_ge(cols_loaded, NCOLS * 16)

                def row_stats(el):
                    dve.wait_ge(x_loaded[el.par], el.dma())
                    wait_for(dve, xn_ready, el.n * QT)
                    for t in range(QT):
                        nc.vector.bn_stats(stats[:, t], xbuf[:, el.par, t]).then_inc(bn_done, 1)
                    wait_apart(dve, bn_done, (el.n + 1) * QT)
                    for t in range(QT):
                        last = nc.vector.bn_aggr(mv[:, t], stats[:, t])
                    last.then_inc(stats_ready, 1)

                def mask_bias(el):
                    dve.wait_ge(m_loaded[el.par], el.dma())
                    nc.vector.tensor_scalar(mbias[:, el.par], mraw[:, el.par], 0.0, mask_value,
                                            ALU.is_equal, ALU.mult).then_inc(mbias_ready, 1)

                def scores_out(el, p):
                    wait_apart(dve, s_done, el.n * pairs + p + 1)
                    for h in range(2):
                        for t in range(QT):
                            nc.vector.tensor_tensor_reduce(
                                out=probs[:, p % ring, h, t], in0=s_bank[2 * (p % 2) + h][:, t * SEQ:(t + 1) * SEQ],
                                in1=mbias[:, el.par], scale=-sm_scale, scalar=BIG, op0=ALU.add, op1=ALU.min,
                                accum_out=negm[:, p % ring, h, t:t + 1]).then_inc(ttr_done, 1)

                def probs_out(el, p):
                    h = 2 * p
                    dve.wait_ge(pt_done, el.n * heads + h + 1)
                    nc.vector.tensor_copy(pT[:, (h // hpg) % 2, h % hpg].rearrange("p t n -> p (t n)"), pt_bank[:]) \
                        .then_inc(even_out, 1)

                def recip(el, p):
                    dve.wait_ge(exp_done, (el.n * pairs + p + 1) * 2 * QT)
                    nc.vector.reciprocal(rinv[:, p % ring], ssum[:, p % ring]).then_inc(recip_done, 1)
                    dve.wait_ge(recip_done, el.n * pairs + p + 1)
                    for t in range(QT):
                        pr = probs[:, p % ring, 0, t]
                        last = nc.vector.tensor_scalar(pr, pr, rinv[:, p % ring, t:t + 1], None, ALU.mult)
                    last.then_inc(even_normed, 1)

                def lo_of(el, u):
                    if u[0] == "v":
                        return
                    dve.wait_ge(hi_done, el.n * NL + SPLIT.index(u) + 1)
                    src = x_bank[USES.index(u) % 2]
                    t = int(u[-1])
                    if u[0] == "t":
                        dst = {"c": cT, "x": xnT}[u[1]]
                        cut = slice(t * P, (t + 1) * P)
                        nc.vector.tensor_tensor(dst[:, LO, :, cut], src[:].rearrange("p (k n) -> p k n", k=KC),
                                                dst[:, HI, :, cut].bitcast(F32), ALU.subtract).then_inc(lo_done, 1)
                        return
                    dst = {"q": qT, "k": kT}[u[0]]
                    fs, bias = feature_rows(u)
                    if bias is None:
                        hi, lo = (dst[:, el.par, part, fs[0]:fs[0] + 2].rearrange("p f n -> p (f n)")
                                  for part in (HI, LO))
                        nc.vector.tensor_tensor(lo, src[:], hi.bitcast(F32), ALU.subtract).then_inc(lo_done, 1)
                    else:
                        for m, f in enumerate(fs):
                            last = nc.vector.scalar_tensor_tensor(
                                dst[:, el.par, LO, f], src[:, m * SEQ:(m + 1) * SEQ], cols[:, bias, f:f + 1],
                                dst[:, el.par, HI, f].bitcast(F32), ALU.add, ALU.subtract)
                        last.then_inc(lo_done, 1)

                def attn_lo(el, g):
                    dve.wait_ge(othi_done, el.n * GROUPS + g + 1)
                    if v_bias is None:
                        nc.vector.tensor_tensor(oT[:, LO, g], o_bank[:, 0:SEQ], oT[:, HI, g].bitcast(F32),
                                                ALU.subtract).then_inc(otlo_done, 1)
                    else:
                        nc.vector.scalar_tensor_tensor(oT[:, LO, g], o_bank[:, 0:SEQ], cols[:, BV, g:g + 1],
                                                       oT[:, HI, g].bitcast(F32), ALU.add, ALU.subtract) \
                            .then_inc(otlo_done, 1)

                def rows_out(el):
                    if out_bias is None:
                        dve.wait_ge(r_loaded[el.par], el.dma())
                    else:
                        dve.wait_ge(res_ready, (el.n + 1) * QT)
                    for t in range(QT):
                        dve.wait_ge(op_done, el.n * QT + t + 1)
                        nc.vector.tensor_tensor(resb[:, el.par, t], s_bank[2 + t][:], resb[:, el.par, t], ALU.add) \
                            .then_inc(out_done, 1)

                row_stats(Element(0, 0, batches))
                for u in PROLOGUE:
                    if u in WEIGHTS:
                        lo_of_weight(u)
                    else:
                        lo_of(Element(0, 0, batches), u)
                mask_bias(Element(0, 0, batches))
                row_stats(Element(0, 1, batches))
                for u in LEAD:
                    lo_of(Element(0, 1, batches), u)

                def iteration(el):
                    scores_out(el, 0)
                    scores_out(el, 1)
                    recip(el, 0)
                    recip(el, 1)
                    scores_out(el, 2)
                    for u in HEAD if el.has(1) else ():
                        lo_of(el.plus(1), u)
                    for p in range(pairs):
                        probs_out(el, p)
                        if p == 0 and el.has(1):
                            mask_bias(el.plus(1))
                        for u in finished(MID[p - 1]) if p > 0 and el.has(1) else ():
                            lo_of(el.plus(1), u)
                        if p + 3 < pairs:
                            scores_out(el, p + 3)
                        if p + 2 < pairs:
                            recip(el, p + 2)
                        for u in finished(BETWEEN[p]) if el.has(1) else ():
                            lo_of(el.plus(1), u)
                        if group_after(p - 1) is not None:
                            attn_lo(el, group_after(p - 1))
                        if p == pairs - 1 and el.has(2):
                            row_stats(el.plus(2))
                    for u in finished(MID[pairs - 1] + LAST[0]) if el.has(1) else ():
                        lo_of(el.plus(1), u)
                    attn_lo(el, GROUPS - 1)
                    for u in finished(LAST[1]) if el.has(1) else ():
                        lo_of(el.plus(1), u)
                    if el.has(2):
                        lo_of(el.plus(2), LEAD[0])
                    rows_out(el)
                    if el.has(2):
                        lo_of(el.plus(2), LEAD[1])

                run_elements(dve, batches, iteration)

            @block.tensor
            def _(pe):
                pe.wait_ge(consts_ready, 2)

                def weight_ready(name):
                    n, _, stage, _ = WEIGHTS[name]
                    if name == "Wq" and normed_twice:
                        pe.wait_ge(w_loaded[n], 16)
                        pe.wait_ge(cols_loaded, NCOLS * 16)
                        for f in range(KC):
                            for k in range(KC):
                                last = nc.tensor.matmul(o_bank[:, f:f + 1], stage[:, k * DIM + f * P:k * DIM + (f + 1) * P],
                                                        cols[:, LBIAS, k:k + 1], start=(k == 0), stop=(k == KC - 1))
                        last.then_inc(qbias_mm, 1)
                        pe.wait_ge(cols_ready, 1)
                    pe.wait_ge(w_lo, n + 1)

                def use(el, u):
                    part, u = (u[-1], u[:-1]) if u[-1] in "ab" else ("", u)
                    n = USES.index(u)
                    before = el if n >= 2 else el.plus(-1)
                    prev = USES[(n - 2) % NU]
                    if part == "b":
                        pass
                    elif prev[0] == "v":
                        wait_for(pe, v_done, before.n * QT + int(prev[1]) + 1)
                    else:
                        wait_for(pe, lo_done, before.n * NL + SPLIT.index(prev) + 1)
                    dst, t = x_bank[n % 2], int(u[-1])
                    if u[0] == "t":
                        if u[1] == "x":
                            pe.wait_ge(xn_ready, el.n * QT + t + 1)
                            src = xn[:, t]
                        else:
                            pe.wait_ge(c_loaded[el.par], el.dma())
                            src = cbuf[:, el.par, t]
                        for k in range(KC):
                            last = nc.tensor.transpose(dst[:, k * P:(k + 1) * P], src[:, k * P:(k + 1) * P], ident[:])
                    elif u[0] == "v":
                        pe.wait_ge(lo_done, el.n * NL + SPLIT.index("tc1") + 1)
                        for k in {"a": range(KC // 2), "b": range(KC // 2, KC), "": range(KC)}[part]:
                            for a, b in TERMS:
                                last = nc.tensor.matmul(dst[:], cT[:, a, k, t * P:(t + 1) * P], wv[:, b, k],
                                                        start=(k == 0 and (a, b) == TERMS[0]),
                                                        stop=(k == KC - 1 and (a, b) == TERMS[-1]))
                    else:
                        w, src, need = (wq, xnT, "tx1") if u[0] == "q" else (wk, cT, "tc1")
                        pe.wait_ge(lo_done, el.n * NL + SPLIT.index(need) + 1)
                        for m, f in enumerate(feature_rows(u)[0]):
                            if part == "ab"[1 - m]:
                                continue
                            for k in range(KC):
                                for a, b in TERMS:
                                    last = nc.tensor.matmul(dst[:, m * SEQ:(m + 1) * SEQ],
                                                            w[:, b, k, f * P:(f + 1) * P], src[:, a, k],
                                                            start=(k == 0 and (a, b) == TERMS[0]),
                                                            stop=(k == KC - 1 and (a, b) == TERMS[-1]))
                    if part != "a":
                        last.then_inc(x_done, 1)

                def scores(el, p):
                    if p == 0:
                        pe.wait_ge(lo_done, (el.n + 1) * NL)
                    wait_for(pe, ttr_done, (el.n * pairs + p - 1) * 2 * QT)
                    if p == 1:
                        wait_for(pe, out_done, el.n * QT)
                    for t in range(QT):
                        for a, b in TERMS:
                            for m in range(2):
                                h = 2 * p + m
                                r = slice((h % hpg) * hd, (h % hpg + 1) * hd)
                                last = nc.tensor.matmul(
                                    s_bank[2 * (p % 2) + m][:, t * SEQ:(t + 1) * SEQ],
                                    qT[r, el.par, a, h // hpg, t * P:(t + 1) * P], kT[r, el.par, b, h // hpg],
                                    start=((a, b) == TERMS[0]), stop=((a, b) == TERMS[-1]))
                    last.then_inc(s_done, 1)

                def transpose_probs(el, h):
                    p, m = h // 2, h % 2
                    pe.wait_ge(odd_normed if m else even_normed, el.n * pairs + p + 1)
                    wait_for(pe, even_out if m else odd_out, el.n * pairs + p + m)
                    for kt in range(QT):
                        for t in range(QT):
                            last = nc.tensor.transpose(pt_bank[:, kt * SEQ + t * P:kt * SEQ + (t + 1) * P],
                                                       probs[:, p % ring, m, t, kt * P:(kt + 1) * P], ident[:])
                    last.then_inc(pt_done, 1)

                def probs_v(el, g):
                    pe.wait_ge(even_out, el.n * pairs + (g + 1) * hpg // 2)
                    pe.wait_ge(odd_out, el.n * pairs + (g + 1) * hpg // 2)
                    pe.wait_ge(v_done, (el.n + 1) * QT)
                    wait_for(pe, otlo_done, el.n * GROUPS + g)
                    for kt in range(QT):
                        for m in range(hpg):
                            c = slice(m * hd, (m + 1) * hd)
                            last = nc.tensor.matmul(o_bank[c, 0:SEQ], vb[:, el.par, kt, g * P + m * hd:g * P + (m + 1) * hd],
                                                    pT[:, g % 2, m, kt], start=(kt == 0), stop=(kt == QT - 1),
                                                    skip_group_check=True)
                    last.then_inc(pv_done, 1)

                def project(el):
                    for t in range(QT):
                        for k in range(KC):
                            if t == 0:
                                pe.wait_ge(otlo_done, el.n * GROUPS + k + 1)
                            for a, b in TERMS:
                                last = nc.tensor.matmul(s_bank[2 + t][:], oT[:, a, k, t * P:(t + 1) * P], wo[:, b, k],
                                                        start=(k == 0 and (a, b) == TERMS[0]),
                                                        stop=(k == KC - 1 and (a, b) == TERMS[-1]))
                        last.then_inc(op_done, 1)

                for u in PE_PROLOGUE:
                    if u in WEIGHTS:
                        weight_ready(u)
                    else:
                        use(Element(0, 0, batches), u)
                for u in LEAD:
                    use(Element(0, 1, batches), u)

                def iteration(el):
                    scores(el, 0)
                    scores(el, 1)
                    for u in HEAD if el.has(1) else ():
                        use(el.plus(1), u)
                    scores(el, 2)
                    for p in range(pairs):
                        transpose_probs(el, 2 * p)
                        if p + 3 < pairs:
                            scores(el, p + 3)
                        for u in BETWEEN[p] if el.has(1) else ():
                            use(el.plus(1), u)
                        transpose_probs(el, 2 * p + 1)
                        if group_after(p - 1) is not None:
                            probs_v(el, group_after(p - 1))
                        for u in MID[p] if el.has(1) else ():
                            use(el.plus(1), u)
                    for u in LAST[0] if el.has(1) else ():
                        use(el.plus(1), u)
                    probs_v(el, GROUPS - 1)
                    for u in LAST[1] if el.has(1) else ():
                        use(el.plus(1), u)
                    if el.has(2):
                        use(el.plus(2), LEAD[0])
                    project(el)
                    if el.has(2):
                        use(el.plus(2), LEAD[1])

                run_elements(pe, batches, iteration)
    return sems


def ternary_ffn_phase(nc, tag, x_in, x_out, w_gate, w_up, w_down, spent=(), tiles=TOK // P):
    inner = w_gate.shape[0]
    NC = inner // DIM
    IK = inner // P
    WN = inner * DIM // P
    MAGIC = 1.5 * 2.0 ** 23
    QMAX = 127.0

    with ExitStack() as ctx:
        def sb(name, shape, dt=F32):
            return ctx.enter_context(nc.sbuf_tensor(f"{tag}_{name}", shape, dt))

        sems = []

        def sem(name):
            sems.append(ctx.enter_context(nc.semaphore(f"{tag}_{name}")))
            return sems[-1]

        wg = sb("wg", [P, KC, inner], BF16)
        wu = sb("wu", [P, KC, inner], BF16)
        wd = sb("wd", [P, IK, DIM], BF16)
        wscale = sb("wscale", [P, 3])
        ident = sb("ident", [P, P], BF16)

        raw = sb("raw", [P, 3, WN])
        tern = sb("tern", [P, 3, WN], BF16)
        ones = sb("ones", [P, P])
        wsum = sb("wsum", [P, 3, 4])
        wpart = sb("wpart", [P, 3])
        winv = sb("winv", [P, 3])
        wmean = sb("wmean", [P, 3])
        (w_abs_act, w_abs_dve, w_part, w_total, w_scale, w_rounded, w_integer, w_turned, w_out,
         consts_ready, ident_zero) = [sem(n) for n in (
             "w_abs_act w_abs_dve w_part w_total w_scale w_rounded w_integer w_turned w_out "
             "consts_ready ident_zero").split()]
        w_loaded = [[sem(f"w_loaded{i}_{c}") for c in range(4)] for i in range(3)]
        SLICES = 4
        SN = WN // SLICES

        def piece(t, n, c):
            return t[:, n, c * SN:(c + 1) * SN]

        turns = []
        for n, dst in enumerate((wg, wu)):
            for half in range(IK // 8):
                for k in range(KC):
                    pieces = [(o, k) for o in range(half * 8, half * 8 + 8)]
                    turns.append((n, dst[:, k, half * 1024:(half + 1) * 1024],
                                  [(o * DIM + k * P) for o, k in pieces]))
        for ik in range(0, IK, 2):
            turns.append((2, wd[:, ik:ik + 2].rearrange("p a b -> p (a b)"),
                          [o * inner + (ik + a) * P for a in range(2) for o in range(KC)]))

        neg_half = sb("neg_half", [P, 1])
        xbuf = sb("xbuf", [P, 2, DIM])
        stats = sb("stats", [P, 2, 6])
        mv = sb("mv", [P, 2, 2])
        ln = sb("ln", [P, 2, 4])
        xn = sb("xn", [P, 2, DIM])
        xmax = sb("xmax", [P, 2, 3])
        xs = sb("xs", [P, 2, 2])
        xround = sb("xround", [P, 2, DIM])
        xq = sb("xq", [P, 2, DIM], BF16)
        hmax = sb("hmax", [P, 2, 3])
        hpart = sb("hpart", [P, 2, NC])
        hs = sb("hs", [P, 2, 1])
        free = raw[:, 0:2].rearrange("p n w -> p (n w)")
        taken = [0]

        def view(size, dt=F32):
            at, n = taken[0], size // (1 if dt == F32 else 2)
            taken[0] += n
            return free[:, at:at + n] if dt == F32 else free[:, at:at + n].bitcast(dt)

        resb = view(2 * DIM).rearrange("p (a d) -> p a d", a=2)
        gate = view(4 * DIM).rearrange("p (c d) -> p c d", c=4)
        hid = view(2 * inner).rearrange("p (a d) -> p a d", a=2)
        hround = view(2 * inner).rearrange("p (a d) -> p a d", a=2)
        hq = view(2 * inner, BF16).rearrange("p (a d) -> p a d", a=2)
        hqT = view(2 * inner, BF16).rearrange("p (a k n) -> p a k n", a=2, n=P)
        xqT = view(2 * DIM, BF16).rearrange("p (a k n) -> p a k n", a=2, n=P)

        g_bank = [ctx.enter_context(nc.psum_tensor(f"{tag}_g{i}", [P, 512], F32)) for i in range(2)]
        u_bank = [ctx.enter_context(nc.psum_tensor(f"{tag}_u{i}", [P, 512], F32)) for i in range(2)]
        tx_bank = ctx.enter_context(nc.psum_tensor(f"{tag}_tx", [P, 1024], BF16))
        th_bank = [ctx.enter_context(nc.psum_tensor(f"{tag}_th{i}", [P, 1024], BF16)) for i in range(IK // 8)]
        d_bank = ctx.enter_context(nc.psum_tensor(f"{tag}_d", [P, 512], F32))
        sum_bank = u_bank[1]
        t_bank = [th_bank[0], th_bank[1], d_bank[:].bitcast(BF16)]
        TH = IK // 8

        (const_ready, x_loaded0, x_loaded1, r_loaded0, r_loaded1, stored0, stored1, bn_done, stats_ready, ln_step,
         xn_ready, xmax_ready, xmax_step, xs_ready, x_round, xq_ready, tx_done, th_done, tx_out, th_out, g_done, silu_done, u_done,
         h_done, hmax_step, hpart_ready, hs_ready, hmax_ready, h_round, hq_ready, d_done, out_done) = [sem(n) for n in (
             "const_ready x_loaded0 x_loaded1 r_loaded0 r_loaded1 stored0 stored1 bn_done stats_ready ln_step "
             "xn_ready xmax_ready xmax_step xs_ready x_round xq_ready tx_done th_done tx_out th_out g_done silu_done u_done "
             "h_done hmax_step hpart_ready hs_ready hmax_ready h_round hq_ready d_done out_done").split()]
        x_loaded, r_loaded, stored = (x_loaded0, x_loaded1), (r_loaded0, r_loaded1), (stored0, stored1)
        first = [Element(0, n, tiles) for n in range(4)]

        def rows(t, el):
            return t[bass.ts(el.n, P), :]

        def quant_scales(dve, el, m, step):
            nc.vector.tensor_scalar(m[:, 1:2], m[:, 0:1], 1e-5, 1.0 / QMAX, ALU.max, ALU.mult).then_inc(step, 1)
            wait_apart(dve, step, el.n * 2 + 1)
            nc.vector.reciprocal(m[:, 2:3], m[:, 1:2]).then_inc(step, 1)

        with nc.Block() as block:
            @block.sync
            def _(sp):
                def load_x(el):
                    src = rows(x_in, el)
                    wait_apart(sp, xn_ready, el.n - 1)
                    sp.dma_start(xbuf[:, el.par], src).then_inc(x_loaded[el.par], 16)

                def load_res(el):
                    src, prev = rows(x_in, el), el.plus(-2)
                    wait_apart(sp, stored[el.par], prev.dma())
                    sp.dma_start(resb[:, el.par], src).then_inc(r_loaded[el.par], 16)

                for n, w in enumerate((w_gate, w_up, w_down)):
                    cols = w.shape[1]
                    view = w.rearrange("(t p) c -> p t c", p=P)
                    t = SN // cols
                    for c in range(SLICES):
                        sp.dma_start(piece(raw, n, c).rearrange("p (t c) -> p t c", c=cols), view[:, c * t:(c + 1) * t]) \
                          .then_inc(w_loaded[n][c], 16)
                    if n == 1:
                        for el in first[:2]:
                            load_x(el)

                for el in first[2:]:
                    load_x(el)
                sp.wait_ge(w_integer, 2 * SLICES)
                load_res(first[0])

                def iteration(el):
                    if el.has(4):
                        load_x(el.plus(4))
                    if el.has(1):
                        load_res(el.plus(1))
                    dst = rows(x_out, el)
                    wait_apart(sp, out_done, el.n + 1)
                    sp.dma_start(dst, resb[:, el.par]).then_inc(stored[el.par], 16)

                run_elements(sp, tiles, iteration, ahead=4)
                for par in range(2):
                    sp.wait_ge(stored[par], tiles // 2 * 16)

            @block.gpsimd
            def _(pool):
                clear_semaphores(nc, spent)
                nc.gpsimd.memset(ident[:], 0.0).then_inc(ident_zero, 1)
                nc.gpsimd.memset(ones[:], 1.0).then_inc(consts_ready, 1)
                pool.wait_ge(ident_zero, 1)
                nc.gpsimd.affine_select(out=ident[:], in_=ident[:], compare_op=ALU.not_equal, fill=1.0, base=0,
                                        pattern=[[-1, P]], channel_multiplier=1).then_inc(consts_ready, 1)

                for n in range(3):
                    wait_apart(pool, w_scale, 3 * n + 3)
                    for c in range(SLICES):
                        nc.gpsimd.tensor_scalar(piece(raw, n, c), piece(raw, n, c), winv[:, n:n + 1], MAGIC,
                                                ALU.mult, ALU.add).then_inc(w_rounded, 1)
                nc.gpsimd.memset(neg_half[:], -0.5).then_inc(const_ready, 1)
                pool.wait_ge(const_ready, 1)

                def normalise(el):
                    def chained(k, ins):
                        ins.then_inc(ln_step, 1)
                        wait_apart(pool, ln_step, el.n * 4 + k)

                    wait_apart(pool, stats_ready, el.n + 1)
                    l, m = ln[:, el.par], mv[:, el.par]
                    chained(1, nc.gpsimd.tensor_scalar(l[:, 0:1], m[:, 1:2], 1.0, EPS, ALU.mult, ALU.add))
                    chained(2, nc.gpsimd.tensor_tensor(l[:, 1:2], l[:, 0:1], neg_half[:], ALU.pow))
                    chained(3, nc.gpsimd.tensor_tensor(l[:, 2:3], m[:, 0:1], l[:, 1:2], ALU.mult))
                    chained(4, nc.gpsimd.tensor_scalar(l[:, 3:4], l[:, 2:3], -1.0, 0.0, ALU.mult, ALU.add))
                    wait_apart(pool, xmax_ready, el.n - 1)
                    nc.gpsimd.tensor_scalar(xn[:, el.par], xbuf[:, el.par], l[:, 1:2], l[:, 3:4],
                                            ALU.mult, ALU.add).then_inc(xn_ready, 1)

                def quantise_x(el):
                    wait_apart(pool, xmax_step, el.n * 2 + 2)
                    nc.gpsimd.tensor_scalar(xround[:, el.par], xn[:, el.par], xmax[:, el.par, 2:3], MAGIC,
                                            ALU.mult, ALU.add).then_inc(x_round, 1)
                    wait_apart(pool, x_round, el.n + 1)
                    wait_apart(pool, tx_done, el.n - 1)
                    nc.gpsimd.tensor_scalar(xq[:, el.par], xround[:, el.par], -MAGIC, 1.0,
                                            ALU.add, ALU.mult).then_inc(xq_ready, 1)

                def quantise_h(el):
                    wait_apart(pool, hmax_step, el.n * 2 + 2)
                    nc.gpsimd.tensor_scalar(hround[:, el.par], hid[:, el.par], hmax[:, el.par, 2:3], MAGIC,
                                            ALU.mult, ALU.add).then_inc(h_round, 1)
                    wait_apart(pool, h_round, el.n + 1)
                    wait_apart(pool, th_done, (el.n - 1) * TH)
                    nc.gpsimd.tensor_scalar(hq[:, el.par], hround[:, el.par], -MAGIC, 1.0,
                                            ALU.add, ALU.mult).then_inc(hq_ready, 1)

                normalise(first[0])
                quantise_x(first[0])
                normalise(first[1])
                quantise_x(first[1])
                normalise(first[2])
                quantise_h(first[0])

                def iteration(el):
                    if el.has(2):
                        quantise_x(el.plus(2))
                    if el.has(3):
                        normalise(el.plus(3))
                    if el.has(1):
                        quantise_h(el.plus(1))

                run_elements(pool, tiles, iteration, ahead=4)

            @block.scalar
            def _(act):
                def magnitudes(n):
                    for c in range(SLICES - 1):
                        act.wait_ge(w_loaded[n][c], 16)
                        nc.scalar.activation(piece(tern, n, c), piece(raw, n, c), ACT.Abs,
                                             accum_out=wsum[:, n, c:c + 1]).then_inc(w_abs_act, 1)

                def integers(n):
                    for c in range(SLICES):
                        act.wait_ge(w_rounded, n * SLICES + c + 1)
                        nc.scalar.activation(piece(tern, n, c), piece(raw, n, c), ACT.Copy, bias=-MAGIC) \
                            .then_inc(w_integer, 1)

                magnitudes(0)
                magnitudes(1)
                integers(0)
                magnitudes(2)
                integers(1)
                integers(2)

                def turned_x(el):
                    act.wait_ge(tx_done, el.n + 1)
                    nc.scalar.activation(xqT[:, el.par].rearrange("p k n -> p (k n)"), tx_bank[:, 0:DIM],
                                         ACT.Copy).then_inc(tx_out, 1)

                def silus(el, cs):
                    for c in cs:
                        act.wait_ge(g_done, el.n * NC + c + 1)
                        wait_for(act, h_done, (el.n - 1) * NC + c + 1)
                        if c == 0:
                            act.wait_ge(xs_ready, el.n * 2 + 1)
                        nc.scalar.activation(gate[:, c % 4], g_bank[c % 2][:], ACT.Silu, scale=xs[:, el.par, 0:1]) \
                            .then_inc(silu_done, 1)

                def turned_h(el):
                    for m in range(IK // 8):
                        act.wait_ge(th_done, el.n * TH + m + 1)
                        nc.scalar.activation(hqT[:, el.par, 8 * m:8 * m + 8].rearrange("p k n -> p (k n)"),
                                             th_bank[m][:], ACT.Copy).then_inc(th_out, 1)

                turned_x(first[0])
                silus(first[0], range(NC))
                turned_x(first[1])

                def iteration(el):
                    if el.has(1):
                        silus(el.plus(1), range(NC - 1))
                    turned_h(el)
                    if el.has(1):
                        silus(el.plus(1), range(NC - 1, NC))
                    if el.has(2):
                        turned_x(el.plus(2))

                run_elements(act, tiles, iteration, ahead=4)

            @block.vector
            def _(dve):
                def scale(n):
                    last = SLICES - 1
                    dve.wait_ge(w_loaded[n][last], 16)
                    nc.vector.tensor_reduce(wsum[:, n, last:last + 1], piece(raw, n, last), AX.X, ALU.add,
                                            apply_absolute_value=True).then_inc(w_abs_dve, 1)
                    dve.wait_ge(w_abs_act, (n + 1) * last)
                    dve.wait_ge(w_abs_dve, n + 1)
                    nc.vector.reduce_sum(wpart[:, n:n + 1], wsum[:, n], AX.X).then_inc(w_part, 1)
                    dve.wait_ge(w_total, n + 1)
                    nc.vector.tensor_scalar(wmean[:, n:n + 1], sum_bank[:, n:n + 1], 1.0 / (inner * DIM), None,
                                            ALU.mult).then_inc(w_scale, 1)
                    dve.wait_ge(w_scale, 3 * n + 1)
                    nc.vector.tensor_scalar(wscale[:, n:n + 1], wmean[:, n:n + 1], 1e-5, None,
                                            ALU.max).then_inc(w_scale, 1)
                    dve.wait_ge(w_scale, 3 * n + 2)
                    nc.vector.reciprocal(winv[:, n:n + 1], wscale[:, n:n + 1]).then_inc(w_scale, 1)

                def turned(n):
                    for i, (m, dst, src) in enumerate(turns):
                        if m == n:
                            dve.wait_ge(w_turned, i + 1)
                            nc.vector.tensor_scalar(dst, t_bank[i % 3][:], 1.0, -1.0, ALU.min, ALU.max) \
                                .then_inc(w_out, 1)

                def row_stats(el):
                    dve.wait_ge(x_loaded[el.par], el.dma())
                    wait_for(dve, ln_step, (el.n - 1) * 4)
                    nc.vector.bn_stats(stats[:, el.par], xbuf[:, el.par]).then_inc(bn_done, 1)
                    wait_apart(dve, bn_done, el.n + 1)
                    nc.vector.bn_aggr(mv[:, el.par], stats[:, el.par]).then_inc(stats_ready, 1)

                def x_scale(el):
                    dve.wait_ge(xn_ready, el.n + 1)
                    wait_for(dve, x_round, el.n - 1)
                    nc.vector.tensor_reduce(xmax[:, el.par, 0:1], xn[:, el.par], AX.X, ALU.max,
                                            apply_absolute_value=True).then_inc(xmax_ready, 1)
                    wait_apart(dve, xmax_ready, el.n + 1)
                    quant_scales(dve, el, xmax[:, el.par], xmax_step)
                    wait_for(dve, silu_done, (el.n - 1) * NC)
                    for n in range(2):
                        nc.vector.tensor_tensor(xs[:, el.par, n:n + 1], xmax[:, el.par, 1:2], wscale[:, n:n + 1],
                                                ALU.mult).then_inc(xs_ready, 1)

                def hidden(el):
                    wait_for(dve, h_round, el.n - 1)
                    dve.wait_ge(xs_ready, (el.n + 1) * 2)
                    def largest(c):
                        dve.wait_ge(h_done, el.n * NC + c + 1)
                        nc.vector.tensor_reduce(hpart[:, el.par, c:c + 1], hid[:, el.par, c * DIM:(c + 1) * DIM], AX.X,
                                                ALU.max, apply_absolute_value=True).then_inc(hpart_ready, 1)

                    for c in range(NC):
                        dve.wait_ge(u_done, el.n * NC + c + 1)
                        dve.wait_ge(silu_done, el.n * NC + c + 1)
                        nc.vector.scalar_tensor_tensor(hid[:, el.par, c * DIM:(c + 1) * DIM], u_bank[c % 2][:],
                                                       xs[:, el.par, 1:2], gate[:, c % 4], ALU.mult, ALU.mult) \
                            .then_inc(h_done, 1)
                        if c > 0:
                            largest(c - 1)
                    largest(NC - 1)
                    dve.wait_ge(hpart_ready, (el.n + 1) * NC)
                    nc.vector.reduce_max(hmax[:, el.par, 0:1], hpart[:, el.par], AX.X).then_inc(hmax_ready, 1)
                    wait_apart(dve, hmax_ready, el.n + 1)
                    quant_scales(dve, el, hmax[:, el.par], hmax_step)
                    nc.vector.tensor_tensor(hs[:, el.par], hmax[:, el.par, 1:2], wscale[:, 2:3], ALU.mult) \
                        .then_inc(hs_ready, 1)

                def rows_out(el):
                    dve.wait_ge(r_loaded[el.par], el.dma())
                    dve.wait_ge(hs_ready, el.n + 1)
                    dve.wait_ge(d_done, el.n + 1)
                    nc.vector.scalar_tensor_tensor(resb[:, el.par], d_bank[:], hs[:, el.par], resb[:, el.par],
                                                   ALU.mult, ALU.add).then_inc(out_done, 1)

                scale(0)
                scale(1)
                turned(0)
                scale(2)
                turned(1)
                for el in first[:2]:
                    row_stats(el)
                    x_scale(el)
                row_stats(first[2])
                turned(2)
                hidden(first[0])

                def iteration(el):
                    if el.has(2):
                        x_scale(el.plus(2))
                    if el.has(3):
                        row_stats(el.plus(3))
                    if el.has(1):
                        hidden(el.plus(1))
                    rows_out(el)

                run_elements(dve, tiles, iteration, ahead=4)

            @block.tensor
            def _(pe):
                pe.wait_ge(consts_ready, 2)

                def total(n):
                    pe.wait_ge(w_part, n + 1)
                    if n > 0:
                        pe.wait_ge(w_scale, 3 * n - 2)
                    nc.tensor.matmul(sum_bank[:, n:n + 1], ones[:], wpart[:, n:n + 1], start=True, stop=True) \
                        .then_inc(w_total, 1)

                def turn(m):
                    for i, (n, dst, src) in enumerate(turns):
                        if n != m:
                            continue
                        pe.wait_ge(w_integer, n * SLICES + max(src) // SN + 1)
                        if i >= 3:
                            pe.wait_ge(w_out, i - 2)
                        for k, at in enumerate(src):
                            last = nc.tensor.transpose(t_bank[i % 3][:, k * P:(k + 1) * P], tern[:, n, at:at + P],
                                                       ident[:])
                        last.then_inc(w_turned, 1)

                total(0)
                total(1)
                turn(0)
                total(2)
                turn(1)
                turn(2)

                def turn_x(el):
                    pe.wait_ge(xq_ready, el.n + 1)
                    wait_for(pe, tx_out, el.n)
                    for k in range(KC):
                        last = nc.tensor.transpose(tx_bank[:, k * P:(k + 1) * P], xq[:, el.par, k * P:(k + 1) * P], ident[:])
                    last.then_inc(tx_done, 1)

                def gate_up(el, cs):
                    if cs[0] == 0:
                        pe.wait_ge(tx_out, el.n + 1)
                    for c in cs:
                        for w, bank, done, read in ((wg, g_bank, g_done, silu_done), (wu, u_bank, u_done, h_done)):
                            wait_for(pe, read, el.n * NC + c - 1)
                            for k in range(KC):
                                last = nc.tensor.matmul(bank[c % 2][:], xqT[:, el.par, k], w[:, k, c * DIM:(c + 1) * DIM],
                                                        start=(k == 0), stop=(k == KC - 1))
                            last.then_inc(done, 1)

                def turn_h(el):
                    pe.wait_ge(hq_ready, el.n + 1)
                    wait_for(pe, th_out, el.n * TH)
                    if isinstance(el.n, int) and el.n == 0:
                        pe.wait_ge(w_out, len(turns))
                    for m in range(TH):
                        for k in range(8):
                            c = (8 * m + k) * P
                            last = nc.tensor.transpose(th_bank[m][:, k * P:(k + 1) * P], hq[:, el.par, c:c + P], ident[:])
                        last.then_inc(th_done, 1)

                def down(el):
                    wait_for(pe, out_done, el.n)
                    for m in range(TH):
                        pe.wait_ge(th_out, el.n * TH + m + 1)
                        for k in range(8 * m, 8 * m + 8):
                            last = nc.tensor.matmul(d_bank[:], hqT[:, el.par, k], wd[:, k], start=(k == 0), stop=(k == IK - 1))
                    last.then_inc(d_done, 1)

                turn_x(first[0])
                gate_up(first[0], range(NC))
                turn_x(first[1])

                def iteration(el):
                    if el.has(1):
                        gate_up(el.plus(1), range(NC - 1))
                    turn_h(el)
                    if el.has(1):
                        gate_up(el.plus(1), range(NC - 1, NC))
                    if el.has(2):
                        turn_x(el.plus(2))
                    down(el)

                run_elements(pe, tiles, iteration, ahead=4)

    return sems


def routed_ffn_phase(nc, tag, x_in, out, w_gate, w1, w2, w3, sw1, sw2, sw3, expert_bias, spent=(), tiles=TOK // P):
    EXPERTS, HID = w1.shape[0], w1.shape[2]
    GROUPS = EXPERTS // 2
    PAIRS = EXPERTS * EXPERTS
    HK = HID // P
    NE = tiles * EXPERTS

    with ExitStack() as ctx:
        def sb(name, shape, dt=F32):
            return ctx.enter_context(nc.sbuf_tensor(f"{tag}_{name}", shape, dt))

        def sem(name):
            return ctx.enter_context(nc.semaphore(f"{tag}_{name}"))

        ew13 = sb("ew13", [P, EXPERTS, KC, 2 * HID])
        ew2 = sb("ew2", [P, EXPERTS, HK, DIM])
        ident = sb("ident", [P, P])
        neg_half = sb("neg_half", [P, 1])
        first_out = sb("first_out", [EXPERTS, DIM])
        xT_first = sb("xT_first", [P, KC, 2 * PAIRS])
        table = sb("table", [PAIRS, 2, 2 * HID], F32R)
        pair = sb("pair", [P, tiles, 2])
        weight = sb("weight", [P, tiles, 2])
        pair_no = sb("pair_no", [P, PAIRS])
        experts_loaded = sem("experts_loaded")
        ident_ready = sem("ident_ready")
        first_ready = sem("first_ready")

        with ExitStack() as shared:
            def ssb(name, shape, dt=F32):
                return shared.enter_context(nc.sbuf_tensor(f"{tag}_{name}", shape, dt))

            def bank(name):
                return shared.enter_context(nc.psum_tensor(f"{tag}_{name}", [P, 512], F32))

            lg_bank = bank("lg")
            with ExitStack() as stage1:
                def tsb(name, shape, dt=F32):
                    return stage1.enter_context(nc.sbuf_tensor(f"{tag}_{name}", shape, dt))

                def tbank(name):
                    return stage1.enter_context(nc.psum_tensor(f"{tag}_{name}", [P, 512], F32))

                raw = ew2[:].rearrange("p e k n -> p (e k) n")[:, 0:3 * KC].rearrange("p (w k) n -> p w k n", k=KC)
                raw_gate = tsb("raw_gate", [P, DIM])
                sw = [tsb(n, [P, 2, KC, DIM], F32R) for n in ("s1", "s3", "s2")]
                gateT = tsb("gateT", [P, KC, EXPERTS])
                xbuf = tsb("xbuf", [P, 2, DIM])
                resb = tsb("resb", [P, 2, DIM])
                stats = tsb("stats", [P, 2, 6])
                mv = tsb("mv", [P, 2, 2])
                ln = tsb("ln", [P, 2, 4])
                xn = tsb("xn", [P, 2, DIM])
                xnT = tsb("xnT", [P, 2, 2, DIM], F32R)
                xnT_full = tsb("xnT_full", [P, 2, DIM])
                act_gate = tsb("act_gate", [P, 2, DIM])
                hid = tsb("hid", [P, 2, DIM])
                hidT = tsb("hidT", [P, 2, 2, DIM], F32R)
                tx_bank, th_bank, g_bank, u_bank, z_bank = [tbank(n) for n in ("tx", "th", "g", "u", "z")]
                w_bank = [tx_bank, th_bank, g_bank, u_bank]

                (ident_zero, first_zero, gate_loaded, gate_ready, w_turned, w_hi, w_lo, x_loaded0, x_loaded1, r_loaded0,
                 r_loaded1, stored0, stored1, bn_done, stats_ready, ln_step, xn_ready, tx_done, tx_hi, tx_full,
                 tx_lo, lg_done, g_done, u_done, silu_done, h_done, th_done, th_hi, th_lo, z_done, out_done) = [
                     sem(n) for n in (
                         "ident_zero first_zero gate_loaded gate_ready w_turned w_hi w_lo x_loaded0 x_loaded1 r_loaded0 "
                         "r_loaded1 stored0 stored1 bn_done stats_ready ln_step xn_ready tx_done tx_hi tx_full "
                         "tx_lo lg_done g_done u_done silu_done h_done th_done th_hi th_lo z_done out_done").split()]
                x_loaded, r_loaded, stored = (x_loaded0, x_loaded1), (r_loaded0, r_loaded1), (stored0, stored1)
                w_loaded = [sem(f"sw_loaded{n}") for n in range(3)]
                first = [Element(0, n, tiles) for n in range(4)]
                turns = [(n, k) for n in range(3) for k in range(KC)]

                def rows(t, el):
                    return t[bass.ts(el.n, P), :]

                with nc.Block() as block:
                    @block.sync
                    def _(sp):
                        def load_x(el):
                            src = rows(x_in, el)
                            wait_apart(sp, xn_ready, el.n - 1)
                            sp.dma_start(xbuf[:, el.par], src).then_inc(x_loaded[el.par], 16)

                        def load_weight(n, w):
                            sp.dma_start(raw[:, n], w.rearrange("(t p) c -> p t c", p=P)).then_inc(w_loaded[n], 16)

                        load_weight(0, sw1)
                        sp.dma_start(raw_gate[0:EXPERTS, :], w_gate).then_inc(gate_loaded, 16)
                        load_x(first[0])
                        load_x(first[1])
                        load_weight(1, sw3)
                        load_weight(2, sw2)
                        sp.dma_start(resb[:, 0], rows(x_in, first[0])).then_inc(r_loaded[0], 16)
                        load_x(first[2])
                        load_x(first[3])
                        for e in range(EXPERTS):
                            for n, w in enumerate((w1, w3)):
                                sp.dma_start(ew13[:, e, :, n * HID:(n + 1) * HID],
                                             w[e].rearrange("(k p) h -> p k h", p=P)).then_inc(experts_loaded, 16)
                        sp.wait_ge(w_turned, len(turns))
                        for e in range(EXPERTS):
                            sp.dma_start(ew2[:, e], w2[e].rearrange("(k p) d -> p k d", p=P)).then_inc(experts_loaded, 16)

                        def iteration(el):
                            if el.has(4):
                                load_x(el.plus(4))
                            if el.has(1):
                                nxt, prev = el.plus(1), el.plus(-1)
                                src = rows(x_in, nxt)
                                wait_apart(sp, stored[prev.par], prev.dma())
                                if isinstance(el.n, int) and el.n == 1:
                                    sp.wait_ge(first_ready, 2)
                                sp.dma_start(resb[:, nxt.par], src).then_inc(r_loaded[nxt.par], 16)
                            dst = rows(out, el)
                            wait_apart(sp, out_done, el.n + 1)
                            sp.dma_start(dst, resb[:, el.par]).then_inc(stored[el.par], 16)

                        run_elements(sp, tiles, iteration, ahead=4)
                        for par in range(2):
                            sp.wait_ge(stored[par], tiles // 2 * 16)

                    @block.gpsimd
                    def _(pool):
                        clear_semaphores(nc, spent)
                        nc.gpsimd.memset(ident[:], 0.0).then_inc(ident_zero, 1)
                        nc.gpsimd.memset(neg_half[:], -0.5).then_inc(ident_ready, 1)
                        nc.gpsimd.memset(xT_first[:], 0.0).then_inc(first_zero, 1)
                        pool.wait_ge(ident_zero, 1)
                        nc.gpsimd.affine_select(out=ident[:], in_=ident[:], compare_op=ALU.not_equal, fill=1.0,
                                                base=0, pattern=[[-1, P]], channel_multiplier=1).then_inc(ident_ready, 1)
                        pool.wait_ge(ident_ready, 2)

                        def normalise(el):
                            def chained(k, ins):
                                ins.then_inc(ln_step, 1)
                                wait_apart(pool, ln_step, el.n * 4 + k)

                            wait_apart(pool, stats_ready, el.n + 1)
                            l, m = ln[:, el.par], mv[:, el.par]
                            chained(1, nc.gpsimd.tensor_scalar(l[:, 0:1], m[:, 1:2], 1.0, EPS, ALU.mult, ALU.add))
                            chained(2, nc.gpsimd.tensor_tensor(l[:, 1:2], l[:, 0:1], neg_half[:], ALU.pow))
                            chained(3, nc.gpsimd.tensor_tensor(l[:, 2:3], m[:, 0:1], l[:, 1:2], ALU.mult))
                            chained(4, nc.gpsimd.tensor_scalar(l[:, 3:4], l[:, 2:3], -1.0, 0.0, ALU.mult, ALU.add))
                            wait_apart(pool, tx_done, el.n - 1)
                            nc.gpsimd.tensor_scalar(xn[:, el.par], xbuf[:, el.par], l[:, 1:2], l[:, 3:4],
                                                    ALU.mult, ALU.add).then_inc(xn_ready, 1)

                        for el in first[:3]:
                            normalise(el)

                        def iteration(el):
                            if el.has(3):
                                normalise(el.plus(3))

                        run_elements(pool, tiles, iteration, ahead=4)

                    @block.scalar
                    def _(act):
                        for i, (n, k) in enumerate(turns):
                            act.wait_ge(w_turned, i + 1)
                            nc.scalar.activation(sw[n][:, HI, k], w_bank[i % 4][:], ACT.Copy) \
                                .then_inc(w_hi, 1)
                        def hi_x(el):
                            act.wait_ge(tx_done, el.n + 1)
                            nc.scalar.activation(xnT_full[:, el.par], tx_bank[:], ACT.Copy).then_inc(tx_full, 1)
                            nc.scalar.activation(xnT[:, el.par, HI], tx_bank[:], ACT.Copy).then_inc(tx_hi, 1)

                        def silu(el):
                            act.wait_ge(g_done, el.n + 1)
                            wait_for(act, h_done, el.n - 1)
                            nc.scalar.activation(act_gate[:, el.par], g_bank[:], ACT.Silu).then_inc(silu_done, 1)

                        def hi_h(el):
                            act.wait_ge(th_done, el.n + 1)
                            nc.scalar.activation(hidT[:, el.par, HI], th_bank[:], ACT.Copy).then_inc(th_hi, 1)

                        hi_x(first[0])
                        silu(first[0])
                        hi_x(first[1])

                        def iteration(el):
                            if el.has(1):
                                silu(el.plus(1))
                            hi_h(el)
                            if el.has(2):
                                hi_x(el.plus(2))

                        run_elements(act, tiles, iteration, ahead=4)

                    @block.vector
                    def _(dve):
                        def row_stats(el):
                            dve.wait_ge(x_loaded[el.par], el.dma())
                            wait_for(dve, ln_step, (el.n - 1) * 4)
                            nc.vector.bn_stats(stats[:, el.par], xbuf[:, el.par]).then_inc(bn_done, 1)
                            wait_apart(dve, bn_done, el.n + 1)
                            nc.vector.bn_aggr(mv[:, el.par], stats[:, el.par]).then_inc(stats_ready, 1)

                        def lo_x(el):
                            dve.wait_ge(tx_hi, el.n + 1)
                            nc.vector.tensor_tensor(xnT[:, el.par, LO], tx_bank[:], xnT[:, el.par, HI].bitcast(F32),
                                                    ALU.subtract).then_inc(tx_lo, 1)

                        def lo_h(el):
                            dve.wait_ge(th_hi, el.n + 1)
                            nc.vector.tensor_tensor(hidT[:, el.par, LO], th_bank[:], hidT[:, el.par, HI].bitcast(F32),
                                                    ALU.subtract).then_inc(th_lo, 1)

                        def hidden(el):
                            dve.wait_ge(silu_done, el.n + 1)
                            dve.wait_ge(u_done, el.n + 1)
                            wait_for(dve, th_done, el.n - 1)
                            nc.vector.tensor_tensor(hid[:, el.par], u_bank[:], act_gate[:, el.par], ALU.mult) \
                                .then_inc(h_done, 1)

                        def rows_out(el):
                            dve.wait_ge(r_loaded[el.par], el.dma())
                            dve.wait_ge(z_done, el.n + 1)
                            nc.vector.tensor_tensor(resb[:, el.par], z_bank[:], resb[:, el.par], ALU.add) \
                                .then_inc(out_done, 1)

                        row_stats(first[0])
                        row_stats(first[1])
                        dve.wait_ge(gate_ready, 1)
                        nc.vector.tensor_copy(gateT[:].rearrange("p k e -> p (k e)"), z_bank[:, 0:KC * EXPERTS]) \
                            .then_inc(gate_ready, 1)
                        for i, (n, k) in enumerate(turns):
                            dve.wait_ge(w_hi, i + 1)
                            nc.vector.tensor_tensor(sw[n][:, LO, k], w_bank[i % 4][:],
                                                    sw[n][:, HI, k].bitcast(F32), ALU.subtract).then_inc(w_lo, 1)
                        row_stats(first[2])
                        dve.wait_ge(first_zero, 1)
                        dve.wait_ge(tx_done, 1)
                        dve.wait_ge(tx_hi, 1)
                        nc.vector.tensor_copy(xT_first[:, :, PAIRS:PAIRS + EXPERTS],
                                              tx_bank[:].rearrange("p (k n) -> p k n", k=KC)[:, :, 0:EXPERTS]) \
                            .then_inc(first_ready, 1)
                        lo_x(first[0])
                        hidden(first[0])
                        lo_x(first[1])

                        def keep_first():
                            dve.wait_ge(out_done, 1)
                            nc.vector.tensor_copy(first_out[:], resb[0:EXPERTS, 0]).then_inc(first_ready, 1)

                        def iteration(el):
                            lo_h(el)
                            if el.has(1):
                                hidden(el.plus(1))
                            if el.has(2):
                                lo_x(el.plus(2))
                            if el.has(3):
                                row_stats(el.plus(3))
                            rows_out(el)
                            if isinstance(el.n, int) and el.n == 0:
                                keep_first()

                        run_elements(dve, tiles, iteration, ahead=4)

                    @block.tensor
                    def _(pe):
                        pe.wait_ge(ident_ready, 2)
                        pe.wait_ge(gate_loaded, 16)
                        for k in range(KC):
                            last = nc.tensor.transpose(z_bank[:, k * EXPERTS:(k + 1) * EXPERTS],
                                                       raw_gate[0:EXPERTS, k * P:(k + 1) * P],
                                                       ident[0:EXPERTS, 0:EXPERTS])
                        last.then_inc(gate_ready, 1)
                        for i, (n, k) in enumerate(turns):
                            if k == 0:
                                pe.wait_ge(w_loaded[n], 16)
                            if i >= 4:
                                pe.wait_ge(w_lo, i - 3)
                            for o in range(KC):
                                last = nc.tensor.transpose(w_bank[i % 4][:, o * P:(o + 1) * P],
                                                           raw[:, n, o, k * P:(k + 1) * P], ident[:])
                            last.then_inc(w_turned, 1)
                        pe.wait_ge(gate_ready, 2)
                        pe.wait_ge(w_lo, len(turns))

                        def turn(bank, src, done):
                            for k in range(KC):
                                last = nc.tensor.transpose(bank[:, k * P:(k + 1) * P], src[:, k * P:(k + 1) * P], ident[:])
                            last.then_inc(done, 1)

                        def turn_x(el):
                            pe.wait_ge(xn_ready, el.n + 1)
                            wait_for(pe, tx_lo, el.n)
                            turn(tx_bank, xn[:, el.par], tx_done)

                        def turn_h(el):
                            pe.wait_ge(h_done, el.n + 1)
                            wait_for(pe, th_lo, el.n)
                            turn(th_bank, hid[:, el.par], th_done)

                        def product(bank, srcT, w, done):
                            for k in range(KC):
                                for a, b in TERMS:
                                    last = nc.tensor.matmul(bank[:], srcT[:, a, k * P:(k + 1) * P], w[:, b, k],
                                                            start=(k == 0 and (a, b) == TERMS[0]),
                                                            stop=(k == KC - 1 and (a, b) == TERMS[-1]))
                            last.then_inc(done, 1)

                        def logits(el):
                            pe.wait_ge(tx_full, el.n + 1)
                            for k in range(KC):
                                last = nc.tensor.matmul(lg_bank[:, bass.ds(el.n * EXPERTS, EXPERTS)],
                                                        xnT_full[:, el.par, k * P:(k + 1) * P], gateT[:, k],
                                                        start=(k == 0), stop=(k == KC - 1))
                            last.then_inc(lg_done, 1)

                        def gate(el):
                            pe.wait_ge(tx_lo, el.n + 1)
                            wait_for(pe, silu_done, el.n)
                            product(g_bank, xnT[:, el.par], sw[0], g_done)

                        def up(el):
                            wait_for(pe, h_done, el.n)
                            product(u_bank, xnT[:, el.par], sw[1], u_done)

                        def down(el):
                            pe.wait_ge(th_lo, el.n + 1)
                            wait_for(pe, out_done, el.n)
                            product(z_bank, hidT[:, el.par], sw[2], z_done)

                        turn_x(first[0])
                        logits(first[0])
                        gate(first[0])
                        up(first[0])
                        turn_x(first[1])

                        def iteration(el):
                            if el.has(1):
                                logits(el.plus(1))
                                gate(el.plus(1))
                            turn_h(el)
                            if el.has(1):
                                up(el.plus(1))
                            if el.has(2):
                                turn_x(el.plus(2))
                            down(el)

                        run_elements(pe, tiles, iteration, ahead=4)

            with ExitStack() as stage2:
                def rsb(name, shape, dt=F32):
                    return stage2.enter_context(nc.sbuf_tensor(f"{tag}_{name}", shape, dt))

                def rbank(name, rows=P):
                    return stage2.enter_context(nc.psum_tensor(f"{tag}_{name}", [rows, 512], F32))

                te = [P, tiles, EXPERTS]
                tc = [P, tiles, 2, EXPERTS]
                top = rsb("top", [P, tiles])
                total = rsb("total", [P, tiles])
                inverse = rsb("inverse", [P, tiles])
                expo = rsb("expo", te)
                prob = rsb("prob", te)
                score = rsb("score", te)
                gscore = rsb("gscore", [P, tiles, GROUPS])
                grank = rsb("grank", [P, tiles, GROUPS])
                gkeep = rsb("gkeep", [P, tiles, GROUPS])
                gdrop = rsb("gdrop", [P, tiles, GROUPS])
                masked = rsb("masked", te)
                group_first = rsb("group_first", [P, tiles, GROUPS * GROUPS])
                expert_first = rsb("expert_first", [P, tiles, PAIRS])
                lower_e = rsb("lower_e", [P, EXPERTS, EXPERTS])
                rank = rsb("rank", te)
                chosen = rsb("chosen", te)
                counts = rsb("counts", [P, EXPERTS])
                before = rsb("before", [P, EXPERTS, EXPERTS])
                run_start = rsb("run_start", [P, EXPERTS])
                run_end = rsb("run_end", [P, EXPERTS])
                past = rsb("past", tc)
                run = rsb("run", [P, tiles, 2])
                row = rsb("row", [P, tiles, 2])
                choice = rsb("choice", tc)
                marked = rsb("marked", tc)
                picked = rsb("picked", tc)
                position = rsb("position", [P, tiles, 2])
                choice_no = rsb("choice_no", [P, 2])
                expert_no = rsb("expert_no", [P, EXPERTS])
                ones = rsb("ones", [P, P])
                bias_row = rsb("bias_row", [P, EXPERTS])
                count_bank = lg_bank[:, NE:]
                table_bank = rbank("table_bank", PAIRS)
                onehot = rsb("onehot", [P, 4, 2, PAIRS], F32R)
                wcol = rsb("wcol", [P, 4, 2])
                onehotT = rsb("onehotT", [PAIRS, 4, 2 * P], F32R)
                act_a = rsb("act_a", [P, 4, 2, HID])
                hrow = rsb("hrow", [P, 4, 2, HID])
                hsplit = rsb("hsplit", [P, 4, 2, 2, HID], F32R)
                hsum = rsb("hsum", [PAIRS, HID])
                hsumT = rsb("hsumT", [P, HK, PAIRS])
                ohT_bank = [rbank(f"ohT{i}", PAIRS) for i in range(2)]
                ab_bank = [[rbank(f"ab{i}{c}") for c in range(2)] for i in range(2)]
                sum_bank = table_bank
                end_bank = lg_bank
                (oh_ready, ohT_done, ohT_out, ab_done, asilu_done, hrow_done, hhi_done, hlo_done, sum_done, hsum_ready, hsumT_done,
                 hsumT_ready, y_done, first_done, first_stored) = [sem(n) for n in (
                     "oh_ready ohT_done ohT_out ab_done asilu_done hrow_done hhi_done hlo_done sum_done hsum_ready hsumT_done "
                     "hsumT_ready y_done first_done first_stored").split()]
                first = [Element(0, n, tiles, 4) for n in range(3)]

                (bias_loaded, shifted, exp_ready, route_step, consts_step, consts_ready, counts_ready, counted,
                 table_done, table_hi, table_lo) = [
                     sem(n) for n in (
                         "bias_loaded shifted exp_ready route_step consts_step route_consts counts_ready counted "
                         "table_done table_hi table_lo").split()]

                with nc.Block() as block:
                    @block.sync
                    def _(sp):
                        sp.dma_start(bias_row[:], expert_bias.rearrange("(a n) -> a n", a=1).broadcast_to([P, EXPERTS])) \
                          .then_inc(bias_loaded, 16)

                        sp.wait_ge(first_done, 1)
                        sp.dma_start(out[0:EXPERTS, :], first_out[:]).then_inc(first_stored, 16)
                        sp.wait_ge(first_stored, 16)

                    @block.gpsimd
                    def _(pool):
                        exact = dict(allow_small_or_imprecise_dtypes=True)
                        nc.gpsimd.memset(group_first[:], 0.0).then_inc(consts_ready, 1)
                        nc.gpsimd.memset(expert_first[:], 0.0).then_inc(consts_ready, 1)
                        nc.gpsimd.memset(lower_e[:], 1.0).then_inc(consts_step, 1)
                        pool.wait_ge(consts_step, 1)
                        nc.gpsimd.affine_select(out=lower_e[:], in_=lower_e[:], compare_op=ALU.is_gt, fill=0.0, base=0,
                                                pattern=[[1, EXPERTS], [-1, EXPERTS]], channel_multiplier=0) \
                            .then_inc(consts_ready, 1)
                        nc.gpsimd.memset(ones[:], 1.0).then_inc(consts_ready, 1)
                        for t, pattern, each in ((position, [[2 * P, tiles], [1, 2]], 2), (choice_no, [[1, 2]], 0),
                                                 (expert_no, [[1, EXPERTS]], 0), (pair_no, [[1, PAIRS]], 0)):
                            nc.gpsimd.iota(t[:], pattern=pattern, base=0, channel_multiplier=each, **exact) \
                                .then_inc(consts_ready, 1)

                    @block.scalar
                    def _(act):
                        act.wait_ge(shifted, 1)
                        nc.scalar.activation(expo[:], expo[:], ACT.Exp).then_inc(exp_ready, 1)

                        def ohT(el):
                            wait_for(act, ab_done, (el.n - 3) * 2)
                            act.wait_ge(ohT_done, el.n + 1)
                            for c in range(2):
                                nc.scalar.activation(onehotT[:, el.par, c * P:(c + 1) * P],
                                                     ohT_bank[el.par % 2][:, c * P:(c + 1) * P], ACT.Copy).then_inc(ohT_out, 1)

                        def silu(el):
                            wait_for(act, hrow_done, (el.n - 3) * 2)
                            for c in range(2):
                                act.wait_ge(ab_done, el.n * 2 + c + 1)
                                nc.scalar.activation(act_a[:, el.par, c], ab_bank[el.par % 2][c][:, 0:HID], ACT.Silu,
                                                     scale=wcol[:, el.par, c:c + 1]).then_inc(asilu_done, 1)

                        def hi(el):
                            wait_for(act, sum_done, el.n - 3)
                            for c in range(2):
                                act.wait_ge(hrow_done, el.n * 2 + c + 1)
                                nc.scalar.activation(hsplit[:, el.par, c, HI], hrow[:, el.par, c], ACT.Copy).then_inc(hhi_done, 1)

                        for el in first:
                            ohT(el)
                        act.wait_ge(table_done, 1)
                        nc.scalar.activation(table[:, HI], table_bank[:], ACT.Copy).then_inc(table_hi, 1)
                        silu(first[0])
                        silu(first[1])

                        def iteration(el):
                            hi(el)
                            if el.has(2):
                                silu(el.plus(2))
                            if el.has(3):
                                ohT(el.plus(3))

                        run_elements(act, tiles, iteration, ahead=4, group=4)
                        act.wait_ge(hsumT_done, 1)
                        nc.scalar.activation(hsumT[:].rearrange("p k n -> p (k n)"), end_bank[:, 0:HK * PAIRS], ACT.Copy) \
                            .then_inc(hsumT_ready, 1)

                    @block.vector
                    def _(dve):
                        count = [0]

                        def step(ins):
                            count[0] += 1
                            ins.then_inc(route_step, 1)
                            dve.wait_ge(route_step, count[0])

                        V = nc.vector

                        def over_experts(ap):
                            return ap.unsqueeze(2).broadcast_to([P, ap.shape[1], EXPERTS])

                        def ranks(dst, src, first, n):
                            for d in range(1, n):
                                low, high = src[:, :, 0:n - d], src[:, :, d:n]
                                V.tensor_tensor(first[:, :, d * n:(n - 1) * (n + 1) + 1:n + 1], low, high, ALU.is_ge)
                                last = V.tensor_tensor(first[:, :, d:(n - d - 1) * (n + 1) + d + 1:n + 1], low, high, ALU.is_lt)
                            step(last)
                            step(V.reduce_sum(dst, first.rearrange("p t (a b) -> p t a b", b=n), AX.X))

                        def by_choice(ap):
                            return ap.unsqueeze(2).broadcast_to(tc)

                        lg = lg_bank[:, 0:NE].rearrange("p (t e) -> p t e", e=EXPERTS)
                        step(V.reduce_max(top[:], lg, AX.X))
                        V.tensor_tensor(expo[:], lg, over_experts(top[:]), ALU.subtract).then_inc(shifted, 1)
                        dve.wait_ge(exp_ready, 1)
                        step(V.reduce_sum(total[:], expo[:], AX.X))
                        step(V.reciprocal(inverse[:], total[:]))
                        step(V.tensor_tensor(prob[:], expo[:], over_experts(inverse[:]), ALU.mult))
                        dve.wait_ge(bias_loaded, 16)
                        step(V.tensor_tensor(score[:], prob[:], bias_row[:].unsqueeze(1).broadcast_to(te), ALU.add))
                        halves = score[:].rearrange("p t (g a) -> p t g a", a=2)
                        step(V.tensor_tensor(gscore[:], halves[:, :, :, 0], halves[:, :, :, 1], ALU.add))
                        dve.wait_ge(consts_ready, 8)
                        ranks(grank[:], gscore[:], group_first[:], GROUPS)
                        step(V.tensor_scalar(gkeep[:], grank[:], 1.5, None, ALU.is_lt))
                        step(V.tensor_scalar(gdrop[:], gkeep[:], -1.0, BIG, ALU.add, ALU.mult))
                        mp = masked[:].rearrange("p t (g a) -> p t g a", a=2)
                        for a in range(2):
                            step(V.tensor_tensor(mp[:, :, :, a], halves[:, :, :, a], gkeep[:], ALU.mult))
                            step(V.tensor_tensor(mp[:, :, :, a], mp[:, :, :, a], gdrop[:], ALU.add))
                        ranks(rank[:], masked[:], expert_first[:], EXPERTS)
                        step(V.tensor_scalar(chosen[:], rank[:], 1.5, None, ALU.is_lt))
                        V.reduce_sum(counts[:], chosen[:].rearrange("p t e -> p e t"), AX.X).then_inc(counts_ready, 1)
                        step(V.tensor_tensor(choice[:], by_choice(rank[:]), choice_no[:].unsqueeze(1).unsqueeze(3)
                                             .broadcast_to(tc), ALU.is_equal))
                        V.tensor_tensor(marked[:], choice[:], expert_no[:].unsqueeze(1).unsqueeze(1).broadcast_to(tc),
                                        ALU.mult)
                        step(V.tensor_tensor(picked[:], choice[:], by_choice(prob[:]), ALU.mult))
                        V.reduce_sum(row[:], marked[:], AX.X)
                        step(V.reduce_sum(weight[:], picked[:], AX.X))
                        dve.wait_ge(counted, 1)
                        step(V.tensor_tensor(before[:], count_bank[:, 0:EXPERTS].unsqueeze(1)
                                             .broadcast_to([P, EXPERTS, EXPERTS]), lower_e[:], ALU.mult))
                        step(V.reduce_sum(run_start[:], before[:], AX.X))
                        step(V.tensor_tensor(run_end[:], run_start[:], count_bank[:, 0:EXPERTS], ALU.add))
                        step(V.tensor_tensor(past[:], position[:].unsqueeze(3).broadcast_to(tc),
                                             run_end[:].unsqueeze(1).unsqueeze(1).broadcast_to(tc), ALU.is_ge))
                        step(V.reduce_sum(run[:], past[:], AX.X))
                        step(V.scalar_tensor_tensor(pair[:], run[:], float(EXPERTS), row[:], ALU.mult, ALU.add))

                        def one_hot(el):
                            wait_for(dve, sum_done, el.n - 3)
                            nc.vector.tensor_copy(wcol[:, el.par], weight[:, bass.ds(el.n, 1)].rearrange("p a c -> p (a c)"))
                            nc.vector.tensor_tensor(onehot[:, el.par], pair_no[:].unsqueeze(1).broadcast_to([P, 2, PAIRS]),
                                                    pair[:, bass.ds(el.n, 1)].rearrange("p a c -> p (a c)").unsqueeze(2)
                                                    .broadcast_to([P, 2, PAIRS]), ALU.is_equal).then_inc(oh_ready, 1)

                        def hidden(el):
                            dve.wait_ge(oh_ready, el.n + 1)
                            wait_for(dve, sum_done, el.n - 3)
                            for c in range(2):
                                dve.wait_ge(asilu_done, el.n * 2 + c + 1)
                                nc.vector.scalar_tensor_tensor(hrow[:, el.par, c], ab_bank[el.par % 2][c][:, HID:2 * HID],
                                                               wcol[:, el.par, c:c + 1], act_a[:, el.par, c],
                                                               ALU.mult, ALU.mult).then_inc(hrow_done, 1)

                        def lo(el):
                            for c in range(2):
                                dve.wait_ge(hhi_done, el.n * 2 + c + 1)
                                nc.vector.tensor_tensor(hsplit[:, el.par, c, LO], hrow[:, el.par, c],
                                                        hsplit[:, el.par, c, HI].bitcast(F32), ALU.subtract).then_inc(hlo_done, 1)

                        for el in first:
                            one_hot(el)
                        dve.wait_ge(table_hi, 1)
                        nc.vector.tensor_tensor(table[:, LO], table_bank[:], table[:, HI].bitcast(F32), ALU.subtract) \
                            .then_inc(table_lo, 1)
                        hidden(first[0])
                        hidden(first[1])

                        def iteration(el):
                            if el.has(3):
                                one_hot(el.plus(3))
                            lo(el)
                            if el.has(2):
                                hidden(el.plus(2))

                        run_elements(dve, tiles, iteration, ahead=4, group=4)
                        dve.wait_ge(sum_done, tiles)
                        nc.vector.tensor_copy(hsum[:], sum_bank[:, 0:HID]).then_inc(hsum_ready, 1)
                        dve.wait_ge(y_done, 1)
                        nc.vector.tensor_tensor(first_out[:], ab_bank[0][0][0:EXPERTS, :], first_out[:], ALU.add) \
                            .then_inc(first_done, 1)

                    @block.tensor
                    def _(pe):
                        def turn(el):
                            wait_apart(pe, oh_ready, el.n + 1)
                            wait_apart(pe, ohT_out, (el.n - 1) * 2)
                            for c in range(2):
                                last = nc.tensor.transpose(ohT_bank[el.par % 2][:, c * P:(c + 1) * P], onehot[:, el.par, c].bitcast(F32), ident[:])
                            last.then_inc(ohT_done, 1)

                        pe.wait_ge(first_ready, 2)
                        pe.wait_ge(experts_loaded, 3 * EXPERTS * 16)
                        for e in range(EXPERTS):
                            if e == EXPERTS // 2 + 1:
                                pe.wait_ge(counts_ready, 1)
                                pe.wait_ge(consts_ready, 8)
                                nc.tensor.matmul(count_bank[:, 0:EXPERTS], ones[:], counts[:], start=True, stop=True) \
                                    .then_inc(counted, 1)
                            if e >= EXPERTS - 2:
                                for el in first[:2] if e == EXPERTS - 2 else first[2:]:
                                    turn(el)
                            window = slice(PAIRS - e * EXPERTS, 2 * PAIRS - e * EXPERTS)
                            for k in range(KC):
                                last = nc.tensor.matmul(table_bank[:], xT_first[:, k, window], ew13[:, e, k],
                                                        start=(e == 0 and k == 0), stop=(e == EXPERTS - 1 and k == KC - 1))
                        last.then_inc(table_done, 1)

                        def pick(el):
                            if isinstance(el.n, int) and el.n == 0:
                                pe.wait_ge(table_lo, 1)
                            for c in range(2):
                                pe.wait_ge(ohT_out, el.n * 2 + c + 1)
                                wait_for(pe, hrow_done, el.n * 2 + c - 3)
                                for part in (HI, LO):
                                    last = nc.tensor.matmul(ab_bank[el.par % 2][c][:], onehotT[:, el.par, c * P:(c + 1) * P],
                                                            table[:, part], start=(part == HI), stop=(part == LO))
                                last.then_inc(ab_done, 1)

                        def add_up(el):
                            for c in range(2):
                                pe.wait_ge(hlo_done, el.n * 2 + c + 1)
                                for part in (HI, LO):
                                    last = nc.tensor.matmul(
                                        sum_bank[:, 0:HID], onehot[:, el.par, c], hsplit[:, el.par, c, part],
                                        start=((c, part) == (0, HI) and isinstance(el.n, int) and el.n == 0),
                                        stop=((c, part) == (1, LO) and isinstance(el.n, int) and el.n == tiles - 1),
                                        skip_group_check=True)
                            last.then_inc(sum_done, 1)

                        pick(first[0])
                        pick(first[1])

                        def iteration(el):
                            if el.has(2):
                                pick(el.plus(2))
                            if el.has(3):
                                turn(el.plus(3))
                            add_up(el)

                        run_elements(pe, tiles, iteration, ahead=4, group=4)
                        pe.wait_ge(hsum_ready, 1)
                        for k in range(HK):
                            last = nc.tensor.transpose(end_bank[:, k * PAIRS:(k + 1) * PAIRS], hsum[:, k * P:(k + 1) * P],
                                                       ident[0:PAIRS, 0:PAIRS])
                        last.then_inc(hsumT_done, 1)
                        pe.wait_ge(hsumT_ready, 1)
                        for e in range(EXPERTS):
                            for k in range(HK):
                                last = nc.tensor.matmul(ab_bank[0][0][0:EXPERTS, :], hsumT[:, k, e * EXPERTS:(e + 1) * EXPERTS],
                                                        ew2[:, e, k], start=(e == 0 and k == 0),
                                                        stop=(e == EXPERTS - 1 and k == HK - 1))
                        last.then_inc(y_done, 1)


def decoder_kernel(nc, x, ctx_1024, mask_if, mask_bk, a_wv, a_bv, a_wk, a_bk, a_wq, a_bq, a_wo, a_bo, f_gate, f_up, f_down,
                   c_gain, c_bias, c_wq, c_wkv, c_wo, m_gate, m_w1, m_w2, m_w3, m_sw1, m_sw2, m_sw3, m_bias, out):
    def rows(t):
        return t.rearrange("b s d -> (b s) d")

    def internal(name, shape):
        return nc.dram_tensor(name, shape, F32, kind="Internal").ap()

    x_rows, ctx_rows, out_rows = rows(x), rows(ctx_1024), rows(out)
    x1, x2, x3 = [internal(n, (TOK, DIM)) for n in ("x1", "x2", "x3")]

    spent_a = attention_phase(
        nc, "a", 16, x_rows, ctx_rows, mask_if.rearrange("b o q k -> (b o q) k"), -1e20, x1,
                    (a_wq, a_wk, a_wv, a_wo), a_bq, a_bk, a_bv, a_bo, None, None)
    spent_b = ternary_ffn_phase(nc, "b", x1, x2, f_gate, f_up, f_down, spent=spent_a)
    attention_phase(nc, "c", 8, x2, ctx_rows, mask_bk, -1e30, x3, (c_wq, c_wkv[:, 0:DIM], c_wkv[:, DIM:2 * DIM], c_wo),
                    None, None, None, None, c_gain, c_bias, spent=spent_b)
    routed_ffn_phase(nc, "m", x3, out_rows, m_gate, m_w1, m_w2, m_w3, m_sw1, m_sw2, m_sw3, m_bias)


INPUTS = ["x", "ctx_1024", "mask_Bx1x1xS2_if1", "mask_BxS2_bk0", "L0_xattn_Wv", "L0_xattn_bv", "L0_xattn_Wk",
          "L0_xattn_bk", "L0_xattn_Wq", "L0_xattn_bq", "L0_xattn_Wo", "L0_xattn_bo", "L0_ffn_w_gate", "L0_ffn_w_up",
          "L0_ffn_w_down", "L1_xattn_ln_g", "L1_xattn_ln_b", "L1_xattn_Wq", "L1_xattn_Wkv", "L1_xattn_Wo",
          "L1_ffn_w_gate", "L1_ffn_w1", "L1_ffn_w2", "L1_ffn_w3", "L1_ffn_sw1", "L1_ffn_sw2", "L1_ffn_sw3",
          "L1_ffn_expert_bias"]


def kernel(**inputs):
    import numpy as np
    import concourse.bacc as bacc
    from concourse.bass_utils import run_bass_kernel_spmd

    nc = bacc.Bacc("TRN2", target_bir_lowering=False, num_devices=1)
    arrays, args = {}, []
    for name in INPUTS:
        a = np.ascontiguousarray(inputs[name])
        arrays[f"in_{name}_dram"] = a
        args.append(nc.dram_tensor(f"in_{name}_dram", a.shape, mybir.dt.from_np(a.dtype), kind="ExternalInput").ap())
    args.append(nc.dram_tensor("out_0_dram", (BATCH, SEQ, DIM), F32, kind="ExternalOutput").ap())
    decoder_kernel(nc, *args)
    return run_bass_kernel_spmd(nc, [arrays], core_ids=[0]).results[0]["out_0_dram"]
```
